# Optimizing a Trainium2 kernel written in Bass

```python
import numpy as np
import jax
import jax.numpy as jnp

def _softmax(x, axis=-1):
    return jax.nn.softmax(x, axis=axis)

def _gelu(x):
    return jax.nn.gelu(x, approximate=True)

def _silu(x):
    return jax.nn.silu(x)

def _sigmoid(x):
    return jax.nn.sigmoid(x)

def _layernorm(x, axis=-1, eps=1e-05):
    m = jnp.mean(x, axis=axis, keepdims=True)
    v = jnp.var(x, axis=axis, keepdims=True)
    return (x - m) / jnp.sqrt(v + eps)

def _scatter_add(tgt, idx, src, axis=0):
    return tgt.at[idx].add(src)

def _segment_sum(src, seg, n):
    return jax.ops.segment_sum(src, seg, n)
kernel_name = 'mk_adj_preln_d4_adj_r2_ca870a'

def setup_inputs(seed: int=0):
    np.random.seed(seed)
    _w = jnp.asarray

    def _rec_inputs():
        import jax
        import jax.numpy as jnp
        _gk = jax.random.key(seed)
        x = 7.22e-05 + 1 * jax.random.normal(jax.random.fold_in(_gk, 1), (16, 512, 256), jnp.float32)
        _a = jax.random.bernoulli(jax.random.fold_in(_gk, 2), 0.03125, (512, 512))
        _a = jnp.logical_or(_a, jnp.swapaxes(_a, -1, -2))
        _a = jnp.logical_or(_a, jnp.eye(512, dtype=bool))
        adj = _a.astype(jnp.int32)
        return (x, adj)
    x, adj = _rec_inputs()

    def _L0_gnn_setup():
        import jax, jax.numpy as jnp
        import numpy as np
        LEAKY_ALPHA = 0.01
        NEG_INF = -1000000000.0
        LN_EPS = 1e-05

        def _gat_heads(x, adj, W, a):
            O = W.shape[-1]
            Wh = jnp.einsum('bnf,hfo->bhno', x, W)
            f1 = jnp.einsum('bhno,ho->bhn', Wh, a[:, :O])
            f2 = jnp.einsum('bhno,ho->bhn', Wh, a[:, O:])
            e = f1[:, :, :, None] + f2[:, :, None, :]
            e = jnp.where(e > 0, e, LEAKY_ALPHA * e)
            e = jnp.where(adj[None, None] > 0, e, NEG_INF)
            attn = jax.nn.softmax(e, axis=-1)
            return jnp.einsum('bhnm,bhmo->bhno', attn, Wh)
        key = jax.random.key(seed)
        ks = jax.random.split(key, 10)
        B, N, F_in, F_hid, H, F_out, D_ff = (8, 1024, 256, 256, 4, 256, 256)
        s = 0.05
        return {'enc_inputs': jax.random.normal(ks[0], (B, N, F_in), jnp.float32), 'adj': jax.random.randint(ks[1], (N, N), 0, 2, jnp.int32), 'W_heads': jax.random.normal(ks[2], (H, F_in, F_hid), jnp.float32) * s, 'a_heads': jax.random.normal(ks[3], (H, 2 * F_hid), jnp.float32) * s, 'W_out': jax.random.normal(ks[4], (H * F_hid, F_out), jnp.float32) * s, 'a_out': jax.random.normal(ks[5], (2 * F_out,), jnp.float32) * s, 'w1': jax.random.normal(ks[6], (F_out, D_ff), jnp.float32) * s, 'b1': jnp.zeros((D_ff,), jnp.float32), 'w2': jax.random.normal(ks[7], (D_ff, F_out), jnp.float32) * s, 'b2': jnp.zeros((F_out,), jnp.float32), 'ln_gamma': jnp.ones((F_out,), jnp.float32), 'ln_beta': jnp.zeros((F_out,), jnp.float32)}
    _L0_gnn_all = _L0_gnn_setup()
    _L0_gnn_in = {k: v for k, v in _L0_gnn_all.items() if k in ('W_heads', 'a_heads', 'W_out', 'a_out', 'w1', 'b1', 'w2', 'b2', 'ln_gamma', 'ln_beta')}
    del _L0_gnn_all

    def _L1_gnn_setup():
        import jax, jax.numpy as jnp
        import numpy as np
        B, N, F, F1 = (512, 75, 256, 128)
        NEG = -1000000000.0
        ALPHA = 0.2
        key = jax.random.key(seed)
        k1, k2, k3, k4 = jax.random.split(key, 4)
        X = jax.random.normal(k1, (B, N, F), dtype=jnp.float32)
        A = jax.random.randint(k2, (N, N), 0, 2, dtype=jnp.int32)
        W = jax.random.normal(k3, (F, F1), dtype=jnp.float32) * (1.0 / np.sqrt(F))
        a = jax.random.normal(k4, (2, F1, 1), dtype=jnp.float32) * (1.0 / np.sqrt(F1))
        return {'X': X, 'A': A, 'W': W, 'a': a}
    _L1_gnn_all = _L1_gnn_setup()
    _L1_gnn_in = {k: v for k, v in _L1_gnn_all.items() if k in ('W', 'a')}
    del _L1_gnn_all

    def _L2_gnn_setup():
        import jax, jax.numpy as jnp
        import numpy as np
        D_MODEL = 256
        NUM_HEADS = 8
        D_HEAD = D_MODEL // NUM_HEADS
        B, N = (4, 1024)
        key = jax.random.key(seed)
        ks = jax.random.split(key, 10)
        s = 1.0 / np.sqrt(D_MODEL)
        inp = {'h': jax.random.normal(ks[0], (B, N, D_MODEL), dtype=jnp.float32), 'adj': jax.random.randint(ks[1], (N, N), 0, 2, dtype=jnp.int32), 'Wq': jax.random.uniform(ks[2], (D_MODEL, D_MODEL), jnp.float32, -s, s), 'bq': jax.random.uniform(ks[3], (D_MODEL,), jnp.float32, -s, s), 'Wk': jax.random.uniform(ks[4], (D_MODEL, D_MODEL), jnp.float32, -s, s), 'bk': jax.random.uniform(ks[5], (D_MODEL,), jnp.float32, -s, s), 'Wv': jax.random.uniform(ks[6], (D_MODEL, D_MODEL), jnp.float32, -s, s), 'bv': jax.random.uniform(ks[7], (D_MODEL,), jnp.float32, -s, s), 'Wo': jax.random.uniform(ks[8], (D_MODEL, D_MODEL), jnp.float32, -s, s), 'bo': jax.random.uniform(ks[9], (D_MODEL,), jnp.float32, -s, s)}
        return inp
    _L2_gnn_all = _L2_gnn_setup()
    _L2_gnn_in = {k: v for k, v in _L2_gnn_all.items() if k in ('Wq', 'bq', 'Wk', 'bk', 'Wv', 'bv', 'Wo', 'bo')}
    del _L2_gnn_all

    def _L3_gnn_setup():
        import jax, jax.numpy as jnp
        import numpy as np
        B, K, DIN, DOUT = (32, 64, 256, 256)
        key = jax.random.key(seed)
        k1, k2, k3, k4 = jax.random.split(key, 4)
        x = jax.random.normal(k1, (B, K, DIN), dtype=jnp.float32)
        adj = jax.random.randint(k2, (K, K), 0, 2, dtype=jnp.int32)
        W = jax.random.normal(k3, (DOUT, 2 * DIN), dtype=jnp.float32) * 0.02
        b = jax.random.normal(k4, (DOUT,), dtype=jnp.float32) * 0.02
        return {'x': x, 'adj': adj, 'W': W, 'b': b}
    _L3_gnn_all = _L3_gnn_setup()
    _L3_gnn_in = {k: v for k, v in _L3_gnn_all.items() if k in ('W', 'b')}
    del _L3_gnn_all
    return {'x': x, 'adj': adj, 'L0_gnn_W_heads': _L0_gnn_in['W_heads'], 'L0_gnn_a_heads': _L0_gnn_in['a_heads'], 'L0_gnn_W_out': _L0_gnn_in['W_out'], 'L0_gnn_a_out': _L0_gnn_in['a_out'], 'L0_gnn_w1': _L0_gnn_in['w1'], 'L0_gnn_b1': _L0_gnn_in['b1'], 'L0_gnn_w2': _L0_gnn_in['w2'], 'L0_gnn_b2': _L0_gnn_in['b2'], 'L0_gnn_ln_gamma': _L0_gnn_in['ln_gamma'], 'L0_gnn_ln_beta': _L0_gnn_in['ln_beta'], 'L1_gnn_W': _L1_gnn_in['W'], 'L1_gnn_a': _L1_gnn_in['a'], 'L2_gnn_Wq': _L2_gnn_in['Wq'], 'L2_gnn_bq': _L2_gnn_in['bq'], 'L2_gnn_Wk': _L2_gnn_in['Wk'], 'L2_gnn_bk': _L2_gnn_in['bk'], 'L2_gnn_Wv': _L2_gnn_in['Wv'], 'L2_gnn_bv': _L2_gnn_in['bv'], 'L2_gnn_Wo': _L2_gnn_in['Wo'], 'L2_gnn_bo': _L2_gnn_in['bo'], 'L3_gnn_W': _L3_gnn_in['W'], 'L3_gnn_b': _L3_gnn_in['b']}

def reference(x, adj, L0_gnn_W_heads, L0_gnn_a_heads, L0_gnn_W_out, L0_gnn_a_out, L0_gnn_w1, L0_gnn_b1, L0_gnn_w2, L0_gnn_b2, L0_gnn_ln_gamma, L0_gnn_ln_beta, L1_gnn_W, L1_gnn_a, L2_gnn_Wq, L2_gnn_bq, L2_gnn_Wk, L2_gnn_bk, L2_gnn_Wv, L2_gnn_bv, L2_gnn_Wo, L2_gnn_bo, L3_gnn_W, L3_gnn_b):
    import jax
    import jax.numpy as jnp

    def _L0_gnn_ref(enc_inputs, adj, W_heads, a_heads, W_out, a_out, w1, b1, w2, b2, ln_gamma, ln_beta):
        import jax, jax.numpy as jnp
        import numpy as np
        LEAKY_ALPHA = 0.01
        NEG_INF = -1000000000.0
        LN_EPS = 1e-05

        def _gat_heads(x, adj, W, a):
            O = W.shape[-1]
            Wh = jnp.einsum('bnf,hfo->bhno', x, W)
            f1 = jnp.einsum('bhno,ho->bhn', Wh, a[:, :O])
            f2 = jnp.einsum('bhno,ho->bhn', Wh, a[:, O:])
            e = f1[:, :, :, None] + f2[:, :, None, :]
            e = jnp.where(e > 0, e, LEAKY_ALPHA * e)
            e = jnp.where(adj[None, None] > 0, e, NEG_INF)
            attn = jax.nn.softmax(e, axis=-1)
            return jnp.einsum('bhnm,bhmo->bhno', attn, Wh)
        B, N, _ = enc_inputs.shape
        h = jax.nn.elu(_gat_heads(enc_inputs, adj, W_heads, a_heads))
        h = jnp.transpose(h, (0, 2, 1, 3)).reshape(B, N, -1)
        out = _gat_heads(h, adj, W_out[None], a_out[None])[:, 0]
        out = jax.nn.elu(out)
        ffn = jnp.maximum(out @ w1 + b1, 0.0) @ w2 + b2
        y = ffn + out
        mu = jnp.mean(y, axis=-1, keepdims=True)
        var = jnp.var(y, axis=-1, keepdims=True)
        return (y - mu) / jnp.sqrt(var + LN_EPS) * ln_gamma + ln_beta

    def _L1_gnn_ref(X, A, W, a):
        import jax, jax.numpy as jnp
        import numpy as np
        B, N, F, F1 = (512, 75, 256, 128)
        NEG = -1000000000.0
        ALPHA = 0.2
        h = jnp.einsum('bnf,fo->bno', X, W)
        att_self = jnp.einsum('bno,od->bnd', h, a[0])
        att_neigh = jnp.einsum('bno,od->bnd', h, a[1])
        e = att_self + jnp.swapaxes(att_neigh, 1, 2)
        e = jax.nn.leaky_relu(e, ALPHA)
        adj = A.astype(h.dtype)
        e = e + NEG * (1.0 - adj)[None, :, :]
        alpha = jax.nn.softmax(e, axis=-1)
        out = jnp.einsum('bij,bjo->bio', alpha, h)
        return jnp.concatenate([out, h], axis=-1)

    def _L2_gnn_ref(h, adj, Wq, bq, Wk, bk, Wv, bv, Wo, bo):
        import jax, jax.numpy as jnp
        import numpy as np
        D_MODEL = 256
        NUM_HEADS = 8
        D_HEAD = D_MODEL // NUM_HEADS
        B, N = (4, 1024)
        b, n, _ = h.shape

        def split_heads(x):
            return x.reshape(b, n, NUM_HEADS, D_HEAD).transpose(0, 2, 1, 3)
        q = split_heads(h @ Wq.T + bq)
        k = split_heads(h @ Wk.T + bk)
        v = split_heads(h @ Wv.T + bv)
        scale = 1.0 / np.sqrt(D_HEAD)
        scores = jnp.einsum('bhqd,bhkd->bhqk', q, k) * scale
        mask = (adj == 0)[None, None, :, :]
        scores = jnp.where(mask, -jnp.inf, scores)
        attn = jax.nn.softmax(scores, axis=-1)
        out = jnp.einsum('bhqk,bhkd->bhqd', attn, v)
        out = out.transpose(0, 2, 1, 3).reshape(b, n, D_MODEL)
        return out @ Wo.T + bo

    def _L3_gnn_ref(x, adj, W, b):
        import jax, jax.numpy as jnp
        import numpy as np
        B, K, DIN, DOUT = (32, 64, 256, 256)
        Din = x.shape[-1]
        Wi, Wj = (W[:, :Din], W[:, Din:])
        mi = jnp.einsum('bkd,od->bko', x, Wi)
        mj = jnp.einsum('bkd,od->bko', x, Wj)
        a = adj.astype(x.dtype)
        deg = a.sum(axis=1)
        out = deg[None, :, None] * (mi + b) + jnp.einsum('ij,bjo->bio', a, mj)
        return out
    h = jnp.maximum(_layernorm(x, axis=-1), 0.0)
    x = x + _L0_gnn_ref(h, adj, L0_gnn_W_heads, L0_gnn_a_heads, L0_gnn_W_out, L0_gnn_a_out, L0_gnn_w1, L0_gnn_b1, L0_gnn_w2, L0_gnn_b2, L0_gnn_ln_gamma, L0_gnn_ln_beta)
    h = jnp.maximum(_layernorm(x, axis=-1), 0.0)
    x = x + _L1_gnn_ref(h, adj, L1_gnn_W, L1_gnn_a)
    h = jnp.maximum(_layernorm(x, axis=-1), 0.0)
    x = x + _L2_gnn_ref(h, adj, L2_gnn_Wq, L2_gnn_bq, L2_gnn_Wk, L2_gnn_bk, L2_gnn_Wv, L2_gnn_bv, L2_gnn_Wo, L2_gnn_bo)
    h = jnp.maximum(_layernorm(x, axis=-1), 0.0)
    x = x + _L3_gnn_ref(h, adj, L3_gnn_W, L3_gnn_b)
    return x

_drawn_inputs = setup_inputs


def setup_inputs(seed=0):
    import zlib

    import numpy as np

    out = dict(_drawn_inputs(seed))
    spreads = {'L0_gnn_b1': (0.0, 0.1),
     'L0_gnn_b2': (0.0, 0.1),
     'L0_gnn_ln_gamma': (1.0, 0.2),
     'L0_gnn_ln_beta': (0.0, 0.1)}
    factors = {'L0_gnn_a_heads': 2.678,
     'L0_gnn_a_out': 8.0,
     'L1_gnn_a': 4.286,
     'L2_gnn_Wq': 8.0,
     'L2_gnn_bq': 48.583,
     'L2_gnn_Wk': 8.0,
     'L2_gnn_bk': 64.0,
     'L2_gnn_bv': 4.921}
    for name, (base, spread) in spreads.items():
        noise = np.random.default_rng([zlib.crc32(name.encode()), seed]).standard_normal(out[name].shape)
        drawn = base * np.exp(spread * noise) if base else spread * noise
        out[name] = jnp.asarray(drawn.astype(out[name].dtype))
    for name, factor in factors.items():
        out[name] = (out[name] * factor).astype(out[name].dtype)
    return out
```

```python
from contextlib import ExitStack

import concourse.bass as bass
from concourse import mybir

F32 = mybir.dt.float32
F32R = mybir.dt.float32r
BF16 = mybir.dt.bfloat16
I32 = mybir.dt.int32
ALU = mybir.AluOpType
ACT = mybir.ActivationFunctionType
AX_X = mybir.AxisListType.X

P = 128
MASKED = -1e30
LOWEST = -3e38
LN_EPS = 1e-5
SLOPE = {"x": 0.01, "y": 0.2}
XRING = 6
YRING = 6


def x_steps(NI, NH):
    s = [(1.5, "dve", "stats", (0,)), (1.0, "pool", "rstd", (0,)), (0.3, "dve", "shift", (0,)),
         (2.0, "act", "norm", (0,))]
    for c in range(2):
        s += [(0.5, "pe", "turn", (c,)), (0.5, "act", "hi", (c,)), (0.6, "dve", "lo", (c,))]
    for h in range(NH):
        for i in range(NI):
            s += [(0.6, "pe", "proj", (h, i)), (0, "act", "wh", (h, i))]
        if h:
            s += [(0.4, "pe", "f2row", (h - 1,)), (0.0, "dve", "rowmax", (h - 1,))]
    s += [(0.5, "pe", "f2row", (NH - 1,)), (2.4, "dve", "rowmax", (NH - 1,)),
          (0.8, "dve", "offsets", (0,))]

    def tiles(h, first, last):
        out = [(0.9, "pe", "rows", (h,)), (0.5, "act", "brow", (h,))] if first == 0 else []
        for j in range(first, last):
            out += [(0.7, "dve", "score", (h, j)), (0.6, "pool", "mask", (h, j)),
                    (0.2, "act", "prob", (h, j))]
        return out

    def aggregate(h):
        out = []
        for i in range(NI):
            out += [(1.7, "pe", "pv", (h, i)), (0, "dve", "recip", (h, i)), (0, "act", "elu_exp", (h, i))]
            if i:
                out += [(0, "dve", "elu", (h, i - 1))]
        return out + [(1.0, "dve", "elu", (h, NI - 1))]

    def turned(h):
        out = []
        for c in range(2):
            out += [(0.5, "pe", "h_turn", (h, c)), (0, "act", "h_hi", (h, c)), (0.5, "dve", "h_lo", (h, c))]
        return out

    s += tiles(0, 0, NI)
    early = XRING - NI
    for h in range(NH):
        a = aggregate(h)
        n = tiles(h + 1, 0, early) if h + 1 < NH else []
        k = 0
        for step in a:
            s.append(step)
            if step[1] == "pe":
                take = (len(n) + NI - 1) // NI
                s += [(0,) + t[1:] for t in n[k:k + take]]
                k += take
        s += [(0,) + t[1:] for t in n[k:]]
        s += turned(h)
        if h + 1 < NH:
            s += tiles(h + 1, early, NI)
        if h % 2:
            for i in range(NI):
                s += [(1.3, "pe", "proj2", (h // 2, i)), (0, "act" if h < 2 else "dve", "wh2", (h // 2, i))]
    s += [(0.5, "pe", "f2row", (NH,)), (2.6, "dve", "rowmax", (NH,)), (0.8, "dve", "offsets", (1,))]
    s += tiles(NH, 0, NI) + aggregate(NH)
    for c in range(2):
        s += [(0.5, "pe", "o_turn", (c,)), (0.5, "act", "o_hi", (c,)), (0.6, "dve", "o_lo", (c,))]
    s += [(0, "pool", "add_b2", ())]
    for m in range(2):
        s += [(1.3, "pe", "ffn1", (m,)), (0.4, "act", "hidden", (m,))]
    for p in range(2):
        s += [(1.8, "pe", "ffn2", (p,)), (0.4, "dve", "ffn_sum", (p,))]
    s += [(1.5, "dve", "stats", (1,)), (1.0, "pool", "rstd", (1,)), (0.3, "dve", "shift", (1,)),
          (2.0, "act", "norm", (1,)), (2.3, "pool", "gain", ()), (1.5, "dve", "out", ())]
    return s


def y_steps(NI, NG, G):
    def norm(n):
        return [(1.5, "dve", "stats", (n,)), (1.0, "pool", "rstd", (n,)), (0.3, "dve", "shift", (n,)),
                (2.0, "act", "norm", (n,))]

    s = norm(0)
    for c in range(2):
        s += [(0.5, "pe", "turn", (0, c)), (0.5, "act", "hi", (0, c))]
    for p in range(2):
        s += [(0.9, "pe", "l1_proj", (p,)), (0.3, "act", "l1_wh", (p,))]
    s += [(0.5, "pe", "l1_f2row", ()), (2.5, "dve", "l1_rowmax", ()), (0.8, "dve", "l1_offsets", ()),
          (0.9, "pe", "l1_rows", ()), (0.5, "act", "l1_brow", ())]
    for j in range(NI):
        s += [(0.7, "dve", "l1_score", (j,)), (0.6, "pool", "l1_mask", (j,)), (0.2, "act", "l1_prob", (j,))]
    s += [(0, "pool", "l1_add_wh", ())]
    for p in range(2):
        s += [(1.8, "pe", "l1_pv", (p,)), (0.8, "dve", "l1_sum", (p,))]
    s += norm(1) + [(0, "pool", "add_bo", ())]
    for c in range(2):
        s += [(0.5, "pe", "turn", (1, c)), (0.5, "act", "hi", (1, c)), (0.6, "dve", "lo", (1, c))]

    def qk(g):
        out = []
        for t in range(2):
            out += [(1.3, "pe", "qk", (g, t)), (0.5, "act", "qk_hi", (g, t)), (0.6, "dve", "qk_lo", (g, t))]
        return out

    def qv():
        out = []
        for p in range(2):
            out += [(1.3, "pe", "v", (p,)), (0.5, "dve", "v_sum", (p,))]
        return out

    for g in range(NG):
        s += qk(g)
        s += qv() if g == 0 else [(2.0, None, None, ())]
        for h in range(G):
            for i in range(NI):
                s += [(0, "pe", "near", (g, h, i)), (0.62, "dve", "near_max", (g, h, i))]
        s += [(0.5, "pe", "max_turn", (g,)), (0.4, "act", "max_hi", (g,)), (0.3, "dve", "max_lo", (g,)),
              (2.5, None, None, ())]
        for k in range(NI):
            for h in range(G):
                s += [(0.65, "pe", "far", (g, k, h)), (0, "act", "far_prob", (g, k, h))]
                if k:
                    s += [(0.25, "pe", "far_pv", (g, k - 1, h))]
        for h in range(G):
            s += [(0.3, "pe", "far_pv", (g, NI - 1, h))]
        s += [(2.0, "dve", "far_recip", (g,)), (0.6, "dve", "far_norm", (g,))]
    for p in range(2):
        s += [(1.8, "pe", "o_proj", (p,)), (0.5, "dve", "o_sum", (p,))]
    s += norm(2)
    for c in range(2):
        s += [(0.5, "pe", "turn", (2, c)), (0.5, "act", "hi", (2, c)), (0.6, "dve", "lo", (2, c))]
    for p in range(2):
        s += [(1.3, "pe", "mj", (p,)), (0.5, "dve", "mj_sum", (p,)), (0.3, "act", "mj_hi", (p,)), (0.5, "dve", "mj_lo", (p,))]
    for p in range(2):
        s += [(1.3, "pe", "mi", (p,)), (0.6, "dve", "mi_sum", (p,))]
    for p in range(2):
        s += [(1.8, "pe", "gather", (p,)), (0.6, "dve", "gather_sum", (p,))]
    return s


def merged(xs, ys):
    placed = []
    for chain, steps, share in (("x", xs, 1.0), ("y", ys, 0.97)):
        total, at = sum(t for t, *_ in steps), 0.0
        for n, (t, engine, step, args) in enumerate(steps):
            placed.append((share * at / total, n, chain, engine, step, args))
            at += t
    placed.sort(key=lambda r: r[:2])
    return [r[2:] for r in placed if r[3]]


def gnn_stack_kernel(nc, x, adj, adj_t, w_heads, a_heads, w_out, a_out, w1, b1, w2, b2, gamma, beta,
                     l1_w, l1_a, wq_t, bq, wk_t, bk, wv_t, bv, wo_t, bo, wi_t, wj_t, b3, out):
    B, N, D = x.shape
    NI = N // P
    DC = D // P
    NH = w_heads.shape[0]
    D1 = l1_w.shape[1]
    HEADS2, DH = 8, 32
    G = P // DH
    NG = HEADS2 // G
    SCALE = float(DH) ** -0.5
    W0 = D + 2
    W1C = D1 + 2
    assert N == 512 and D == 256 and NI == 4 and DC == 2

    XS, YS = x_steps(NI, NH), y_steps(NI, NG, G)
    TOGETHER = merged(XS, YS)
    X_ALONE, Y_ALONE = merged(XS, []), merged([], YS)

    ctx = ExitStack()
    with ctx:
        def sb(name, shape, dt=F32):
            return ctx.enter_context(nc.sbuf_tensor(name, shape, dt))

        def sem(name):
            return ctx.enter_context(nc.semaphore(name))

        wh_hi, wh_lo = sb("wh_hi", [P, DC, NH, W0], F32R), sb("wh_lo", [P, DC, NH, W0], F32R)
        wo2_hi, wo2_lo = sb("wo2_hi", [P, NH * DC, W0], F32R), sb("wo2_lo", [P, NH * DC, W0], F32R)
        w1_hi, w1_lo = sb("w1_hi", [P, DC, D], F32R), sb("w1_lo", [P, DC, D], F32R)
        w2_sb, wl1 = sb("w2_sb", [P, DC, D]), sb("wl1", [P, DC, W1C])
        sq = {n: (sb(f"{n}_hi", [P, DC, D], F32R), sb(f"{n}_lo", [P, DC, D], F32R))
              for n in ("wq", "wk", "wv", "wi", "wj")}
        wo_sb = sb("wo_sb", [P, DC, D])
        mask_n, mask_t = sb("mask_n", [P, NI, N], BF16), sb("mask_t", [P, NI, N], BF16)
        adjt = sb("adjt", [P, NI, N], F32R)
        ident, ident_b, ones = sb("ident", [P, P]), sb("ident_b", [P, P], BF16), sb("ones", [P, DH])
        rows = {n: sb(f"{n}_rows", [P, D]) for n in ("b2", "gamma", "beta", "bv", "bo", "b3")}
        b1_col, bq_col, bk_col = sb("b1_col", [P, DC]), sb("bq_col", [P, DC]), sb("bk_col", [P, DC])
        deg, power = sb("deg", [P, NI]), sb("power", [P, NI])

        def small(chain, heads):
            return {
                "stats": sb(f"{chain}_stats", [P, NI, 6]), "mv": sb(f"{chain}_mv", [P, NI, 2]),
                "var": sb(f"{chain}_var", [P, NI]), "rstd": sb(f"{chain}_rstd", [P, NI]),
                "shift": sb(f"{chain}_shift", [P, NI]), "max": sb(f"{chain}_max", [P, NI, heads]),
                "sum": sb(f"{chain}_f12", [P, NI, heads]), "m": sb(f"{chain}_m", [P, NI, heads]),
                "a": sb(f"{chain}_a", [P, NI, heads]), "b": sb(f"{chain}_b", [P, NI, heads]),
                "c": sb(f"{chain}_c", [P, NI, heads]), "d": sb(f"{chain}_d", [P, NI, heads]),
            }

        XT, YT = small("x", NH + 1), small("y", 1)

        x_in = sb("x_in", [P, NI, D])
        x_h = sb("x_h", [P, NI, D])
        x_fr = sb("x_fr", [P, 8, N], F32R)
        whx = sb("whx", [P, NI, NH, D + 4])
        brow = sb("brow", [P, N])
        xp = sb("xp", [P, XRING, N])
        elu_e, x_r = sb("elu_e", [P, 2, D]), sb("x_r", [P, NI])
        y_x, y_h = sb("y_x", [P, NI, D]), sb("y_h", [P, NI, D])
        y_t, y_fr = sb("y_t", [P, DC, N]), sb("y_fr", [P, 4, N], F32R)
        wh1 = sb("wh1", [P, NI, D1 + 4])
        y_v = sb("y_v", [P, NI, D])
        x_junk, y_junk = elu_e[:, :, :].bitcast(BF16), sb("y_junk", [P, 2, N], BF16)
        yp = sb("yp", [P, YRING, N])
        qk_part = sb("qk_part", [P, 4, N], F32R)
        qs, ks = sb("qs", [P, G, N], F32R), sb("ks", [P, G, N], F32R)
        max2, y_r = sb("max2", [P, G * NI]), sb("y_r", [P, NI])
        negm = sb("negm", [G * NI, 2, P], F32R)

        XB = [ctx.enter_context(nc.psum_tensor(f"x_bank{i}", [P, 512], F32)) for i in range(4)]
        YB = [ctx.enter_context(nc.psum_tensor(f"y_bank{i}", [P, 512], F32)) for i in range(4)]

        s_load, s_split, s_init = sem("weights_loaded"), sem("setup_step"), sem("constants_ready")
        s_id, s_apart = sem("identity_ready"), sem("wait_kept_apart")
        names = """x_in_loaded x_stats x_aggr x_var x_rstd x_shift x_norm x_hi x_lo x_wh x_rowmax
        x_small x_brow x_score x_mask x_prob x_recip x_elu_exp x_elu_shift x_elu x_h_hi x_h_lo x_wh2a
        x_wh2b x_o_hi x_o_lo x_b2 x_hidden x_ffn x_gain x_beta x_out
        y_stats y_aggr y_var y_rstd y_shift y_norm y_hi0 y_hi y_lo y_wh y_rowmax y_small y_brow y_score
        y_mask y_prob y_wh_added y_recip y_l1 y_bo y_qk_hi y_qk_lo y_v y_stacked y_near_max y_max_hi y_max_lo
        y_max_row y_far_prob y_frecip y_ctx y_o y_mj_sum y_mj_hi y_mj_lo y_mi y_out y_stored""".split()
        S = {n: sem(n) for n in names}
        xfull = [sem(f"x_bank{i}_full") for i in range(4)]
        yfull = [sem(f"y_bank{i}_full") for i in range(4)]

        PER = {n: 1 for n in names}
        PER.update(x_in_loaded=16, x_stats=2 * NI, x_aggr=2 * NI, x_var=2, x_rstd=2,
                   x_shift=2, x_norm=2 * NI, x_hi=2, x_lo=2, x_wh=NH * NI, x_rowmax=(NH + 1) * NI, x_small=12,
                   x_brow=NH + 1, x_score=(NH + 1) * NI, x_mask=(NH + 1) * NI, x_prob=(NH + 1) * NI,
                   x_recip=(NH + 1) * NI, x_elu_exp=(NH + 1) * NI, x_elu_shift=(NH + 1) * NI,
                   x_elu=(NH + 1) * NI, x_h_hi=NH * 2, x_h_lo=NH * 2, x_wh2a=NI, x_wh2b=NI, x_o_hi=2,
                   x_o_lo=2, x_hidden=2, x_ffn=2, y_stats=3 * NI, y_aggr=3 * NI, y_var=3, y_rstd=3,
                   y_shift=3, y_norm=3 * NI, y_hi0=2, y_hi=4, y_lo=4, y_wh=2, y_rowmax=NI, y_small=6,
                   y_score=NI, y_mask=NI, y_prob=NI, y_recip=NI, y_l1=NI, y_qk_hi=2 * NG,
                   y_qk_lo=2 * NG, y_v=2, y_stacked=16 * 6 * G * NG, y_near_max=G * NI * NG,
                   y_max_hi=NG, y_max_lo=NG, y_max_row=32 * NG, y_far_prob=NG * NI * G, y_frecip=NG,
                   y_ctx=NG, y_o=2, y_mj_sum=2, y_mj_hi=2, y_mj_lo=2, y_mi=NI, y_out=2, y_stored=16)

        def after(name, b, n):
            v = b * PER[name] + n
            return (s_init, 1) if isinstance(v, int) and v <= 0 else (S[name], v)

        def uses(order, chain, bank_of):
            found, per = {}, [0] * 4
            for c, engine, step, args in order:
                if c == chain and engine == "pe":
                    for key in bank_of(step, args):
                        bank = key[0] if key[0] is not None else (per[0] + per[1]) % 2
                        found[key[1]] = (bank, per[bank])
                        per[bank] += 1
            return found, per

        def x_bank_of(step, args):
            if step == "rows":
                return [(2, ("arow",) + args), (3, ("brow",) + args)]
            if step == "f2row":
                return [(2 + args[0] % 2, ("f2row",) + args)]
            return [(None, (step,) + args)]

        def y_bank_of(step, args):
            if step == "l1_rows":
                return [(2, ("arow",)), (3, ("brow",))]
            if step == "l1_f2row":
                return [(2, ("f2row",))]
            if step == "far_pv":
                g, k, h = args
                return [(2, ("far_sum", g)), (3, ("far_ctx", g))] if k == 0 and h == 0 else []
            return [(None, (step,) + args)]

        XU, XN = uses(X_ALONE, "x", x_bank_of)
        YU, YN = uses(Y_ALONE, "y", y_bank_of)

        def x_released(key):
            k, a = key[0], key[1:]
            return {"turn": lambda: ("x_lo", a[0] + 1), "proj": lambda: ("x_wh", a[0] * NI + a[1] + 1),
                    "f2row": lambda: ("x_rowmax", (a[0] + 1) * NI), "arow": lambda: ("x_score", (a[0] + 1) * NI),
                    "brow": lambda: ("x_brow", a[0] + 1), "pv": lambda: ("x_elu", a[0] * NI + a[1] + 1),
                    "h_turn": lambda: ("x_h_lo", a[0] * 2 + a[1] + 1),
                    "proj2": lambda: ("x_wh2b" if a[0] else "x_wh2a", a[1] + 1),
                    "o_turn": lambda: ("x_o_lo", a[0] + 1), "ffn1": lambda: ("x_hidden", a[0] + 1),
                    "ffn2": lambda: ("x_ffn", a[0] + 1)}[k]()

        def y_released(key):
            k, a = key[0], key[1:]
            return {"turn": lambda: ("y_hi0", a[1] + 1) if a[0] == 0 else ("y_lo", (a[0] - 1) * 2 + a[1] + 1),
                    "l1_proj": lambda: ("y_wh", a[0] + 1), "f2row": lambda: ("y_rowmax", NI),
                    "arow": lambda: ("y_score", NI), "brow": lambda: ("y_brow", 1),
                    "l1_pv": lambda: ("y_l1", 2 * a[0] + 2),
                    "qk": lambda: ("y_qk_lo", a[0] * 2 + a[1] + 1), "v": lambda: ("y_v", a[0] + 1),
                    "near": lambda: ("y_near_max", (a[0] * G + a[1]) * NI + a[2] + 1),
                    "max_turn": lambda: ("y_max_lo", a[0] + 1),
                    "far": lambda: ("y_far_prob", (a[0] * NI + a[1]) * G + a[2] + 1),
                    "far_sum": lambda: ("y_frecip", a[0] + 1), "far_ctx": lambda: ("y_ctx", a[0] + 1),
                    "o_proj": lambda: ("y_o", a[0] + 1), "mj": lambda: ("y_mj_sum", a[0] + 1),
                    "mi": lambda: ("y_mi", 2 * a[0] + 2), "gather": lambda: ("y_out", a[0] + 1)}[k]()

        def emptied(chain, b, *key):
            U, N_, released = (XU, XN, x_released) if chain == "x" else (YU, YN, y_released)
            bank, n = U[key]
            before = [k for k, v in U.items() if v == (bank, n - 1 if n else N_[bank] - 1)][0]
            name, count = released(before)
            if n:
                return after(name, b, count)
            return after(name, b, 0) if chain == "x" else after("x_out", b, 1)

        def bank_of(chain, *key):
            return (XB if chain == "x" else YB)[(XU if chain == "x" else YU)[key][0]]

        def full(chain, *key):
            bank, _ = (XU if chain == "x" else YU)[key]
            return (xfull if chain == "x" else yfull)[bank]

        def filled(chain, b, *key):
            U, N_, fulls = (XU, XN, xfull) if chain == "x" else (YU, YN, yfull)
            bank, n = U[key]
            return fulls[bank], b * N_[bank] + n + 1

        def split3(pe, outp, hi_l, lo_l, hi_r, lo_r, pairs, start=True, stop=True):
            todo = [(a, b_) for l, r in pairs for a, b_ in
                    ((hi_l(l), hi_r(r)), (hi_l(l), lo_r(r)), (lo_l(l), hi_r(r)))]
            for n, (a, b_) in enumerate(todo):
                last = pe.matmul(outp, a, b_, start=start and n == 0, stop=stop and n == len(todo) - 1)
            return last

        x_v = x.rearrange("b (i p) d -> b p i d", p=P)
        out_v = out.rearrange("b (i p) d -> b p i d", p=P)
        block = ctx.enter_context(nc.Block())

        def turns(engine, steps, name):
            def run(order, xb, yb):
                for chain, e, step, args in order:
                    if e == name:
                        steps[chain + "_" + step](xb if chain == "x" else yb, *args)

            run(X_ALONE, 0, None)
            with engine.Fori(1, B) as b:
                run(TOGETHER, b, b - 1)
            run(Y_ALONE, None, B - 1)

        LOADS = 0
        st_w = whx[:, :, :, :].rearrange("p a b c -> p (a b c)")
        st_x = xp[:, :, :].rearrange("p a b -> p (a b)")
        st_y = yp[:, :, :].rearrange("p a b -> p (a b)")
        w_st = st_w[:, 0:DC * NH * W0].rearrange("p (c h o) -> p c h o", c=DC, h=NH)
        sq_st = {n: (st_x if k < 4 else st_y)[:, (k % 4) * 512:(k % 4) * 512 + 512].rearrange("p (c o) -> p c o", c=DC)
                 for k, n in enumerate(sq)}
        w1_st = y_h[:, 0:2, :]
        adj_i = st_y[:, 512:512 + 2048].bitcast(I32).rearrange("p (i n) -> p i n", i=NI)
        adj_t_i = [v.bitcast(I32).rearrange("p (i n) -> p i n", i=2)
                   for v in (y_t[:, :, :].rearrange("p a b -> p (a b)"), st_x[:, 2048:3072])]
        a_st = x_h[:, :, :].rearrange("p a b -> p (a b)")
        a_st2 = x_in[:, :, :].rearrange("p a b -> p (a b)")
        ysx, ysv = y_x[:, :, :].rearrange("p a b -> p (a b)"), y_v[:, :, :].rearrange("p a b -> p (a b)")

        @block.sync
        def _(sp):
            def load(dst, src, name=s_load):
                sp.dma_start(dst, src).then_inc(name, 16)

            for c in range(DC):
                load(w_st[:, c, :, 0:D], w_heads[:, c * P:(c + 1) * P, :].rearrange("h p o -> p h o"))
            load(a_st[:, 0:1024].rearrange("p (h o) -> p h o", h=NH), a_heads[:, 0:D].partition_broadcast(P))
            load(a_st2[:, 0:1024].rearrange("p (h o) -> p h o", h=NH), a_heads[:, D:2 * D].partition_broadcast(P))
            load(brow[:, :], a_out.partition_broadcast(P))
            load(elu_e[:, 0, :], l1_a.rearrange("s o u -> (s o u)").partition_broadcast(P))
            for c in range(DC):
                load(wl1[:, c, 0:D1], l1_w[c * P:(c + 1) * P, :])
                load(w2_sb[:, c, :], w2[c * P:(c + 1) * P, :])
                load(wo_sb[:, c, :], wo_t[c * P:(c + 1) * P, :])
                load(w1_st[:, c, :], w1[c * P:(c + 1) * P, :])
            for n, src in (("wq", wq_t), ("wk", wk_t), ("wv", wv_t), ("wi", wi_t), ("wj", wj_t)):
                load(sq_st[n], src.rearrange("(c p) o -> p c o", p=P))
            load(adj_i, adj.rearrange("(i p) n -> p i n", p=P))
            for n, src in (("b2", b2), ("gamma", gamma), ("beta", beta), ("bv", bv), ("bo", bo), ("b3", b3)):
                load(rows[n][:, :], src.partition_broadcast(P))
            for t, src in ((b1_col, b1), (bq_col, bq), (bk_col, bk)):
                sp.dma_start(t[:, :], src.rearrange("(c p) -> p c", p=P), allow_slow_non_contiguous=True)\
                    .then_inc(s_load, 16)
            load(ysx, w_out[0:4 * P, :].rearrange("(k p) o -> p k o", p=P))
            load(ysv, w_out[4 * P:8 * P, :].rearrange("(k p) o -> p k o", p=P))
            for k in (0, 1):
                load(adj_t_i[k], adj_t[2 * k * P:2 * (k + 1) * P, :].rearrange("(i p) n -> p i n", p=P))

            def x_load(b):
                sp.wait_ge(*after("x_out", b, 0))
                sp.dma_start(x_in[:, :, :], x_v[b]).then_inc(S["x_in_loaded"], 16)

            def y_stack(b, g):
                for t, dst in ((0, qs), (1, ks)):
                    sp.wait_ge(*after("y_qk_lo", b, g * 2 + t + 1))
                    if g and t == 0:
                        sp.wait_ge(*filled("y", b, "far", g - 1, NI - 1, G - 1))
                    for r, part in enumerate(((0, 0, 1), (0, 1, 0))[t]):
                        for h in range(G):
                            sp.dma_start(dst[DH * r:DH * (r + 1), h, :].bitcast(F32),
                                         qk_part[DH * h:DH * (h + 1), 2 * t + part, :].bitcast(F32)).then_inc(S["y_stacked"], 16)

            def y_max_row(b, g):
                for r, name in ((0, "y_max_hi"), (1, "y_max_lo")):
                    sp.wait_ge(*after(name, b, g + 1))
                    sp.dma_start(qs[3 * DH + r:3 * DH + r + 1, :, :].rearrange("p h (i n) -> p (h i) n", i=NI).bitcast(F32),
                                 negm[:, r, :].bitcast(F32)).then_inc(S["y_max_row"], 16)

            def y_store(b):
                sp.wait_ge(*after("y_out", b, 2))
                sp.dma_start(out_v[b], y_x[:, :, :]).then_inc(S["y_stored"], 16)

            sp.wait_ge(s_init, 1)
            x_load(0)
            x_load(1)

            def y_all(b):
                for g in range(NG):
                    y_stack(b, g)
                    y_max_row(b, g)

            with sp.Fori(1, B - 1) as b:
                y_all(b - 1)
                y_store(b - 1)
                x_load(b + 1)
            y_all(B - 2)
            y_store(B - 2)
            y_all(B - 1)
            y_store(B - 1)
            sp.wait_ge(S["y_stored"], 16 * B)

        N_LOADS = DC + 4 + DC * 4 + 5 + 1 + 6 + 3 + 4

        @block.gpsimd
        def _(pool):
            pool.memset(ident[:, :], 0.0).then_inc(s_id, 1)
            pool.memset(ident_b[:, :], 0.0).then_inc(s_id, 1)
            pool.wait_ge(s_id, 2)
            for t in (ident, ident_b):
                pool.affine_select(out=t[:, :], in_=t[:, :], compare_op=ALU.not_equal, fill=1.0, base=0,
                                   pattern=[[-1, P]], channel_multiplier=1).then_inc(s_id, 1)
            pool.memset(ones[:, :], 1.0).then_inc(s_id, 1)
            pool.memset(power[:, :], -0.5).then_inc(s_id, 1)
            pool.wait_ge(s_id, 6)
            pool.wait_ge(s_init, 1)

            def rstd(chain, T, k):
                def step(b, n):
                    pool.wait_ge(*after(f"{chain}_var", b, n + 1))
                    pool.tensor_tensor(T["rstd"][:, :], T["var"][:, :], power[:, :], ALU.pow)\
                        .then_inc(S[f"{chain}_rstd"], 1)
                return step

            def x_mask(b, h, j):
                n = h * NI + j
                pool.wait_ge(*after("x_score", b, n + 1))
                pool.tensor_tensor(xp[:, n % XRING, :], xp[:, n % XRING, :], mask_t[:, j, :], ALU.add)\
                    .then_inc(S["x_mask"], 1)

            def x_add_b2(b):
                pool.wait_ge(*filled("x", b, "o_turn", 1))
                pool.wait_ge(*after("x_elu", b, (NH + 1) * NI))
                pool.tensor_tensor(x_h[:, :, :], x_h[:, :, :], rows["b2"][:, None, :].broadcast_to([P, NI, D]),
                                   ALU.add).then_inc(S["x_b2"], 1)
                pool.tensor_tensor(x_in[:, :, :], x_in[:, :, :], rows["beta"][:, None, :].broadcast_to([P, NI, D]),
                                   ALU.add).then_inc(S["x_beta"], 1)

            def x_gain(b):
                pool.wait_ge(*after("x_norm", b, 2 * NI))
                pool.tensor_tensor(x_h[:, :, :], x_h[:, :, :], rows["gamma"][:, None, :].broadcast_to([P, NI, D]),
                                   ALU.mult).then_inc(S["x_gain"], 1)

            def y_l1_mask(b, j):
                pool.wait_ge(*after("y_score", b, j + 1))
                pool.tensor_tensor(yp[:, j, :], yp[:, j, :], mask_t[:, j, :], ALU.add).then_inc(S["y_mask"], 1)

            def y_l1_add_wh(b):
                pool.wait_ge(*after("y_norm", b, NI))
                pool.wait_ge(*after("y_wh", b, 2))
                pool.tensor_tensor(y_x[:, :, D1:D], y_x[:, :, D1:D], wh1[:, :, 0:D1], ALU.add)\
                    .then_inc(S["y_wh_added"], 1)

            def y_add_bo(b):
                pool.wait_ge(*after("y_norm", b, 2 * NI))
                pool.tensor_tensor(y_x[:, :, :], y_x[:, :, :], rows["bo"][:, None, :].broadcast_to([P, NI, D]),
                                   ALU.add).then_inc(S["y_bo"], 1)

            turns(pool, {"x_rstd": rstd("x", XT, 2), "x_mask": x_mask, "x_add_b2": x_add_b2, "x_gain": x_gain,
                         "y_rstd": rstd("y", YT, 3), "y_l1_mask": y_l1_mask, "y_l1_add_wh": y_l1_add_wh,
                         "y_add_bo": y_add_bo}, "pool")

        @block.scalar
        def _(act):
            act.wait_ge(s_init, 1)

            def x_norm(b, n):
                act.wait_ge(*after("x_shift", b, n + 1))
                act.wait_ge(*after("x_rstd", b, n + 1))
                if n == 0:
                    act.wait_ge(*after("x_out", b, 0))
                for i in range(NI):
                    src = x_in if n == 0 else x_h
                    act.activation(x_h[:, i, :], src[:, i, :], ACT.Relu if n == 0 else ACT.Identity,
                                   bias=XT["shift"][:, i:i + 1], scale=XT["rstd"][:, i:i + 1])\
                        .then_inc(S["x_norm"], 1)

            def y_norm(b, n):
                act.wait_ge(*after("y_shift", b, n + 1))
                act.wait_ge(*after("y_rstd", b, n + 1))
                for i in range(NI):
                    act.activation(y_h[:, i, :], y_x[:, i, :], ACT.Relu,
                                   bias=YT["shift"][:, i:i + 1], scale=YT["rstd"][:, i:i + 1])\
                        .then_inc(S["y_norm"], 1)

            def x_hi(b, c):
                act.wait_ge(*filled("x", b, "turn", c))
                act.activation(x_fr[:, c, :], bank_of("x", "turn", c)[:, :], ACT.Copy).then_inc(S["x_hi"], 1)

            def x_wh(b, h, i):
                act.wait_ge(*filled("x", b, "proj", h, i))
                act.activation(whx[:, i, h, 0:W0], bank_of("x", "proj", h, i)[:, 0:W0], ACT.Copy)\
                    .then_inc(S["x_wh"], 1)

            def x_brow(b, h):
                bank = bank_of("x", "brow", h)
                act.wait_ge(*filled("x", b, "brow", h))
                act.wait_ge(*after("x_score", b, h * NI))
                act.activation(brow[:, :], bank[:, :], ACT.Copy).then_inc(S["x_brow"], 1)

            def x_prob(b, h, j):
                n = h * NI + j
                act.wait_ge(*after("x_mask", b, n + 1))
                act.activation(xp[:, n % XRING, :], xp[:, n % XRING, :], ACT.Exp, bias=XT["d"][:, j, h:h + 1])\
                    .then_inc(S["x_prob"], 1)

            def x_elu_exp(b, h, i):
                n = h * NI + i
                bank = bank_of("x", "pv", h, i)
                act.wait_ge(*filled("x", b, "pv", h, i))
                act.wait_ge(*after("x_recip", b, n + 1))
                act.wait_ge(*after("x_elu", b, max(n - 1, 0)))
                act.activation(elu_e[:, n % 2, :], bank[:, 0:D], ACT.Exp, scale=x_r[:, i:i + 1])\
                    .then_inc(S["x_elu_exp"], 1)

            def x_h_hi(b, h, c):
                act.wait_ge(*filled("x", b, "h_turn", h, c))
                act.activation(x_fr[:, (h % 2) * 2 + c, :], bank_of("x", "h_turn", h, c)[:, :], ACT.Copy)\
                    .then_inc(S["x_h_hi"], 1)

            def x_wh2(b, p, i):
                act.wait_ge(*filled("x", b, "proj2", p, i))
                act.activation(whx[:, i, 0, 0:W0], bank_of("x", "proj2", p, i)[:, 0:W0], ACT.Copy)\
                    .then_inc(S["x_wh2a"], 1)

            def x_o_hi(b, c):
                act.wait_ge(*filled("x", b, "o_turn", c))
                act.activation(x_fr[:, c, :], bank_of("x", "o_turn", c)[:, :], ACT.Copy)\
                    .then_inc(S["x_o_hi"], 1)

            def x_hidden(b, m):
                bank = bank_of("x", "ffn1", m)
                act.wait_ge(*filled("x", b, "ffn1", m))
                act.activation(whx[:, m, 1:3, 0:D], bank[:, :].rearrange("p (a n) -> p a n", a=2), ACT.Relu,
                               bias=b1_col[:, m:m + 1]).then_inc(S["x_hidden"], 1)

            def y_hi(b, n, c):
                bank = bank_of("y", "turn", n, c)
                act.wait_ge(*filled("y", b, "turn", n, c))
                if n == 0:
                    act.activation(y_t[:, c, :], bank[:, :], ACT.Copy).then_inc(S["y_hi0"], 1)
                else:
                    act.activation(y_fr[:, c, :], bank[:, :], ACT.Copy).then_inc(S["y_hi"], 1)

            def y_l1_wh(b, p):
                bank = bank_of("y", "l1_proj", p)
                act.wait_ge(*filled("y", b, "l1_proj", p))
                act.activation(wh1[:, 2 * p:2 * p + 2, 0:W1C],
                               bank[:, 0:2 * W1C].rearrange("p (a n) -> p a n", a=2), ACT.Copy)\
                    .then_inc(S["y_wh"], 1)

            def y_l1_brow(b):
                bank = bank_of("y", "brow")
                act.wait_ge(*filled("y", b, "brow"))
                act.activation(y_v[:, 0:2, :].rearrange("p a n -> p (a n)"), bank[:, :], ACT.Copy)\
                    .then_inc(S["y_brow"], 1)

            def y_l1_prob(b, j):
                act.wait_ge(*after("y_mask", b, j + 1))
                act.activation(yp[:, j, :], yp[:, j, :], ACT.Exp, bias=YT["d"][:, j, 0:1]).then_inc(S["y_prob"], 1)

            def y_qk_hi(b, g, t):
                bank = bank_of("y", "qk", g, t)
                act.wait_ge(*filled("y", b, "qk", g, t))
                if g:
                    act.wait_ge(*after("y_stacked", b, 16 * 6 * G * g))
                act.activation(qk_part[:, 2 * t, :], bank[:, :], ACT.Identity,
                               bias=(bq_col, bk_col)[t][:, g:g + 1]).then_inc(S["y_qk_hi"], 1)

            def y_max_hi(b, g):
                bank = bank_of("y", "max_turn", g)
                act.wait_ge(*filled("y", b, "max_turn", g))
                if g:
                    act.wait_ge(*after("y_max_row", b, 32 * g))
                act.activation(negm[:, 0, :], bank[0:G * NI, 0:P], ACT.Copy, scale=-1.0).then_inc(S["y_max_hi"], 1)

            def y_far_prob(b, g, k, h):
                n = (g * NI + k) * G + h
                bank = bank_of("y", "far", g, k, h)
                act.wait_ge(*filled("y", b, "far", g, k, h))
                act.activation(yp[:, n % YRING, :], bank[:, :], ACT.Exp, scale=SCALE).then_inc(S["y_far_prob"], 1)

            def y_mj_hi(b, p):
                act.wait_ge(*after("y_mj_sum", b, p + 1))
                act.activation(qk_part[:, p, :], y_h[:, 2 * p:2 * p + 2, :].rearrange("p a n -> p (a n)"), ACT.Copy)\
                    .then_inc(S["y_mj_hi"], 1)

            turns(act, {"x_norm": x_norm, "x_hi": x_hi, "x_wh": x_wh, "x_brow": x_brow, "x_prob": x_prob,
                        "x_elu_exp": x_elu_exp, "x_h_hi": x_h_hi, "x_wh2": x_wh2, "x_o_hi": x_o_hi,
                        "x_hidden": x_hidden, "y_norm": y_norm, "y_hi": y_hi, "y_l1_wh": y_l1_wh,
                        "y_l1_brow": y_l1_brow, "y_l1_prob": y_l1_prob, "y_qk_hi": y_qk_hi,
                        "y_max_hi": y_max_hi, "y_far_prob": y_far_prob, "y_mj_hi": y_mj_hi}, "act")

        @block.tensor
        def _(pe):
            pe.wait_ge(s_id, 6)
            pe.wait_ge(s_init, 1)

            def turned(chain, src, bank, c, key, rows_=P):
                for i in range(NI):
                    last = pe.transpose(bank[:, i * P:(i + 1) * P], src[:, i, c * P:(c + 1) * P], ident[:, :])
                last.then_inc(full(chain, *key), 1)

            def broadcast(chain, columns, bank, key):
                for i in range(NI):
                    last = pe.transpose(bank[:, i * P:(i + 1) * P], columns(i).broadcast_to([P, P]), ident[:, :])
                last.then_inc(full(chain, *key), 1)

            def x_turn(b, c):
                bank = bank_of("x", "turn", c)
                pe.wait_ge(*emptied("x", b, "turn", c))
                pe.wait_ge(*after("x_norm", b, NI))
                turned("x", x_h, bank, c, ("turn", c))

            def x_proj(b, h, i):
                bank = bank_of("x", "proj", h, i)
                pe.wait_ge(*emptied("x", b, "proj", h, i))
                pe.wait_ge(*after("x_lo", b, DC))
                n = slice(i * P, (i + 1) * P)
                split3(pe, bank[:, 0:W0], lambda c: x_fr[:, c, n], lambda c: x_fr[:, 2 + c, n],
                       lambda c: wh_hi[:, c, h, :], lambda c: wh_lo[:, c, h, :], [(c, c) for c in range(DC)])\
                    .then_inc(full("x", "proj", h, i), 1)

            def x_f2row(b, h):
                bank = bank_of("x", "f2row", h)
                pe.wait_ge(*emptied("x", b, "f2row", h))
                if h < NH:
                    pe.wait_ge(*after("x_wh", b, (h + 1) * NI))
                else:
                    pe.wait_ge(*after("x_wh2b", b, NI))
                broadcast("x", lambda i: whx[:, i, h % NH, D + 1:D + 2], bank, ("f2row", h))

            def x_rows(b, h):
                bank = bank_of("x", "arow", h)
                pe.wait_ge(*emptied("x", b, "arow", h))
                pe.wait_ge(*after("x_small", b, 6 if h < NH else 12))
                broadcast("x", lambda i: XT["a"][:, i, h:h + 1], bank, ("arow", h))
                bank = bank_of("x", "brow", h)
                pe.wait_ge(*emptied("x", b, "brow", h))
                broadcast("x", lambda i: XT["b"][:, i, h:h + 1], bank, ("brow", h))

            def x_pv(b, h, i):
                bank = bank_of("x", "pv", h, i)
                pe.wait_ge(*emptied("x", b, "pv", h, i))
                pe.wait_ge(*after("x_prob", b, (h + 1) * NI))
                for j in range(NI):
                    t = xp[:, (h * NI + j) % XRING, i * P:(i + 1) * P]
                    last = pe.matmul(bank[:, 0:D + 3], t, whx[:, j, h % NH, 0:D + 3], start=(j == 0), stop=(j == NI - 1))
                last.then_inc(full("x", "pv", h, i), 1)

            def x_h_turn(b, h, c):
                bank = bank_of("x", "h_turn", h, c)
                pe.wait_ge(*emptied("x", b, "h_turn", h, c))
                pe.wait_ge(*after("x_elu", b, (h + 1) * NI))
                turned("x", x_h, bank, c, ("h_turn", h, c))

            def x_proj2(b, p, i):
                bank = bank_of("x", "proj2", p, i)
                pe.wait_ge(*emptied("x", b, "proj2", p, i))
                pe.wait_ge(*after("x_h_lo", b, 4 * (p + 1)))
                n = slice(i * P, (i + 1) * P)
                split3(pe, bank[:, 0:W0], lambda k: x_fr[:, k, n], lambda k: x_fr[:, 4 + k, n],
                       lambda k: wo2_hi[:, 4 * p + k, :], lambda k: wo2_lo[:, 4 * p + k, :],
                       [(k, k) for k in range(4)]).then_inc(full("x", "proj2", p, i), 1)

            def x_o_turn(b, c):
                bank = bank_of("x", "o_turn", c)
                pe.wait_ge(*emptied("x", b, "o_turn", c))
                pe.wait_ge(*after("x_elu", b, (NH + 1) * NI))
                turned("x", x_h, bank, c, ("o_turn", c))

            def x_ffn1(b, m):
                bank = bank_of("x", "ffn1", m)
                pe.wait_ge(*emptied("x", b, "ffn1", m))
                pe.wait_ge(*after("x_o_lo", b, DC))
                n = slice(m * P, (m + 1) * P)
                split3(pe, bank[:, :], lambda c: w1_hi[:, c, n], lambda c: w1_lo[:, c, n],
                       lambda c: x_fr[:, c, :], lambda c: x_fr[:, 2 + c, :], [(c, c) for c in range(DC)])\
                    .then_inc(full("x", "ffn1", m), 1)

            def x_ffn2(b, p):
                bank = bank_of("x", "ffn2", p)
                pe.wait_ge(*emptied("x", b, "ffn2", p))
                pe.wait_ge(*after("x_hidden", b, 2))
                for i in (0, 1):
                    for m in range(DC):
                        last = pe.matmul(bank[:, i * D:(i + 1) * D], whx[:, m, 1 + p, i * P:(i + 1) * P],
                                         w2_sb[:, m, :], start=(m == 0), stop=(m == DC - 1))
                last.then_inc(full("x", "ffn2", p), 1)

            def y_turn(b, n, c):
                bank = bank_of("y", "turn", n, c)
                pe.wait_ge(*emptied("y", b, "turn", n, c))
                pe.wait_ge(*after("y_norm", b, (n + 1) * NI))
                turned("y", y_h, bank, c, ("turn", n, c))

            def y_l1_proj(b, p):
                bank = bank_of("y", "l1_proj", p)
                pe.wait_ge(*emptied("y", b, "l1_proj", p))
                pe.wait_ge(*after("y_hi0", b, DC))
                for i in (0, 1):
                    for c in range(DC):
                        last = pe.matmul(bank[:, i * W1C:(i + 1) * W1C], y_t[:, c, (2 * p + i) * P:(2 * p + i + 1) * P],
                                         wl1[:, c, :], start=(c == 0), stop=(c == DC - 1))
                last.then_inc(full("y", "l1_proj", p), 1)

            def y_l1_f2row(b):
                bank = bank_of("y", "f2row")
                pe.wait_ge(*emptied("y", b, "f2row"))
                pe.wait_ge(*after("y_wh", b, 2))
                broadcast("y", lambda i: wh1[:, i, D1 + 1:D1 + 2], bank, ("f2row",))

            def y_l1_rows(b):
                bank = bank_of("y", "arow")
                pe.wait_ge(*emptied("y", b, "arow"))
                pe.wait_ge(*after("y_small", b, 6))
                broadcast("y", lambda i: YT["a"][:, i, 0:1], bank, ("arow",))
                bank = bank_of("y", "brow")
                pe.wait_ge(*emptied("y", b, "brow"))
                broadcast("y", lambda i: YT["b"][:, i, 0:1], bank, ("brow",))

            def y_l1_pv(b, p):
                bank = bank_of("y", "l1_pv", p)
                pe.wait_ge(*emptied("y", b, "l1_pv", p))
                pe.wait_ge(*after("y_prob", b, NI))
                for i in (0, 1):
                    for j in range(NI):
                        last = pe.matmul(bank[:, i * 256:i * 256 + D1 + 3], yp[:, j, (2 * p + i) * P:(2 * p + i + 1) * P],
                                         wh1[:, j, 0:D1 + 3], start=(j == 0), stop=(j == NI - 1))
                last.then_inc(full("y", "l1_pv", p), 1)

            def y_qk(b, g, t):
                bank = bank_of("y", "qk", g, t)
                pe.wait_ge(*emptied("y", b, "qk", g, t))
                pe.wait_ge(*after("y_lo", b, DC))
                w_hi, w_lo = sq[("wq", "wk")[t]]
                n = slice(g * P, (g + 1) * P)
                split3(pe, bank[:, :], lambda c: w_hi[:, c, n], lambda c: w_lo[:, c, n],
                       lambda c: y_fr[:, c, :], lambda c: y_fr[:, 2 + c, :], [(c, c) for c in range(DC)])\
                    .then_inc(full("y", "qk", g, t), 1)

            def nodes_by(b, key, p, name):
                bank = bank_of("y", *key)
                pe.wait_ge(*emptied("y", b, *key))
                w_hi, w_lo = sq[name]
                for i in (0, 1):
                    n = slice((2 * p + i) * P, (2 * p + i + 1) * P)
                    last = split3(pe, bank[:, i * D:(i + 1) * D], lambda c: y_fr[:, c, n], lambda c: y_fr[:, 2 + c, n],
                                  lambda c: w_hi[:, c, :], lambda c: w_lo[:, c, :], [(c, c) for c in range(DC)])
                last.then_inc(full("y", *key), 1)

            def y_v_(b, p):
                nodes_by(b, ("v", p), p, "wv")

            def y_near(b, g, h, i):
                bank = bank_of("y", "near", g, h, i)
                pe.wait_ge(*emptied("y", b, "near", g, h, i))
                if h == 0 and i == 0:
                    pe.wait_ge(*after("y_stacked", b, 16 * 6 * G * (g + 1)))
                pe.matmul(bank[:, :], qs[0:3 * DH, h, i * P:(i + 1) * P], ks[0:3 * DH, h, :], start=True, stop=True)\
                    .then_inc(full("y", "near", g, h, i), 1)

            def y_max_turn(b, g):
                bank = bank_of("y", "max_turn", g)
                pe.wait_ge(*emptied("y", b, "max_turn", g))
                pe.wait_ge(*after("y_near_max", b, (g + 1) * G * NI))
                pe.transpose(bank[0:G * NI, 0:P], max2[:, :], ident[:, :]).then_inc(full("y", "max_turn", g), 1)

            def y_far(b, g, k, h):
                bank = bank_of("y", "far", g, k, h)
                pe.wait_ge(*emptied("y", b, "far", g, k, h))
                if k == 0 and h == 0:
                    pe.wait_ge(*after("y_max_row", b, 32 * (g + 1)))
                pe.matmul(bank[:, :], ks[0:3 * DH + 2, h, k * P:(k + 1) * P], qs[0:3 * DH + 2, h, :],
                          start=True, stop=False)
                pe.matmul(bank[:, :], ident_b[:, :], mask_t[:, k, :], start=False, stop=True)\
                    .then_inc(full("y", "far", g, k, h), 1)

            def y_far_pv(b, g, k, h):
                if k == 0 and h == 0:
                    pe.wait_ge(*emptied("y", b, "far_sum", g))
                    pe.wait_ge(*emptied("y", b, "far_ctx", g))
                    if g == 0:
                        pe.wait_ge(*after("y_v", b, 2))
                n = (g * NI + k) * G + h
                pe.wait_ge(*after("y_far_prob", b, n + 1))
                q = slice(DH * h, DH * (h + 1))
                probs = yp[:, n % YRING, :]
                f = (g * G + h) * DH
                a = pe.matmul(YB[2][q, :], ones[:, :], probs, start=(k == 0), stop=(k == NI - 1))
                c = pe.matmul(YB[3][q, :], y_v[:, k, f:f + DH], probs, start=(k == 0), stop=(k == NI - 1))
                if k == NI - 1 and h == G - 1:
                    a.then_inc(full("y", "far_sum", g), 1)
                    c.then_inc(full("y", "far_ctx", g), 1)

            def y_o_proj(b, p):
                bank = bank_of("y", "o_proj", p)
                pe.wait_ge(*emptied("y", b, "o_proj", p))
                pe.wait_ge(*after("y_ctx", b, NG))
                for i in (0, 1):
                    for c in range(DC):
                        last = pe.matmul(bank[:, i * D:(i + 1) * D], y_t[:, c, (2 * p + i) * P:(2 * p + i + 1) * P],
                                         wo_sb[:, c, :], start=(c == 0), stop=(c == DC - 1))
                last.then_inc(full("y", "o_proj", p), 1)

            def y_mj(b, p):
                pe.wait_ge(*after("y_lo", b, 2 * DC))
                nodes_by(b, ("mj", p), p, "wj")

            def y_mi(b, p):
                nodes_by(b, ("mi", p), p, "wi")

            def y_gather(b, p):
                bank = bank_of("y", "gather", p)
                pe.wait_ge(*emptied("y", b, "gather", p))
                pe.wait_ge(*after("y_mj_lo", b, 2))
                for i in (0, 1):
                    n = slice((2 * p + i) * P, (2 * p + i + 1) * P)
                    for j in range(NI):
                        for part in (0, 2):
                            mj = qk_part[:, part + j // 2, (j % 2) * D:(j % 2 + 1) * D]
                            last = pe.matmul(bank[:, i * D:(i + 1) * D], adjt[:, j, n], mj,
                                             start=(j == 0 and part == 0), stop=(j == NI - 1 and part == 2))
                last.then_inc(full("y", "gather", p), 1)

            turns(pe, {"x_turn": x_turn, "x_proj": x_proj, "x_f2row": x_f2row, "x_rows": x_rows, "x_pv": x_pv,
                       "x_h_turn": x_h_turn, "x_proj2": x_proj2, "x_o_turn": x_o_turn, "x_ffn1": x_ffn1,
                       "x_ffn2": x_ffn2, "y_turn": y_turn, "y_l1_proj": y_l1_proj, "y_l1_f2row": y_l1_f2row,
                       "y_l1_rows": y_l1_rows, "y_l1_pv": y_l1_pv, "y_qk": y_qk, "y_v": y_v_, "y_near": y_near,
                       "y_max_turn": y_max_turn, "y_far": y_far, "y_far_pv": y_far_pv, "y_o_proj": y_o_proj,
                       "y_mj": y_mj, "y_mi": y_mi, "y_gather": y_gather}, "pe")

        @block.vector
        def _(dve):
            done = [0]

            def step(ins):
                done[0] += 1
                ins.then_inc(s_split, 1)

            def settle():
                dve.wait_ge(s_split, done[0])

            dve.wait_ge(s_load, 16 * N_LOADS)
            a1 = a_st[:, 0:1024].rearrange("p (h o) -> p h o", h=NH)
            a2 = a_st2[:, 0:1024].rearrange("p (h o) -> p h o", h=NH)
            scratch = qk_part[:, 0, 0:D].bitcast(F32)
            scratch = elu_e[:, 1, :]
            for c in range(DC):
                for h in range(NH):
                    for s, a in ((0, a1), (1, a2)):
                        step(dve.tensor_tensor_reduce(scratch, w_st[:, c, h, 0:D], a[:, h, :], 1.0, 0.0,
                                                      ALU.mult, ALU.add, w_st[:, c, h, D + s:D + s + 1]))
                        settle()
            for k in range(NH * DC):
                st = (ysx if k < 4 else ysv)[:, (k % 4) * D:(k % 4 + 1) * D]
                step(dve.tensor_copy(wo2_hi[:, k, 0:D], st))
                settle()
                step(dve.tensor_tensor(wo2_lo[:, k, 0:D], st, wo2_hi[:, k, 0:D].bitcast(F32), ALU.subtract))
                for s in (0, 1):
                    step(dve.tensor_tensor_reduce(scratch, st, brow[:, s * D:(s + 1) * D], 1.0, 0.0, ALU.mult,
                                                  ALU.add, XT["max"][:, s, 0:1]))
                    settle()
                    step(dve.tensor_copy(wo2_hi[:, k, D + s:D + s + 1], XT["max"][:, s, 0:1]))
                    settle()
                    step(dve.tensor_tensor(wo2_lo[:, k, D + s:D + s + 1], XT["max"][:, s, 0:1],
                                           wo2_hi[:, k, D + s:D + s + 1].bitcast(F32), ALU.subtract))
                    settle()
            for c in range(DC):
                for s in (0, 1):
                    step(dve.tensor_tensor_reduce(scratch[:, 0:D1], wl1[:, c, 0:D1], elu_e[:, 0, s * D1:(s + 1) * D1],
                                                  1.0, 0.0, ALU.mult, ALU.add, wl1[:, c, D1 + s:D1 + s + 1]))
                    settle()
            for hi, lo, st in [(wh_hi, wh_lo, w_st), (w1_hi, w1_lo, w1_st)] + [sq[n] + (sq_st[n],) for n in sq]:
                full_ = (slice(None),) * len(st.shape)
                step(dve.tensor_copy(hi[full_], st))
                settle()
                step(dve.tensor_tensor(lo[full_], st, hi[full_].bitcast(F32), ALU.subtract))
            step(dve.tensor_scalar(mask_n[:, :, :], adj_i, 0.0, MASKED, ALU.is_le, ALU.mult))
            for k in (0, 1):
                step(dve.tensor_scalar(mask_t[:, 2 * k:2 * k + 2, :], adj_t_i[k], 0.0, MASKED, ALU.is_le, ALU.mult))
                step(dve.tensor_copy(adjt[:, 2 * k:2 * k + 2, :], adj_t_i[k]))
            settle()
            for i in range(NI):
                step(dve.tensor_copy(elu_e[:, :, :].rearrange("p a b -> p (a b)"), adj_i[:, i, :]))
                settle()
                step(dve.reduce_sum(deg[:, i:i + 1], elu_e[:, :, :].rearrange("p a b -> p (a b)"), AX_X))
                settle()
            step(dve.memset(ks[3 * DH:P, :, :].bitcast(F32), 1.0))
            step(dve.memset(whx[:, :, :, D + 2:D + 4], 1.0))
            step(dve.memset(wh1[:, :, D1 + 2:D1 + 4], 1.0))
            settle()
            dve.memset(y_junk[:, :, 0:2], 0.0).then_inc(s_init, 1)
            dve.wait_ge(s_init, 1)

            def apart():
                dve.sem_inc(s_apart, 1)

            def stats(chain, T, source):
                def go(b, n):
                    source(b, n)
                    src = {("x", 0): x_in, ("x", 1): x_h}.get((chain, n), y_x)
                    for i in range(NI):
                        dve.bn_stats(T["stats"][:, i, :], src[:, i, :]).then_inc(S[f"{chain}_stats"], 1)
                    for i in range(NI):
                        dve.wait_ge(*after(f"{chain}_stats", b, n * NI + i + 1))
                        apart()
                        dve.bn_aggr(T["mv"][:, i, :], T["stats"][:, i, :]).then_inc(S[f"{chain}_aggr"], 1)
                    dve.wait_ge(*after(f"{chain}_aggr", b, (n + 1) * NI))
                    dve.tensor_scalar(T["var"][:, :], T["mv"][:, :, 1], LN_EPS, None, ALU.add)\
                        .then_inc(S[f"{chain}_var"], 1)
                return go

            def shift(chain, T):
                def go(b, n):
                    dve.wait_ge(*after(f"{chain}_rstd", b, n + 1))
                    dve.scalar_tensor_tensor(out=T["shift"][:, :], in0=T["mv"][:, :, 0], scalar=-1.0,
                                             in1=T["rstd"][:, :], op0=ALU.mult, op1=ALU.mult)\
                        .then_inc(S[f"{chain}_shift"], 1)
                return go

            def x_source(b, n):
                if n == 0:
                    dve.wait_ge(*after("x_in_loaded", b, 16))
                else:
                    dve.wait_ge(*after("x_ffn", b, 2))

            def y_source(b, n):
                if n == 0:
                    dve.wait_ge(*after("x_out", b, 1))
                elif n == 1:
                    dve.wait_ge(*after("y_l1", b, NI))
                    dve.wait_ge(*after("y_wh_added", b, 1))
                else:
                    dve.wait_ge(*after("y_o", b, 2))

            def x_lo(b, c):
                bank = bank_of("x", "turn", c)
                dve.wait_ge(*filled("x", b, "turn", c))
                dve.wait_ge(*after("x_hi", b, c + 1))
                dve.tensor_tensor(x_fr[:, 2 + c, :], bank[:, :], x_fr[:, c, :].bitcast(F32), ALU.subtract)\
                    .then_inc(S["x_lo"], 1)

            def x_rowmax(b, h):
                bank = bank_of("x", "f2row", h)
                dve.wait_ge(*filled("x", b, "f2row", h))
                if h == NH:
                    dve.wait_ge(*after("x_elu", b, NH * NI))
                apart()
                for i in range(NI):
                    n = h * NI + i
                    if n >= 2:
                        dve.wait_ge(*after("x_rowmax", b, n - 1))
                        apart()
                    dve.tensor_tensor_reduce(x_junk[:, n % 2, :], mask_n[:, i, :], bank[:, :], 1.0, LOWEST, ALU.add, ALU.max,
                                             XT["max"][:, i, h:h + 1]).then_inc(S["x_rowmax"], 1)

            def offsets(chain, T, b, n, f1, f2, hs):
                name, slope = f"{chain}_small", SLOPE[chain]
                v = {k: T[k][:, :, hs] for k in ("max", "sum", "m", "a", "b", "c", "d")}
                dve.tensor_scalar(v["c"], f2, 1.0 - slope, None, ALU.mult).then_inc(S[name], 1)
                dve.tensor_scalar(v["d"], f2, slope, None, ALU.mult).then_inc(S[name], 1)
                dve.tensor_tensor(v["sum"], v["max"], f1, ALU.add).then_inc(S[name], 1)
                dve.wait_ge(*after(name, b, n + 3))
                dve.scalar_tensor_tensor(out=v["m"], in0=v["sum"], scalar=slope, in1=v["sum"], op0=ALU.mult,
                                         op1=ALU.max).then_inc(S[name], 1)
                dve.wait_ge(*after(name, b, n + 4))
                dve.tensor_tensor(v["a"], f1, v["m"], ALU.subtract).then_inc(S[name], 1)
                dve.scalar_tensor_tensor(out=v["b"], in0=f1, scalar=slope, in1=v["m"], op0=ALU.mult,
                                         op1=ALU.subtract).then_inc(S[name], 1)

            def x_offsets(b, n):
                hs = slice(0, NH) if n == 0 else slice(NH, NH + 1)
                heads = slice(0, NH) if n == 0 else slice(0, 1)
                dve.wait_ge(*after("x_rowmax", b, NH * NI if n == 0 else (NH + 1) * NI))
                offsets("x", XT, b, 6 * n, whx[:, :, heads, D], whx[:, :, heads, D + 1], hs)

            def x_score(b, h, j):
                n = h * NI + j
                if j == 0:
                    bank = bank_of("x", "arow", h)
                    dve.wait_ge(*filled("x", b, "arow", h))
                    dve.wait_ge(*after("x_brow", b, h + 1))
                    dve.wait_ge(*after("x_small", b, 6 if h < NH else 12))
                if n >= XRING and (j == 0 or (n - XRING) % NI == 0):
                    dve.wait_ge(*filled("x", b, "pv", (n - XRING) // NI, NI - 1))
                bank = XB[XU[("arow", h)][0]]
                dve.scalar_tensor_tensor(out=xp[:, n % XRING, :], in0=bank[:, :], scalar=XT["c"][:, j, h:h + 1],
                                         in1=brow[:, :], op0=ALU.add, op1=ALU.max).then_inc(S["x_score"], 1)

            def x_recip(b, h, i):
                bank = bank_of("x", "pv", h, i)
                dve.wait_ge(*filled("x", b, "pv", h, i))
                dve.reciprocal(x_r[:, i:i + 1], bank[:, D + 2:D + 3]).then_inc(S["x_recip"], 1)

            def x_elu(b, h, i):
                n = h * NI + i
                dve.wait_ge(*after("x_elu_exp", b, n + 1))
                dve.tensor_scalar(elu_e[:, n % 2, :], elu_e[:, n % 2, :], 1.0, 1.0, ALU.min, ALU.subtract)\
                    .then_inc(S["x_elu_shift"], 1)
                dve.wait_ge(*after("x_elu_shift", b, n + 1))
                if h:
                    if i == 0 and h < NH:
                        dve.wait_ge(*filled("x", b, "h_turn", h - 1, 1))
                bank = XB[XU[("pv", h, i)][0]]
                dve.scalar_tensor_tensor(out=x_h[:, i, :], in0=bank[:, 0:D], scalar=x_r[:, i:i + 1],
                                         in1=elu_e[:, n % 2, :], op0=ALU.mult, op1=ALU.max)\
                    .then_inc(S["x_elu"], 1)

            def x_h_lo(b, h, c):
                bank = bank_of("x", "h_turn", h, c)
                dve.wait_ge(*filled("x", b, "h_turn", h, c))
                dve.wait_ge(*after("x_h_hi", b, 2 * h + c + 1))
                k = (h % 2) * 2 + c
                dve.tensor_tensor(x_fr[:, 4 + k, :], bank[:, :], x_fr[:, k, :].bitcast(F32), ALU.subtract)\
                    .then_inc(S["x_h_lo"], 1)

            def x_wh2(b, p, i):
                bank = bank_of("x", "proj2", p, i)
                dve.wait_ge(*filled("x", b, "proj2", p, i))
                dve.wait_ge(*after("x_wh2a", b, NI))
                dve.tensor_tensor(whx[:, i, 0, 0:W0], bank[:, 0:W0], whx[:, i, 0, 0:W0], ALU.add)\
                    .then_inc(S["x_wh2b"], 1)

            def x_o_lo(b, c):
                bank = bank_of("x", "o_turn", c)
                dve.wait_ge(*filled("x", b, "o_turn", c))
                dve.wait_ge(*after("x_o_hi", b, c + 1))
                dve.tensor_tensor(x_fr[:, 2 + c, :], bank[:, :], x_fr[:, c, :].bitcast(F32), ALU.subtract)\
                    .then_inc(S["x_o_lo"], 1)

            def x_ffn_sum(b, p):
                bank = bank_of("x", "ffn2", p)
                dve.wait_ge(*filled("x", b, "ffn2", p))
                dve.wait_ge(*after("x_b2", b, 1))
                part = x_h[:, 2 * p:2 * p + 2, :]
                ins = dve.tensor_tensor(part, bank[:, :].rearrange("p (a n) -> p a n", a=2), part, ALU.add)
                ins.then_inc(S["x_ffn"], 1)

            def x_out(b):
                dve.wait_ge(*after("x_gain", b, 1))
                dve.wait_ge(*after("x_beta", b, 1))
                dve.wait_ge(*after("y_stored", b, 0))
                dve.tensor_tensor(y_x[:, :, :], x_h[:, :, :], x_in[:, :, :], ALU.add).then_inc(S["x_out"], 1)

            def y_lo(b, n, c):
                bank = bank_of("y", "turn", n, c)
                dve.wait_ge(*filled("y", b, "turn", n, c))
                dve.wait_ge(*after("y_hi", b, 2 * (n - 1) + c + 1))
                dve.tensor_tensor(y_fr[:, 2 + c, :], bank[:, :], y_fr[:, c, :].bitcast(F32), ALU.subtract)\
                    .then_inc(S["y_lo"], 1)

            def y_l1_rowmax(b):
                bank = bank_of("y", "f2row")
                dve.wait_ge(*filled("y", b, "f2row"))
                apart()
                for i in range(NI):
                    if i >= 2:
                        dve.wait_ge(*after("y_rowmax", b, i - 1))
                        apart()
                    dve.tensor_tensor_reduce(y_junk[:, i % 2, :], mask_n[:, i, :], bank[:, :], 1.0, LOWEST, ALU.add, ALU.max,
                                             YT["max"][:, i, 0:1]).then_inc(S["y_rowmax"], 1)

            def y_l1_offsets(b):
                dve.wait_ge(*after("y_rowmax", b, NI))
                offsets("y", YT, b, 0, wh1[:, :, D1:D1 + 1], wh1[:, :, D1 + 1:D1 + 2], slice(0, 1))

            def y_l1_score(b, j):
                if j == 0:
                    dve.wait_ge(*filled("y", b, "arow"))
                    dve.wait_ge(*after("y_brow", b, 1))
                    dve.wait_ge(*after("y_small", b, 6))
                bank = YB[YU[("arow",)][0]]
                dve.scalar_tensor_tensor(out=yp[:, j, :], in0=bank[:, :], scalar=YT["c"][:, j, 0:1],
                                         in1=y_v[:, 0:2, :].rearrange("p a n -> p (a n)"), op0=ALU.add, op1=ALU.max)\
                    .then_inc(S["y_score"], 1)

            def y_l1_sum(b, p):
                bank = bank_of("y", "l1_pv", p)
                dve.wait_ge(*filled("y", b, "l1_pv", p))
                for i in (0, 1):
                    k = 2 * p + i
                    dve.reciprocal(y_r[:, k:k + 1], bank[:, i * 256 + D1 + 2:i * 256 + D1 + 3]).then_inc(S["y_recip"], 1)
                for i in (0, 1):
                    k = 2 * p + i
                    dve.wait_ge(*after("y_recip", b, k + 1))
                    dve.scalar_tensor_tensor(out=y_x[:, k, 0:D1], in0=bank[:, i * 256:i * 256 + D1],
                                             scalar=y_r[:, k:k + 1], in1=y_x[:, k, 0:D1], op0=ALU.mult, op1=ALU.add)\
                        .then_inc(S["y_l1"], 1)

            def y_qk_lo(b, g, t):
                bank = bank_of("y", "qk", g, t)
                dve.wait_ge(*filled("y", b, "qk", g, t))
                dve.wait_ge(*after("y_qk_hi", b, 2 * g + t + 1))
                dve.scalar_tensor_tensor(out=qk_part[:, 2 * t + 1, :], in0=bank[:, :],
                                         scalar=(bq_col, bk_col)[t][:, g:g + 1], in1=qk_part[:, 2 * t, :].bitcast(F32),
                                         op0=ALU.add, op1=ALU.subtract).then_inc(S["y_qk_lo"], 1)

            def y_v_sum(b, p):
                bank = bank_of("y", "v", p)
                dve.wait_ge(*filled("y", b, "v", p))
                dve.tensor_tensor(y_v[:, 2 * p:2 * p + 2, :], bank[:, :].rearrange("p (a n) -> p a n", a=2),
                                  rows["bv"][:, None, :].broadcast_to([P, 2, D]), ALU.add).then_inc(S["y_v"], 1)

            def y_near_max(b, g, h, i):
                bank = bank_of("y", "near", g, h, i)
                dve.wait_ge(*filled("y", b, "near", g, h, i))
                n = h * NI + i
                if g or n >= 2:
                    dve.wait_ge(*after("y_near_max", b, g * G * NI + n - 1))
                apart()
                dve.tensor_tensor_reduce(y_junk[:, n % 2, :], mask_n[:, i, :], bank[:, :], 1.0, LOWEST, ALU.add, ALU.max,
                                         max2[:, n:n + 1]).then_inc(S["y_near_max"], 1)

            def y_max_lo(b, g):
                bank = bank_of("y", "max_turn", g)
                dve.wait_ge(*filled("y", b, "max_turn", g))
                dve.wait_ge(*after("y_max_hi", b, g + 1))
                dve.scalar_tensor_tensor(out=negm[:, 1, :], in0=bank[0:G * NI, 0:P], scalar=-1.0,
                                         in1=negm[:, 0, :].bitcast(F32), op0=ALU.mult, op1=ALU.subtract)\
                    .then_inc(S["y_max_lo"], 1)

            def y_far_recip(b, g):
                bank = bank_of("y", "far_sum", g)
                dve.wait_ge(*filled("y", b, "far_sum", g))
                dve.reciprocal(y_h[:, 0:2, :].rearrange("p a n -> p (a n)"), bank[:, :]).then_inc(S["y_frecip"], 1)

            def y_far_norm(b, g):
                bank = bank_of("y", "far_ctx", g)
                dve.wait_ge(*filled("y", b, "far_ctx", g))
                dve.wait_ge(*after("y_frecip", b, g + 1))
                dve.tensor_tensor(y_t[:, g, :], bank[:, :], y_h[:, 0:2, :].rearrange("p a n -> p (a n)"), ALU.mult)\
                    .then_inc(S["y_ctx"], 1)

            def y_o_sum(b, p):
                bank = bank_of("y", "o_proj", p)
                dve.wait_ge(*filled("y", b, "o_proj", p))
                dve.wait_ge(*after("y_bo", b, 1))
                part = y_x[:, 2 * p:2 * p + 2, :]
                dve.tensor_tensor(part, bank[:, :].rearrange("p (a n) -> p a n", a=2), part, ALU.add)\
                    .then_inc(S["y_o"], 1)

            def y_mj_sum(b, p):
                bank = bank_of("y", "mj", p)
                dve.wait_ge(*filled("y", b, "mj", p))
                dve.tensor_tensor(y_h[:, 2 * p:2 * p + 2, :], bank[:, :].rearrange("p (a n) -> p a n", a=2),
                                  rows["b3"][:, None, :].broadcast_to([P, 2, D]), ALU.add).then_inc(S["y_mj_sum"], 1)

            def y_mj_lo(b, p):
                dve.wait_ge(*after("y_mj_hi", b, p + 1))
                dve.tensor_tensor(qk_part[:, 2 + p, :], y_h[:, 2 * p:2 * p + 2, :].rearrange("p a n -> p (a n)"),
                                  qk_part[:, p, :].bitcast(F32), ALU.subtract).then_inc(S["y_mj_lo"], 1)

            def y_mi_sum(b, p):
                bank = bank_of("y", "mi", p)
                dve.wait_ge(*filled("y", b, "mi", p))
                for i in (0, 1):
                    k = 2 * p + i
                    dve.scalar_tensor_tensor(out=y_x[:, k, :], in0=bank[:, i * D:(i + 1) * D],
                                             scalar=deg[:, k:k + 1], in1=y_x[:, k, :], op0=ALU.mult, op1=ALU.add)\
                        .then_inc(S["y_mi"], 1)

            def y_gather_sum(b, p):
                bank = bank_of("y", "gather", p)
                dve.wait_ge(*filled("y", b, "gather", p))
                dve.wait_ge(*after("y_mi", b, NI))
                part = y_x[:, 2 * p:2 * p + 2, :]
                dve.tensor_tensor(part, bank[:, :].rearrange("p (a n) -> p a n", a=2), part, ALU.add)\
                    .then_inc(S["y_out"], 1)

            turns(dve, {"x_stats": stats("x", XT, x_source), "x_shift": shift("x", XT), "x_lo": x_lo,
                        "x_rowmax": x_rowmax, "x_offsets": x_offsets, "x_score": x_score, "x_recip": x_recip,
                        "x_elu": x_elu, "x_h_lo": x_h_lo, "x_wh2": x_wh2, "x_o_lo": x_o_lo,
                        "x_ffn_sum": x_ffn_sum, "x_out": x_out, "y_stats": stats("y", YT, y_source),
                        "y_shift": shift("y", YT), "y_lo": y_lo, "y_l1_rowmax": y_l1_rowmax,
                        "y_l1_offsets": y_l1_offsets, "y_l1_score": y_l1_score, "y_l1_sum": y_l1_sum,
                        "y_qk_lo": y_qk_lo, "y_v_sum": y_v_sum, "y_near_max": y_near_max, "y_max_lo": y_max_lo,
                        "y_far_recip": y_far_recip, "y_far_norm": y_far_norm, "y_o_sum": y_o_sum,
                        "y_mj_sum": y_mj_sum, "y_mj_lo": y_mj_lo, "y_mi_sum": y_mi_sum,
                        "y_gather_sum": y_gather_sum}, "dve")


def kernel(**inputs):
    import numpy as _np
    import concourse.bacc as _bacc
    from concourse import mybir as _mybir
    from concourse.bass_utils import run_bass_kernel_spmd as _run

    g = {n: _np.asarray(a) for n, a in inputs.items()}
    D = g["x"].shape[-1]
    laid = {
        "x": g["x"], "adj": g["adj"], "adj_t": g["adj"].T,
        "w_heads": g["L0_gnn_W_heads"], "a_heads": g["L0_gnn_a_heads"], "w_out": g["L0_gnn_W_out"],
        "a_out": g["L0_gnn_a_out"], "w1": g["L0_gnn_w1"], "b1": g["L0_gnn_b1"], "w2": g["L0_gnn_w2"],
        "b2": g["L0_gnn_b2"], "gamma": g["L0_gnn_ln_gamma"], "beta": g["L0_gnn_ln_beta"],
        "l1_w": g["L1_gnn_W"], "l1_a": g["L1_gnn_a"],
        "wq_t": g["L2_gnn_Wq"].T, "bq": g["L2_gnn_bq"], "wk_t": g["L2_gnn_Wk"].T, "bk": g["L2_gnn_bk"],
        "wv_t": g["L2_gnn_Wv"].T, "bv": g["L2_gnn_bv"], "wo_t": g["L2_gnn_Wo"].T, "bo": g["L2_gnn_bo"],
        "wi_t": g["L3_gnn_W"][:, :D].T, "wj_t": g["L3_gnn_W"][:, D:].T, "b3": g["L3_gnn_b"],
    }
    nc = _bacc.Bacc("TRN2", target_bir_lowering=False, num_devices=1)
    arrays, args = {}, []
    for name, a in laid.items():
        a = _np.ascontiguousarray(a)
        arrays[f"in_{name}_dram"] = a
        args.append(nc.dram_tensor(f"in_{name}_dram", a.shape, _mybir.dt.from_np(a.dtype), kind="ExternalInput").ap())
    args.append(nc.dram_tensor("out_0_dram", g["x"].shape, _mybir.dt.float32, kind="ExternalOutput").ap())
    gnn_stack_kernel(nc, *args)
    r = _run(nc, [arrays], core_ids=[0])
    return r.results[0]["out_0_dram"]
```

```python
from contextlib import ExitStack

import concourse.bass as bass
from concourse import mybir

F32 = mybir.dt.float32
F32R = mybir.dt.float32r
BF16 = mybir.dt.bfloat16
I32 = mybir.dt.int32
ALU = mybir.AluOpType
ACT = mybir.ActivationFunctionType
AX_X = mybir.AxisListType.X

P = 128
MASKED = -1e30
LOWEST = -3e38
LN_EPS = 1e-5
SLOPE = {"x": 0.01, "y": 0.2}
XRING = 6
YRING = 4
QRING = 3


def x_steps(NI, NH):
    s = [(0, "pool", "residual", ())]
    for h in range(NH - 1):
        s += [(0.4, "pe", "f2row", (h,)), (2.4, "dve", "rowmax", (h,))]
    s += [(0.5, "pe", "f2row", (NH - 1,)), (2.4, "dve", "rowmax", (NH - 1,)),
          (0.8, "dve", "offsets", (0,))]

    def tiles(h, first, last):
        out = [(0.9, "pe", "rows", (h,)), (0.5, "act", "brow", (h,))] if first == 0 else []
        for j in range(first, last):
            out += [(0.7, "dve", "score", (h, j)), (0.6, "pool", "mask", (h, j)),
                    (0.2, "act", "prob", (h, j))]
        return out

    def aggregate(h):
        out = []
        for i in range(NI):
            out += [(1.7, "pe", "pv", (h, i)), (0, "dve", "recip", (h, i)), (0, "act", "elu_exp", (h, i))]
            if i:
                out += [(0, "dve", "elu", (h, i - 1))]
        return out + [(1.0, "dve", "elu", (h, NI - 1))]

    def turned(h):
        out = []
        for c in range(2):
            out += [(0.5, "pe", "h_turn", (h, c)), (0, "act", "h_hi", (h, c)), (0.5, "dve", "h_lo", (h, c))]
        return out

    s += tiles(0, 0, NI)
    early = XRING - NI
    for h in range(NH):
        a = aggregate(h)
        n = tiles(h + 1, 0, early) if h + 1 < NH else []
        k = 0
        for step in a:
            s.append(step)
            if step[1] == "pe":
                take = (len(n) + NI - 1) // NI
                s += [(0,) + t[1:] for t in n[k:k + take]]
                k += take
        s += [(0,) + t[1:] for t in n[k:]]
        s += turned(h)
        if h + 1 < NH:
            s += tiles(h + 1, early, NI)
        if h % 2:
            for i in range(NI):
                s += [(1.3, "pe", "proj2", (h // 2, i)), (0, "act" if h < 2 else "dve", "wh2", (h // 2, i))]
    s += [(0.5, "pe", "f2row", (NH,)), (2.6, "dve", "rowmax", (NH,)), (0.8, "dve", "offsets", (1,))]
    s += tiles(NH, 0, NI) + aggregate(NH)
    for c in range(2):
        s += [(0.5, "pe", "o_turn", (c,)), (0.5, "act", "o_hi", (c,)), (0.6, "dve", "o_lo", (c,))]
    s += [(0, "pool", "add_b2", ())]
    s += x_head(NI, NH)[0]
    for m in range(2):
        s += [(1.3, "pe", "ffn1", (m,)), (0.4, "act", "hidden", (m,))]
    for p in range(2):
        s += [(1.8, "pe", "ffn2", (p,)), (0.4, "dve", "ffn_sum", (p,))]
    own = [(1.5, "dve", "stats", (1,)), (1.0, "pool", "rstd", (1,)), (0.3, "dve", "shift", (1,)),
           (2.0, "act", "norm", (1,)), (2.3, "pool", "gain", ()), (1.5, "dve", "out", ())]
    ahead = x_head(NI, NH)[1]
    for n, step in enumerate(ahead):
        if n % 6 == 0 and own:
            s.append(own.pop(0))
        s.append(step)
    return s + own


def x_head(NI, NH):
    first = [(1.5, "dve", "next_stats", (0,)), (1.0, "pool", "next_rstd", (0,)), (0.3, "dve", "next_shift", (0,)),
             (2.0, "act", "next_norm", (0,))]
    second = []
    for c in range(2):
        second += [(0.5, "pe", "next_turn", (c,)), (0.5, "act", "next_hi", (c,)), (0.6, "dve", "next_lo", (c,))]
    for h in range(NH):
        for i in range(NI):
            second += [(0.6, "pe", "next_proj", (h, i)), (0, "act", "next_wh", (h, i))]
    return first, second


def y_steps(NI, NG, G):
    def norm(n):
        return [(1.5, "dve", "stats", (n,)), (1.0, "pool", "rstd", (n,)), (0.3, "dve", "shift", (n,)),
                (2.0, "act", "norm", (n,))]

    s = norm(0)
    for c in range(2):
        s += [(0.5, "pe", "turn", (0, c)), (0.5, "act", "hi", (0, c))]
    for p in range(2):
        s += [(0.9, "pe", "l1_proj", (p,)), (0.3, "act", "l1_wh", (p,))]
    s += [(0.5, "pe", "l1_f2row", ()), (2.5, "dve", "l1_rowmax", ()), (0.8, "dve", "l1_offsets", ()),
          (0.9, "pe", "l1_rows", ()), (0.5, "act", "l1_brow", ())]
    for j in range(NI):
        s += [(0.7, "dve", "l1_score", (j,)), (0.6, "pool", "l1_mask", (j,)), (0.2, "act", "l1_prob", (j,))]
    s += [(0, "pool", "l1_add_wh", ())]
    for p in range(2):
        s += [(1.8, "pe", "l1_pv", (p,)), (0.8, "dve", "l1_sum", (p,))]
    s += norm(1) + [(0, "pool", "add_bo", ())]
    for c in range(2):
        s += [(0.5, "pe", "turn", (1, c)), (0.5, "act", "hi", (1, c)), (0.6, "dve", "lo", (1, c))]

    def qk(g):
        out = []
        for t in range(2):
            out += [(1.3, "pe", "qk", (g, t)), (0.5, "act", "qk_hi", (g, t)), (0.6, "dve", "qk_lo", (g, t))]
        return out

    def qv():
        out = []
        for p in range(2):
            out += [(1.3, "pe", "v", (p,)), (0.5, "dve", "v_sum", (p,))]
        return out

    def stack(h):
        return [(0.45, "pe", "stack", (h, 0)), (0.2, "act", "stack_q", (h,)), (0.45, "pe", "stack", (h, 1)),
                (0.6, "dve", "stack_k", (h,))]

    def far(h, k):
        n = h * NI + k
        out = [(0.45, "pe", "far", (h, k)), (0.2, "act", "far_prob", (h, k))]
        if n % (G * NI) >= 2:
            out += [(0.45, "pe", "far_pv", divmod(n - 2, NI))]
        return out

    def near(h, i):
        return [(0.2, "pe", "near", (h, i)), (0.4, "dve", "near_max", (h, i))]

    H = NG * G
    s += qk(0) + stack(0) + qv()
    for h in range(H + 1):
        if h < H:
            s += near(h, 0) + near(h, 1)
        if h:
            s += far(h - 1, 0)
        if h < H:
            s += near(h, 2)
        if h:
            s += far(h - 1, 1)
        if h < H:
            s += near(h, 3)
        if h:
            s += far(h - 1, 2)
        if h < H:
            s += [(0.3, "pe", "max_turn", (h,)), (0.3, "act", "max_hi", (h,)), (0.3, "dve", "max_lo", (h,))]
        if h:
            s += far(h - 1, 3)
        if h and h % G == 0:
            g = h // G - 1
            s += [(0.3, "pe", "far_pv", (h - 1, NI - 2)), (0.3, "pe", "far_pv", (h - 1, NI - 1)),
                  (0.6, "act", "far_sums", (g,)), (0.1, "act", "far_ctx", (g,)), (0.5, "pe", "sum_turn", (g,)),
                  (0.6, "dve", "far_recip", (g,)), (0.5, "pe", "recip_rows", (g,)), (0.6, "dve", "far_norm", (g,))]
        if h + 1 < H:
            s += stack(h + 1)
        if h + 2 < H and (h + 2) % G == 0:
            s += qk((h + 2) // G)
    for p in range(2):
        s += [(1.8, "pe", "o_proj", (p,)), (0.5, "dve", "o_sum", (p,))]
    s += norm(2)
    for c in range(2):
        s += [(0.5, "pe", "turn", (2, c)), (0.5, "act", "hi", (2, c)), (0.6, "dve", "lo", (2, c))]
    for p in range(2):
        s += [(1.3, "pe", "mj", (p,)), (0.5, "dve", "mj_sum", (p,)), (0.3, "act", "mj_hi", (p,)), (0.5, "dve", "mj_lo", (p,))]
    for p in range(2):
        s += [(1.3, "pe", "mi", (p,)), (0.6, "dve", "mi_sum", (p,))]
    for p in range(2):
        s += [(1.8, "pe", "gather", (p,)), (0.6, "dve", "gather_sum", (p,))]
    return s


PACE = [0, 26, 32, 36, 39, 43, 46, 69, 87, 106, 125, 127, 134, 135, 142, 179, 197, 205, 216, 231, 265,
        282, 294, 301, 306, 312, 315, 317, 319, 319, 319]


def merged(xs, ys):
    parts = len(PACE) - 1
    marks = [round(len(xs) * k / parts) for k in range(parts + 1)]
    order, y = [], 0
    for k in range(parts if ys else 0):
        for n in range(marks[k], marks[k + 1]):
            due = int(PACE[k] + (PACE[k + 1] - PACE[k]) * (n - marks[k]) / (marks[k + 1] - marks[k]))
            order += [("y",) + s[1:] for s in ys[y:due]] + [("x",) + xs[n][1:]]
            y = max(y, due)
    return order + [("y",) + s[1:] for s in ys[y:]] if order else [("x",) + s[1:] for s in xs] + [("y",) + s[1:] for s in ys]


def gnn_stack_kernel(nc, x, adj, adj_t, w_heads, a_heads, w_out, a_out, w1, b1, w2, b2, gamma, beta,
                     l1_w, l1_a, wq_t, bq, wk_t, bk, wv_t, bv, wo_t, bo, wi_t, wj_t, b3, out):
    B, N, D = x.shape
    NI = N // P
    DC = D // P
    NH = w_heads.shape[0]
    D1 = l1_w.shape[1]
    HEADS2, DH = 8, 32
    G = P // DH
    NG = HEADS2 // G
    SCALE = float(DH) ** -0.5
    W0 = D + 2
    W1C = D1 + 2
    assert N == 512 and D == 256 and NI == 4 and DC == 2

    XS, YS = x_steps(NI, NH), y_steps(NI, NG, G)
    TOGETHER = merged(XS, YS)
    X_ALONE, Y_ALONE = merged(XS, []), merged([], YS)
    X_HEAD = merged(sum(x_head(NI, NH), []), [])
    LAST_TOGETHER = [step for step in TOGETHER if not step[2].startswith("next_")]

    ctx = ExitStack()
    with ctx:
        def sb(name, shape, dt=F32):
            return ctx.enter_context(nc.sbuf_tensor(name, shape, dt))

        def sem(name):
            return ctx.enter_context(nc.semaphore(name))

        wh_hi, wh_lo = sb("wh_hi", [P, DC, NH, W0], F32R), sb("wh_lo", [P, DC, NH, W0], F32R)
        wo2_hi, wo2_lo = sb("wo2_hi", [P, NH * DC, W0], F32R), sb("wo2_lo", [P, NH * DC, W0], F32R)
        w1_hi, w1_lo = sb("w1_hi", [P, DC, D], F32R), sb("w1_lo", [P, DC, D], F32R)
        w2_sb, wl1 = sb("w2_sb", [P, DC, D]), sb("wl1", [P, DC, W1C])
        sq = {n: (sb(f"{n}_hi", [P, DC, D], F32R), sb(f"{n}_lo", [P, DC, D], F32R))
              for n in ("wq", "wk", "wv", "wi", "wj")}
        wo_sb = sb("wo_sb", [P, DC, D])
        mask_n, mask_t = sb("mask_n", [P, NI, N], BF16), sb("mask_t", [P, NI, N], BF16)
        adjt = sb("adjt", [P, NI, N], F32R)
        ident, ident_b, ones = sb("ident", [P, P]), sb("ident_b", [P, P], BF16), sb("ones", [P, DH])
        rows = {n: sb(f"{n}_rows", [P, D]) for n in ("b2", "gamma", "beta", "bv", "bo", "b3")}
        b1_col, bq_col, bk_col = sb("b1_col", [P, DC]), sb("bq_col", [P, DC]), sb("bk_col", [P, DC])
        deg, power = sb("deg", [P, NI]), sb("power", [P, NI])

        def small(chain, heads):
            return {
                "stats": sb(f"{chain}_stats", [P, NI, 6]), "mv": sb(f"{chain}_mv", [P, NI, 2]),
                "var": sb(f"{chain}_var", [P, NI]), "rstd": sb(f"{chain}_rstd", [P, NI]),
                "shift": sb(f"{chain}_shift", [P, NI]), "max": sb(f"{chain}_max", [P, NI, heads]),
                "sum": sb(f"{chain}_f12", [P, NI, heads]), "m": sb(f"{chain}_m", [P, NI, heads]),
                "a": sb(f"{chain}_a", [P, NI, heads]), "b": sb(f"{chain}_b", [P, NI, heads]),
                "c": sb(f"{chain}_c", [P, NI, heads]), "d": sb(f"{chain}_d", [P, NI, heads]),
            }

        XT, YT = small("x", NH + 1), small("y", 1)
        XT0 = {"stats": sb("x0_stats", [P, NI, 6]), "mv": sb("x0_mv", [P, NI, 2]), "var": sb("x0_var", [P, NI]),
               "rstd": sb("x0_rstd", [P, NI]), "shift": sb("x0_shift", [P, NI])}

        x_in = sb("x_in", [P, NI, D])
        x_res = sb("x_res", [P, NI, D])
        x_h = sb("x_h", [P, NI, D])
        x_fr = sb("x_fr", [P, 8, N], F32R)
        whx = sb("whx", [P, NI, NH, D + 4])
        brow = sb("brow", [P, N])
        xp = sb("xp", [P, XRING, N])
        x_n = xp[:, 0:2, :].rearrange("p a (i d) -> p (a i) d", i=2)
        elu_e, x_r = sb("elu_e", [P, 2, D]), sb("x_r", [P, NI])
        y_x, y_h = sb("y_x", [P, NI, D]), sb("y_h", [P, NI, D])
        y_t, y_fr = sb("y_t", [P, DC, N]), sb("y_fr", [P, 4, N], F32R)
        wh1 = sb("wh1", [P, NI, D1 + 4])
        y_v = sb("y_v", [P, NI, D])
        x_junk, y_junk = elu_e[:, :, :].bitcast(BF16), sb("y_junk", [P, 2, N], BF16)
        yp = sb("yp", [P, YRING, N])
        qk_part = sb("qk_part", [P, 4, N], F32R)
        qs, ks = sb("qs", [P, QRING, N], F32R), sb("ks", [P, QRING, N], F32R)
        pick = sb("pick", [P, G, 7, DH], F32R)
        max2, y_r = sb("max2", [P, 2, NI]), sb("y_r", [P, NI])
        negm = sb("negm", [NI, 2, 2, P], F32R)
        y_rs = sb("y_rs", [P, NI, G])

        XB = [ctx.enter_context(nc.psum_tensor(f"x_bank{i}", [P, 512], F32)) for i in range(4)]
        YB = [ctx.enter_context(nc.psum_tensor(f"y_bank{i}", [P, 512], F32)) for i in range(4)]

        s_load, s_split, s_init = sem("weights_loaded"), sem("setup_step"), sem("constants_ready")
        s_id, s_apart = sem("identity_ready"), sem("wait_kept_apart")
        names = """x_in_loaded x0_stats x0_aggr x0_var x0_rstd x0_shift x0_norm x_stats x_aggr x_var x_rstd x_shift x_norm x_hi x_lo x_wh x_rowmax
        x_small x_brow x_score x_mask x_prob x_recip x_elu_exp x_elu_shift x_elu x_h_hi x_h_lo x_wh2a
        x_wh2b x_o_hi x_o_lo x_b2 x_hidden x_ffn x_gain x_res x_out
        y_stats y_aggr y_var y_rstd y_shift y_norm y_hi0 y_hi y_lo y_wh y_rowmax y_small y_brow y_score
        y_mask y_prob y_wh_added y_recip y_l1 y_bo y_qk_hi y_qk_lo y_v y_stack_q y_stack_k y_near_max y_max_hi y_max_lo
        y_max_row y_far_prob y_far_sums y_ctx0 y_frecip y_recip_wide y_ctx y_o y_mj_sum y_mj_hi y_mj_lo y_mi y_out y_stored""".split()
        S = {n: sem(n) for n in names}
        xfull = [sem(f"x_bank{i}_full") for i in range(4)]
        yfull = [sem(f"y_bank{i}_full") for i in range(4)]

        PER = {n: 1 for n in names}
        PER.update(x_in_loaded=16, x0_stats=NI, x0_aggr=NI, x0_norm=NI, x_stats=NI, x_aggr=NI, x_norm=NI, x_hi=2, x_lo=2, x_wh=NH * NI, x_rowmax=(NH + 1) * NI, x_small=12,
                   x_brow=NH + 1, x_score=(NH + 1) * NI, x_mask=(NH + 1) * NI, x_prob=(NH + 1) * NI,
                   x_recip=(NH + 1) * NI, x_elu_exp=(NH + 1) * NI, x_elu_shift=(NH + 1) * NI,
                   x_elu=(NH + 1) * NI, x_h_hi=NH * 2, x_h_lo=NH * 2, x_wh2a=NI, x_wh2b=NI, x_o_hi=2,
                   x_o_lo=2, x_hidden=2, x_ffn=2, y_stats=3 * NI, y_aggr=3 * NI, y_var=3, y_rstd=3,
                   y_shift=3, y_norm=3 * NI, y_hi0=2, y_hi=4, y_lo=4, y_wh=2, y_rowmax=NI, y_small=6,
                   y_score=NI, y_mask=NI, y_prob=NI, y_recip=NI, y_l1=NI, y_qk_hi=2 * NG,
                   y_qk_lo=2 * NG, y_v=2, y_stack_q=HEADS2, y_stack_k=HEADS2, y_near_max=HEADS2 * NI,
                   y_max_hi=HEADS2, y_max_lo=HEADS2, y_max_row=32 * HEADS2, y_far_prob=HEADS2 * NI,
                   y_far_sums=NG, y_ctx0=NG, y_frecip=NG, y_recip_wide=NG, y_ctx=NG, y_o=2, y_mj_sum=2, y_mj_hi=2, y_mj_lo=2, y_mi=NI, y_out=2, y_stored=16)

        def after(name, b, n):
            v = b * PER[name] + n
            return (s_init, 1) if isinstance(v, int) and v <= 0 else (S[name], v)

        def uses(order, chain, bank_of):
            found, per = {}, [0] * 4
            for c, engine, step, args in order:
                if c == chain and engine == "pe":
                    for key in bank_of(step, args):
                        bank = key[0] if key[0] is not None else (per[0] + per[1]) % 2
                        found[key[1]] = (bank, per[bank])
                        per[bank] += 1
            return found, per

        def x_bank_of(step, args):
            if step == "rows":
                return [(2, ("arow",) + args), (3, ("brow",) + args)]
            if step == "f2row":
                return [(2 + args[0] % 2, ("f2row",) + args)]
            return [(None, (step,) + args)]

        def y_bank_of(step, args):
            if step == "l1_rows":
                return [(2, ("arow",)), (3, ("brow",))]
            if step == "l1_f2row":
                return [(2, ("f2row",))]
            if step == "far_pv":
                h, k = args
                return [(2, ("far_sum", h // G)), (3, ("far_ctx", h // G))] if k == 0 and h % G == 0 else []
            return [(None, (step,) + args)]

        X_ORDER = [(c, e, step.replace("next_", ""), args) for c, e, step, args in
                   X_HEAD + [s for s in X_ALONE if not s[2].startswith("next_")]]
        XU, XN = uses(X_ORDER, "x", x_bank_of)
        YU, YN = uses(Y_ALONE, "y", y_bank_of)

        def x_released(key):
            k, a = key[0], key[1:]
            return {"turn": lambda: ("x_lo", a[0] + 1), "proj": lambda: ("x_wh", a[0] * NI + a[1] + 1),
                    "f2row": lambda: ("x_rowmax", (a[0] + 1) * NI), "arow": lambda: ("x_score", (a[0] + 1) * NI),
                    "brow": lambda: ("x_brow", a[0] + 1), "pv": lambda: ("x_elu", a[0] * NI + a[1] + 1),
                    "h_turn": lambda: ("x_h_lo", a[0] * 2 + a[1] + 1),
                    "proj2": lambda: ("x_wh2b" if a[0] else "x_wh2a", a[1] + 1),
                    "o_turn": lambda: ("x_o_lo", a[0] + 1), "ffn1": lambda: ("x_hidden", a[0] + 1),
                    "ffn2": lambda: ("x_ffn", a[0] + 1)}[k]()

        def y_released(key):
            k, a = key[0], key[1:]
            return {"turn": lambda: ("y_hi0", a[1] + 1) if a[0] == 0 else ("y_lo", (a[0] - 1) * 2 + a[1] + 1),
                    "l1_proj": lambda: ("y_wh", a[0] + 1), "f2row": lambda: ("y_rowmax", NI),
                    "arow": lambda: ("y_score", NI), "brow": lambda: ("y_brow", 1),
                    "l1_pv": lambda: ("y_l1", 2 * a[0] + 2),
                    "qk": lambda: ("y_qk_lo", a[0] * 2 + a[1] + 1), "v": lambda: ("y_v", a[0] + 1),
                    "stack": lambda: ("y_stack_k" if a[1] else "y_stack_q", a[0] + 1),
                    "near": lambda: ("y_near_max", a[0] * NI + a[1] + 1),
                    "max_turn": lambda: ("y_max_lo", a[0] + 1),
                    "far": lambda: ("y_far_prob", a[0] * NI + a[1] + 1),
                    "far_sum": lambda: ("y_far_sums", a[0] + 1), "far_ctx": lambda: ("y_ctx0", a[0] + 1),
                    "sum_turn": lambda: ("y_frecip", a[0] + 1), "recip_rows": lambda: ("y_ctx", a[0] + 1),
                    "o_proj": lambda: ("y_o", a[0] + 1), "mj": lambda: ("y_mj_sum", a[0] + 1),
                    "mi": lambda: ("y_mi", 2 * a[0] + 2), "gather": lambda: ("y_out", a[0] + 1)}[k]()

        def emptied(chain, b, *key):
            U, N_, released = (XU, XN, x_released) if chain == "x" else (YU, YN, y_released)
            bank, n = U[key]
            before = [k for k, v in U.items() if v == (bank, n - 1 if n else N_[bank] - 1)][0]
            name, count = released(before)
            if n:
                return after(name, b, count)
            return after(name, b, 0) if chain == "x" else after("x_out", b, 1)

        def bank_of(chain, *key):
            return (XB if chain == "x" else YB)[(XU if chain == "x" else YU)[key][0]]

        def full(chain, *key):
            bank, _ = (XU if chain == "x" else YU)[key]
            return (xfull if chain == "x" else yfull)[bank]

        def filled(chain, b, *key):
            U, N_, fulls = (XU, XN, xfull) if chain == "x" else (YU, YN, yfull)
            bank, n = U[key]
            return fulls[bank], b * N_[bank] + n + 1

        def split3(pe, outp, hi_l, lo_l, hi_r, lo_r, pairs, start=True, stop=True):
            todo = [(a, b_) for l, r in pairs for a, b_ in
                    ((hi_l(l), hi_r(r)), (hi_l(l), lo_r(r)), (lo_l(l), hi_r(r)))]
            for n, (a, b_) in enumerate(todo):
                last = pe.matmul(outp, a, b_, start=start and n == 0, stop=stop and n == len(todo) - 1)
            return last

        x_v = x.rearrange("b (i p) d -> b p i d", p=P)
        out_v = out.rearrange("b (i p) d -> b p i d", p=P)
        block = ctx.enter_context(nc.Block())

        def turns(engine, steps, name):
            def run(order, xb, yb):
                for chain, e, step, args in order:
                    if e == name:
                        graph = yb if chain == "y" else xb + 1 if step.startswith("next_") else xb
                        steps[chain + "_" + step](graph, *args)

            run(X_HEAD, -1, None)
            run(X_ALONE, 0, None)
            with engine.Fori(1, B - 1) as b:
                run(TOGETHER, b, b - 1)
            run(LAST_TOGETHER, B - 1, B - 2)
            run(Y_ALONE, None, B - 1)

        LOADS = 0
        st_w = whx[:, :, :, :].rearrange("p a b c -> p (a b c)")
        st_x = xp[:, :, :].rearrange("p a b -> p (a b)")
        st_y = yp[:, :, :].rearrange("p a b -> p (a b)")
        st_r = x_res[:, :, :].rearrange("p a b -> p (a b)")
        w_st = st_w[:, 0:DC * NH * W0].rearrange("p (c h o) -> p c h o", c=DC, h=NH)
        sq_st = {n: (st_x if k < 4 else st_r)[:, (k % 4) * 512:(k % 4) * 512 + 512].rearrange("p (c o) -> p c o", c=DC)
                 for k, n in enumerate(sq)}
        w1_st = y_h[:, 0:2, :]
        adj_i = st_y[:, 0:2048].bitcast(I32).rearrange("p (i n) -> p i n", i=NI)
        adj_t_i = [v.bitcast(I32).rearrange("p (i n) -> p i n", i=2)
                   for v in (y_t[:, :, :].rearrange("p a b -> p (a b)"), st_x[:, 2048:3072])]
        a_st = x_h[:, :, :].rearrange("p a b -> p (a b)")
        a_st2 = x_in[:, :, :].rearrange("p a b -> p (a b)")
        ysx, ysv = y_x[:, :, :].rearrange("p a b -> p (a b)"), y_v[:, :, :].rearrange("p a b -> p (a b)")

        @block.sync
        def _(sp):
            def load(dst, src, name=s_load):
                sp.dma_start(dst, src).then_inc(name, 16)

            for c in range(DC):
                load(w_st[:, c, :, 0:D], w_heads[:, c * P:(c + 1) * P, :].rearrange("h p o -> p h o"))
            load(a_st[:, 0:1024].rearrange("p (h o) -> p h o", h=NH), a_heads[:, 0:D].partition_broadcast(P))
            load(a_st2[:, 0:1024].rearrange("p (h o) -> p h o", h=NH), a_heads[:, D:2 * D].partition_broadcast(P))
            load(brow[:, :], a_out.partition_broadcast(P))
            load(elu_e[:, 0, :], l1_a.rearrange("s o u -> (s o u)").partition_broadcast(P))
            for c in range(DC):
                load(wl1[:, c, 0:D1], l1_w[c * P:(c + 1) * P, :])
                load(w2_sb[:, c, :], w2[c * P:(c + 1) * P, :])
                load(wo_sb[:, c, :], wo_t[c * P:(c + 1) * P, :])
                load(w1_st[:, c, :], w1[c * P:(c + 1) * P, :])
            for n, src in (("wq", wq_t), ("wk", wk_t), ("wv", wv_t), ("wi", wi_t), ("wj", wj_t)):
                load(sq_st[n], src.rearrange("(c p) o -> p c o", p=P))
            load(adj_i, adj.rearrange("(i p) n -> p i n", p=P))
            for n, src in (("b2", b2), ("gamma", gamma), ("beta", beta), ("bv", bv), ("bo", bo), ("b3", b3)):
                load(rows[n][:, :], src.partition_broadcast(P))
            for t, src in ((b1_col, b1), (bq_col, bq), (bk_col, bk)):
                sp.dma_start(t[:, :], src.rearrange("(c p) -> p c", p=P), allow_slow_non_contiguous=True)\
                    .then_inc(s_load, 16)
            load(ysx, w_out[0:4 * P, :].rearrange("(k p) o -> p k o", p=P))
            load(ysv, w_out[4 * P:8 * P, :].rearrange("(k p) o -> p k o", p=P))
            for k in (0, 1):
                load(adj_t_i[k], adj_t[2 * k * P:2 * (k + 1) * P, :].rearrange("(i p) n -> p i n", p=P))

            def x_load(b):
                sp.wait_ge(*after("x0_norm", b, 0))
                sp.wait_ge(*after("x_res", b, 0))
                sp.dma_start(x_in[:, :, :], x_v[b]).then_inc(S["x_in_loaded"], 16)

            def y_max_row(b, h):
                for r, name in ((0, "y_max_hi"), (1, "y_max_lo")):
                    sp.wait_ge(*after(name, b, h + 1))
                    sp.dma_start(qs[3 * DH + r:3 * DH + r + 1, h % QRING, :].rearrange("p (i n) -> p i n", i=NI).bitcast(F32),
                                 negm[:, h % 2, r, :].bitcast(F32)).then_inc(S["y_max_row"], 16)

            def y_store(b):
                sp.wait_ge(*after("y_out", b, 2))
                sp.dma_start(out_v[b], y_x[:, :, :]).then_inc(S["y_stored"], 16)

            sp.wait_ge(s_init, 1)
            x_load(0)
            x_load(1)

            def y_all(b):
                for h in range(HEADS2):
                    y_max_row(b, h)

            with sp.Fori(1, B - 1) as b:
                x_load(b + 1)
                y_all(b - 1)
                y_store(b - 1)
            y_all(B - 2)
            y_store(B - 2)
            y_all(B - 1)
            y_store(B - 1)
            sp.wait_ge(S["y_stored"], 16 * B)

        N_LOADS = DC + 4 + DC * 4 + 5 + 1 + 6 + 3 + 4

        @block.gpsimd
        def _(pool):
            pool.memset(ident[:, :], 0.0).then_inc(s_id, 1)
            pool.memset(ident_b[:, :], 0.0).then_inc(s_id, 1)
            pool.wait_ge(s_id, 2)
            for t in (ident, ident_b):
                pool.affine_select(out=t[:, :], in_=t[:, :], compare_op=ALU.not_equal, fill=1.0, base=0,
                                   pattern=[[-1, P]], channel_multiplier=1).then_inc(s_id, 1)
            pool.memset(ones[:, :], 1.0).then_inc(s_id, 1)
            pool.memset(power[:, :], -0.5).then_inc(s_id, 1)
            pool.wait_ge(s_id, 6)
            pool.wait_ge(s_init, 1)

            def rstd(chain, T, k):
                def step(b, n):
                    pool.wait_ge(*after(f"{chain}_var", b, (n if chain == "y" else 0) + 1))
                    pool.tensor_tensor(T["rstd"][:, :], T["var"][:, :], power[:, :], ALU.pow)\
                        .then_inc(S[f"{chain}_rstd"], 1)
                return step

            def x_mask(b, h, j):
                n = h * NI + j
                pool.wait_ge(*after("x_score", b, n + 1))
                pool.tensor_tensor(xp[:, n % XRING, :], xp[:, n % XRING, :], mask_t[:, j, :], ALU.add)\
                    .then_inc(S["x_mask"], 1)

            def x_add_b2(b):
                pool.wait_ge(*filled("x", b, "o_turn", 1))
                pool.wait_ge(*after("x_elu", b, (NH + 1) * NI))
                pool.tensor_tensor(x_h[:, :, :], x_h[:, :, :], rows["b2"][:, None, :].broadcast_to([P, NI, D]),
                                   ALU.add).then_inc(S["x_b2"], 1)

            def x_residual(b):
                pool.wait_ge(*after("x_in_loaded", b, 16))
                pool.wait_ge(*after("x_out", b, 0))
                pool.tensor_tensor(x_res[:, :, :], x_in[:, :, :], rows["beta"][:, None, :].broadcast_to([P, NI, D]),
                                   ALU.add).then_inc(S["x_res"], 1)

            def x_gain(b):
                pool.wait_ge(*after("x_norm", b, NI))
                pool.tensor_tensor(x_h[:, :, :], x_h[:, :, :], rows["gamma"][:, None, :].broadcast_to([P, NI, D]),
                                   ALU.mult).then_inc(S["x_gain"], 1)

            def y_l1_mask(b, j):
                pool.wait_ge(*after("y_score", b, j + 1))
                pool.tensor_tensor(yp[:, j, :], yp[:, j, :], mask_t[:, j, :], ALU.add).then_inc(S["y_mask"], 1)

            def y_l1_add_wh(b):
                pool.wait_ge(*after("y_norm", b, NI))
                pool.wait_ge(*after("y_wh", b, 2))
                pool.tensor_tensor(y_x[:, :, D1:D], y_x[:, :, D1:D], wh1[:, :, 0:D1], ALU.add)\
                    .then_inc(S["y_wh_added"], 1)

            def y_add_bo(b):
                pool.wait_ge(*after("y_norm", b, 2 * NI))
                pool.tensor_tensor(y_x[:, :, :], y_x[:, :, :], rows["bo"][:, None, :].broadcast_to([P, NI, D]),
                                   ALU.add).then_inc(S["y_bo"], 1)

            turns(pool, {"x_rstd": rstd("x", XT, 2), "x_next_rstd": rstd("x0", XT0, 1), "x_residual": x_residual, "x_mask": x_mask, "x_add_b2": x_add_b2, "x_gain": x_gain,
                         "y_rstd": rstd("y", YT, 3), "y_l1_mask": y_l1_mask, "y_l1_add_wh": y_l1_add_wh,
                         "y_add_bo": y_add_bo}, "pool")

        @block.scalar
        def _(act):
            act.wait_ge(s_init, 1)

            def x_next_norm(b, n):
                act.wait_ge(*after("x0_shift", b, 1))
                act.wait_ge(*after("x0_rstd", b, 1))
                if not isinstance(b, int) or b > 0:
                    act.wait_ge(*filled("x", b - 1, "pv", NH, NI - 1))
                for i in range(NI):
                    act.activation(x_n[:, i, :], x_in[:, i, :], ACT.Relu, bias=XT0["shift"][:, i:i + 1],
                                   scale=XT0["rstd"][:, i:i + 1]).then_inc(S["x0_norm"], 1)

            def x_norm(b, n):
                act.wait_ge(*after("x_shift", b, 1))
                act.wait_ge(*after("x_rstd", b, 1))
                for i in range(NI):
                    act.activation(x_h[:, i, :], x_h[:, i, :], ACT.Identity, bias=XT["shift"][:, i:i + 1],
                                   scale=XT["rstd"][:, i:i + 1]).then_inc(S["x_norm"], 1)

            def y_norm(b, n):
                act.wait_ge(*after("y_shift", b, n + 1))
                act.wait_ge(*after("y_rstd", b, n + 1))
                for i in range(NI):
                    act.activation(y_h[:, i, :], y_x[:, i, :], ACT.Relu,
                                   bias=YT["shift"][:, i:i + 1], scale=YT["rstd"][:, i:i + 1])\
                        .then_inc(S["y_norm"], 1)

            def x_hi(b, c):
                act.wait_ge(*filled("x", b, "turn", c))
                act.activation(x_fr[:, c, :], bank_of("x", "turn", c)[:, :], ACT.Copy).then_inc(S["x_hi"], 1)

            def x_wh(b, h, i):
                act.wait_ge(*filled("x", b, "proj", h, i))
                act.activation(whx[:, i, h, 0:W0], bank_of("x", "proj", h, i)[:, 0:W0], ACT.Copy)\
                    .then_inc(S["x_wh"], 1)

            def x_brow(b, h):
                bank = bank_of("x", "brow", h)
                act.wait_ge(*filled("x", b, "brow", h))
                act.wait_ge(*after("x_score", b, h * NI))
                act.activation(brow[:, :], bank[:, :], ACT.Copy).then_inc(S["x_brow"], 1)

            def x_prob(b, h, j):
                n = h * NI + j
                act.wait_ge(*after("x_mask", b, n + 1))
                act.activation(xp[:, n % XRING, :], xp[:, n % XRING, :], ACT.Exp, bias=XT["d"][:, j, h:h + 1])\
                    .then_inc(S["x_prob"], 1)

            def x_elu_exp(b, h, i):
                n = h * NI + i
                bank = bank_of("x", "pv", h, i)
                act.wait_ge(*filled("x", b, "pv", h, i))
                act.wait_ge(*after("x_recip", b, n + 1))
                act.wait_ge(*after("x_elu", b, max(n - 1, 0)))
                act.activation(elu_e[:, n % 2, :], bank[:, 0:D], ACT.Exp, scale=x_r[:, i:i + 1])\
                    .then_inc(S["x_elu_exp"], 1)

            def x_h_hi(b, h, c):
                act.wait_ge(*filled("x", b, "h_turn", h, c))
                act.activation(x_fr[:, (h % 2) * 2 + c, :], bank_of("x", "h_turn", h, c)[:, :], ACT.Copy)\
                    .then_inc(S["x_h_hi"], 1)

            def x_wh2(b, p, i):
                act.wait_ge(*filled("x", b, "proj2", p, i))
                act.activation(whx[:, i, 0, 0:W0], bank_of("x", "proj2", p, i)[:, 0:W0], ACT.Copy)\
                    .then_inc(S["x_wh2a"], 1)

            def x_o_hi(b, c):
                act.wait_ge(*filled("x", b, "o_turn", c))
                act.activation(x_fr[:, c, :], bank_of("x", "o_turn", c)[:, :], ACT.Copy)\
                    .then_inc(S["x_o_hi"], 1)

            def x_hidden(b, m):
                bank = bank_of("x", "ffn1", m)
                act.wait_ge(*filled("x", b, "ffn1", m))
                act.activation(whx[:, m, 1:3, 0:D], bank[:, :].rearrange("p (a n) -> p a n", a=2), ACT.Relu,
                               bias=b1_col[:, m:m + 1]).then_inc(S["x_hidden"], 1)

            def y_hi(b, n, c):
                bank = bank_of("y", "turn", n, c)
                act.wait_ge(*filled("y", b, "turn", n, c))
                if n == 0:
                    act.activation(y_t[:, c, :], bank[:, :], ACT.Copy).then_inc(S["y_hi0"], 1)
                else:
                    act.activation(y_fr[:, c, :], bank[:, :], ACT.Copy).then_inc(S["y_hi"], 1)

            def y_l1_wh(b, p):
                bank = bank_of("y", "l1_proj", p)
                act.wait_ge(*filled("y", b, "l1_proj", p))
                act.activation(wh1[:, 2 * p:2 * p + 2, 0:W1C],
                               bank[:, 0:2 * W1C].rearrange("p (a n) -> p a n", a=2), ACT.Copy)\
                    .then_inc(S["y_wh"], 1)

            def y_l1_brow(b):
                bank = bank_of("y", "brow")
                act.wait_ge(*filled("y", b, "brow"))
                act.activation(y_v[:, 0:2, :].rearrange("p a n -> p (a n)"), bank[:, :], ACT.Copy)\
                    .then_inc(S["y_brow"], 1)

            def y_l1_prob(b, j):
                act.wait_ge(*after("y_mask", b, j + 1))
                act.activation(yp[:, j, :], yp[:, j, :], ACT.Exp, bias=YT["d"][:, j, 0:1]).then_inc(S["y_prob"], 1)

            def y_qk_hi(b, g, t):
                bank = bank_of("y", "qk", g, t)
                act.wait_ge(*filled("y", b, "qk", g, t))
                act.activation(qk_part[:, 2 * t, :], bank[:, :], ACT.Identity,
                               bias=(bq_col, bk_col)[t][:, g:g + 1]).then_inc(S["y_qk_hi"], 1)

            def y_stack_q(b, h):
                bank = bank_of("y", "stack", h, 0)
                act.wait_ge(*filled("y", b, "stack", h, 0))
                act.activation(qs[0:3 * DH, h % QRING, :], bank[0:3 * DH, :], ACT.Copy).then_inc(S["y_stack_q"], 1)

            def y_max_hi(b, h):
                bank = bank_of("y", "max_turn", h)
                act.wait_ge(*filled("y", b, "max_turn", h))
                if h >= 2:
                    act.wait_ge(*after("y_max_row", b, 32 * (h - 1)))
                act.activation(negm[:, h % 2, 0, :], bank[0:NI, 0:P], ACT.Copy, scale=-1.0)\
                    .then_inc(S["y_max_hi"], 1)

            def y_far_prob(b, h, k):
                n = h * NI + k
                bank = bank_of("y", "far", h, k)
                act.wait_ge(*filled("y", b, "far", h, k))
                act.activation(yp[:, n % YRING, :], bank[:, :], ACT.Exp, scale=SCALE).then_inc(S["y_far_prob"], 1)

            def y_far_sums(b, g):
                act.wait_ge(*filled("y", b, "far_sum", g))
                act.activation(y_h[:, 0:2, :].rearrange("p a n -> p (a n)"), bank_of("y", "far_sum", g)[:, :],
                               ACT.Copy).then_inc(S["y_far_sums"], 1)

            def y_far_ctx(b, g):
                act.wait_ge(*filled("y", b, "far_ctx", g))
                act.activation(y_t[:, g, :], bank_of("y", "far_ctx", g)[:, :], ACT.Copy).then_inc(S["y_ctx0"], 1)

            def y_mj_hi(b, p):
                act.wait_ge(*after("y_mj_sum", b, p + 1))
                act.activation(qk_part[:, p, :], y_h[:, 2 * p:2 * p + 2, :].rearrange("p a n -> p (a n)"), ACT.Copy)\
                    .then_inc(S["y_mj_hi"], 1)

            turns(act, {"x_norm": x_norm, "x_next_norm": x_next_norm, "x_next_hi": x_hi, "x_next_wh": x_wh, "x_brow": x_brow, "x_prob": x_prob,
                        "x_elu_exp": x_elu_exp, "x_h_hi": x_h_hi, "x_wh2": x_wh2, "x_o_hi": x_o_hi,
                        "x_hidden": x_hidden, "y_norm": y_norm, "y_hi": y_hi, "y_l1_wh": y_l1_wh,
                        "y_l1_brow": y_l1_brow, "y_l1_prob": y_l1_prob, "y_qk_hi": y_qk_hi,
                        "y_stack_q": y_stack_q,
                        "y_max_hi": y_max_hi, "y_far_prob": y_far_prob, "y_far_sums": y_far_sums,
                        "y_far_ctx": y_far_ctx, "y_mj_hi": y_mj_hi}, "act")

        @block.tensor
        def _(pe):
            pe.wait_ge(s_id, 6)
            pe.wait_ge(s_init, 1)

            def turned(chain, src, bank, c, key, rows_=P):
                for i in range(NI):
                    last = pe.transpose(bank[:, i * P:(i + 1) * P], src[:, i, c * P:(c + 1) * P], ident[:, :])
                last.then_inc(full(chain, *key), 1)

            def broadcast(chain, columns, bank, key):
                for i in range(NI):
                    last = pe.transpose(bank[:, i * P:(i + 1) * P], columns(i).broadcast_to([P, P]), ident[:, :])
                last.then_inc(full(chain, *key), 1)

            def x_turn(b, c):
                bank = bank_of("x", "turn", c)
                pe.wait_ge(*emptied("x", b, "turn", c))
                pe.wait_ge(*after("x0_norm", b, NI))
                turned("x", x_n, bank, c, ("turn", c))

            def x_proj(b, h, i):
                bank = bank_of("x", "proj", h, i)
                pe.wait_ge(*emptied("x", b, "proj", h, i))
                pe.wait_ge(*after("x_lo", b, DC))
                n = slice(i * P, (i + 1) * P)
                split3(pe, bank[:, 0:W0], lambda c: x_fr[:, c, n], lambda c: x_fr[:, 2 + c, n],
                       lambda c: wh_hi[:, c, h, :], lambda c: wh_lo[:, c, h, :], [(c, c) for c in range(DC)])\
                    .then_inc(full("x", "proj", h, i), 1)

            def x_f2row(b, h):
                bank = bank_of("x", "f2row", h)
                pe.wait_ge(*emptied("x", b, "f2row", h))
                if h < NH:
                    pe.wait_ge(*after("x_wh", b, (h + 1) * NI))
                else:
                    pe.wait_ge(*after("x_wh2b", b, NI))
                broadcast("x", lambda i: whx[:, i, h % NH, D + 1:D + 2], bank, ("f2row", h))

            def x_rows(b, h):
                bank = bank_of("x", "arow", h)
                pe.wait_ge(*emptied("x", b, "arow", h))
                pe.wait_ge(*after("x_small", b, 6 if h < NH else 12))
                broadcast("x", lambda i: XT["a"][:, i, h:h + 1], bank, ("arow", h))
                bank = bank_of("x", "brow", h)
                pe.wait_ge(*emptied("x", b, "brow", h))
                broadcast("x", lambda i: XT["b"][:, i, h:h + 1], bank, ("brow", h))

            def x_pv(b, h, i):
                bank = bank_of("x", "pv", h, i)
                pe.wait_ge(*emptied("x", b, "pv", h, i))
                pe.wait_ge(*after("x_prob", b, (h + 1) * NI))
                for j in range(NI):
                    t = xp[:, (h * NI + j) % XRING, i * P:(i + 1) * P]
                    last = pe.matmul(bank[:, 0:D + 3], t, whx[:, j, h % NH, 0:D + 3], start=(j == 0), stop=(j == NI - 1))
                last.then_inc(full("x", "pv", h, i), 1)

            def x_h_turn(b, h, c):
                bank = bank_of("x", "h_turn", h, c)
                pe.wait_ge(*emptied("x", b, "h_turn", h, c))
                pe.wait_ge(*after("x_elu", b, (h + 1) * NI))
                turned("x", x_h, bank, c, ("h_turn", h, c))

            def x_proj2(b, p, i):
                bank = bank_of("x", "proj2", p, i)
                pe.wait_ge(*emptied("x", b, "proj2", p, i))
                pe.wait_ge(*after("x_h_lo", b, 4 * (p + 1)))
                n = slice(i * P, (i + 1) * P)
                split3(pe, bank[:, 0:W0], lambda k: x_fr[:, k, n], lambda k: x_fr[:, 4 + k, n],
                       lambda k: wo2_hi[:, 4 * p + k, :], lambda k: wo2_lo[:, 4 * p + k, :],
                       [(k, k) for k in range(4)]).then_inc(full("x", "proj2", p, i), 1)

            def x_o_turn(b, c):
                bank = bank_of("x", "o_turn", c)
                pe.wait_ge(*emptied("x", b, "o_turn", c))
                pe.wait_ge(*after("x_elu", b, (NH + 1) * NI))
                turned("x", x_h, bank, c, ("o_turn", c))

            def x_ffn1(b, m):
                bank = bank_of("x", "ffn1", m)
                pe.wait_ge(*emptied("x", b, "ffn1", m))
                pe.wait_ge(*after("x_o_lo", b, DC))
                n = slice(m * P, (m + 1) * P)
                split3(pe, bank[:, :], lambda c: w1_hi[:, c, n], lambda c: w1_lo[:, c, n],
                       lambda c: x_fr[:, c, :], lambda c: x_fr[:, 2 + c, :], [(c, c) for c in range(DC)])\
                    .then_inc(full("x", "ffn1", m), 1)

            def x_ffn2(b, p):
                bank = bank_of("x", "ffn2", p)
                pe.wait_ge(*emptied("x", b, "ffn2", p))
                pe.wait_ge(*after("x_hidden", b, 2))
                for i in (0, 1):
                    for m in range(DC):
                        last = pe.matmul(bank[:, i * D:(i + 1) * D], whx[:, m, 1 + p, i * P:(i + 1) * P],
                                         w2_sb[:, m, :], start=(m == 0), stop=(m == DC - 1))
                last.then_inc(full("x", "ffn2", p), 1)

            def y_turn(b, n, c):
                bank = bank_of("y", "turn", n, c)
                pe.wait_ge(*emptied("y", b, "turn", n, c))
                pe.wait_ge(*after("y_norm", b, (n + 1) * NI))
                turned("y", y_h, bank, c, ("turn", n, c))

            def y_l1_proj(b, p):
                bank = bank_of("y", "l1_proj", p)
                pe.wait_ge(*emptied("y", b, "l1_proj", p))
                pe.wait_ge(*after("y_hi0", b, DC))
                for i in (0, 1):
                    for c in range(DC):
                        last = pe.matmul(bank[:, i * W1C:(i + 1) * W1C], y_t[:, c, (2 * p + i) * P:(2 * p + i + 1) * P],
                                         wl1[:, c, :], start=(c == 0), stop=(c == DC - 1))
                last.then_inc(full("y", "l1_proj", p), 1)

            def y_l1_f2row(b):
                bank = bank_of("y", "f2row")
                pe.wait_ge(*emptied("y", b, "f2row"))
                pe.wait_ge(*after("y_wh", b, 2))
                broadcast("y", lambda i: wh1[:, i, D1 + 1:D1 + 2], bank, ("f2row",))

            def y_l1_rows(b):
                bank = bank_of("y", "arow")
                pe.wait_ge(*emptied("y", b, "arow"))
                pe.wait_ge(*after("y_small", b, 6))
                broadcast("y", lambda i: YT["a"][:, i, 0:1], bank, ("arow",))
                bank = bank_of("y", "brow")
                pe.wait_ge(*emptied("y", b, "brow"))
                broadcast("y", lambda i: YT["b"][:, i, 0:1], bank, ("brow",))

            def y_l1_pv(b, p):
                bank = bank_of("y", "l1_pv", p)
                pe.wait_ge(*emptied("y", b, "l1_pv", p))
                pe.wait_ge(*after("y_prob", b, NI))
                for i in (0, 1):
                    for j in range(NI):
                        last = pe.matmul(bank[:, i * 256:i * 256 + D1 + 3], yp[:, j, (2 * p + i) * P:(2 * p + i + 1) * P],
                                         wh1[:, j, 0:D1 + 3], start=(j == 0), stop=(j == NI - 1))
                last.then_inc(full("y", "l1_pv", p), 1)

            def y_qk(b, g, t):
                bank = bank_of("y", "qk", g, t)
                pe.wait_ge(*emptied("y", b, "qk", g, t))
                pe.wait_ge(*after("y_lo", b, DC))
                w_hi, w_lo = sq[("wq", "wk")[t]]
                n = slice(g * P, (g + 1) * P)
                split3(pe, bank[:, :], lambda c: w_hi[:, c, n], lambda c: w_lo[:, c, n],
                       lambda c: y_fr[:, c, :], lambda c: y_fr[:, 2 + c, :], [(c, c) for c in range(DC)])\
                    .then_inc(full("y", "qk", g, t), 1)

            def nodes_by(b, key, p, name):
                bank = bank_of("y", *key)
                pe.wait_ge(*emptied("y", b, *key))
                w_hi, w_lo = sq[name]
                for i in (0, 1):
                    n = slice((2 * p + i) * P, (2 * p + i + 1) * P)
                    last = split3(pe, bank[:, i * D:(i + 1) * D], lambda c: y_fr[:, c, n], lambda c: y_fr[:, 2 + c, n],
                                  lambda c: w_hi[:, c, :], lambda c: w_lo[:, c, :], [(c, c) for c in range(DC)])
                last.then_inc(full("y", *key), 1)

            def y_v_(b, p):
                nodes_by(b, ("v", p), p, "wv")

            def y_stack(b, h, t):
                bank = bank_of("y", "stack", h, t)
                g = h // G
                pe.wait_ge(*emptied("y", b, "stack", h, t))
                pe.wait_ge(*after("y_qk_lo", b, 2 * g + t + 1))
                for part, first in ((0, (2, 3)[t]), (1, (0, 4)[t])):
                    last = pe.matmul(bank[0:3 * DH, :],
                                     pick[:, h % G, first:first + 3, :].rearrange("p a n -> p (a n)"),
                                     qk_part[:, 2 * t + part, :], start=(part == 0), stop=(part == 1))
                last.then_inc(full("y", "stack", h, t), 1)

            def y_near(b, h, i):
                bank, slot = bank_of("y", "near", h, i), h % QRING
                pe.wait_ge(*emptied("y", b, "near", h, i))
                if i == 0:
                    pe.wait_ge(*after("y_stack_q", b, h + 1))
                    pe.wait_ge(*after("y_stack_k", b, h + 1))
                pe.matmul(bank[:, :], qs[0:3 * DH, slot, i * P:(i + 1) * P], ks[0:3 * DH, slot, :], start=True, stop=True)\
                    .then_inc(full("y", "near", h, i), 1)

            def y_max_turn(b, h):
                bank = bank_of("y", "max_turn", h)
                pe.wait_ge(*emptied("y", b, "max_turn", h))
                pe.wait_ge(*after("y_near_max", b, (h + 1) * NI))
                pe.transpose(bank[0:NI, 0:P], max2[:, h % 2, :], ident[:, :]).then_inc(full("y", "max_turn", h), 1)

            def y_far(b, h, k):
                bank, slot = bank_of("y", "far", h, k), h % QRING
                pe.wait_ge(*emptied("y", b, "far", h, k))
                if k == 0:
                    pe.wait_ge(*after("y_max_row", b, 32 * (h + 1)))
                pe.matmul(bank[:, :], ks[0:3 * DH + 2, slot, k * P:(k + 1) * P], qs[0:3 * DH + 2, slot, :],
                          start=True, stop=False)
                pe.matmul(bank[:, :], ident_b[:, :], mask_t[:, k, :], start=False, stop=True)\
                    .then_inc(full("y", "far", h, k), 1)

            def y_far_pv(b, h, k):
                if k == 0 and h % G == 0:
                    pe.wait_ge(*emptied("y", b, "far_sum", h // G))
                    pe.wait_ge(*emptied("y", b, "far_ctx", h // G))
                    if h == 0:
                        pe.wait_ge(*after("y_v", b, 2))
                n = h * NI + k
                pe.wait_ge(*after("y_far_prob", b, n + 1))
                q = slice(DH * (h % G), DH * (h % G + 1))
                probs = yp[:, n % YRING, :]
                a = pe.matmul(YB[2][q, :], ones[:, :], probs, start=(k == 0), stop=(k == NI - 1))
                c = pe.matmul(YB[3][q, :], y_v[:, k, h * DH:(h + 1) * DH], probs, start=(k == 0), stop=(k == NI - 1))
                if k == NI - 1 and h % G == G - 1:
                    a.then_inc(full("y", "far_sum", h // G), 1)
                    c.then_inc(full("y", "far_ctx", h // G), 1)

            def y_sum_turn(b, g):
                bank = bank_of("y", "sum_turn", g)
                pe.wait_ge(*emptied("y", b, "sum_turn", g))
                pe.wait_ge(*after("y_far_sums", b, g + 1))
                sums = y_h[:, 0:2, :].rearrange("p a n -> p (a n)")
                for i in range(NI):
                    last = pe.transpose(bank[:, i * P:(i + 1) * P], sums[:, i * P:(i + 1) * P], ident[:, :])
                last.then_inc(full("y", "sum_turn", g), 1)

            def y_recip_rows(b, g):
                bank = bank_of("y", "recip_rows", g)
                pe.wait_ge(*emptied("y", b, "recip_rows", g))
                pe.wait_ge(*after("y_recip_wide", b, g + 1))
                wide = y_h[:, 2:4, :].rearrange("p a n -> p (a n)")
                for i in range(NI):
                    last = pe.transpose(bank[:, i * P:(i + 1) * P], wide[:, i * P:(i + 1) * P], ident[:, :])
                last.then_inc(full("y", "recip_rows", g), 1)

            def y_o_proj(b, p):
                bank = bank_of("y", "o_proj", p)
                pe.wait_ge(*emptied("y", b, "o_proj", p))
                pe.wait_ge(*after("y_ctx", b, NG))
                for i in (0, 1):
                    for c in range(DC):
                        last = pe.matmul(bank[:, i * D:(i + 1) * D], y_t[:, c, (2 * p + i) * P:(2 * p + i + 1) * P],
                                         wo_sb[:, c, :], start=(c == 0), stop=(c == DC - 1))
                last.then_inc(full("y", "o_proj", p), 1)

            def y_mj(b, p):
                pe.wait_ge(*after("y_lo", b, 2 * DC))
                nodes_by(b, ("mj", p), p, "wj")

            def y_mi(b, p):
                nodes_by(b, ("mi", p), p, "wi")

            def y_gather(b, p):
                bank = bank_of("y", "gather", p)
                pe.wait_ge(*emptied("y", b, "gather", p))
                pe.wait_ge(*after("y_mj_lo", b, 2))
                for i in (0, 1):
                    n = slice((2 * p + i) * P, (2 * p + i + 1) * P)
                    for j in range(NI):
                        for part in (0, 2):
                            mj = qk_part[:, part + j // 2, (j % 2) * D:(j % 2 + 1) * D]
                            last = pe.matmul(bank[:, i * D:(i + 1) * D], adjt[:, j, n], mj,
                                             start=(j == 0 and part == 0), stop=(j == NI - 1 and part == 2))
                last.then_inc(full("y", "gather", p), 1)

            turns(pe, {"x_next_turn": x_turn, "x_next_proj": x_proj, "x_f2row": x_f2row, "x_rows": x_rows, "x_pv": x_pv,
                       "x_h_turn": x_h_turn, "x_proj2": x_proj2, "x_o_turn": x_o_turn, "x_ffn1": x_ffn1,
                       "x_ffn2": x_ffn2, "y_turn": y_turn, "y_l1_proj": y_l1_proj, "y_l1_f2row": y_l1_f2row,
                       "y_l1_rows": y_l1_rows, "y_l1_pv": y_l1_pv, "y_qk": y_qk, "y_v": y_v_, "y_stack": y_stack, "y_near": y_near,
                       "y_max_turn": y_max_turn, "y_far": y_far, "y_far_pv": y_far_pv,
                       "y_sum_turn": y_sum_turn, "y_recip_rows": y_recip_rows, "y_o_proj": y_o_proj,
                       "y_mj": y_mj, "y_mi": y_mi, "y_gather": y_gather}, "pe")

        @block.vector
        def _(dve):
            done = [0]

            def step(ins):
                done[0] += 1
                ins.then_inc(s_split, 1)

            def settle():
                dve.wait_ge(s_split, done[0])

            dve.wait_ge(s_id, 6)
            dve.wait_ge(s_load, 16 * N_LOADS)
            a1 = a_st[:, 0:1024].rearrange("p (h o) -> p h o", h=NH)
            a2 = a_st2[:, 0:1024].rearrange("p (h o) -> p h o", h=NH)
            scratch = qk_part[:, 0, 0:D].bitcast(F32)
            scratch = elu_e[:, 1, :]
            for c in range(DC):
                for h in range(NH):
                    for s, a in ((0, a1), (1, a2)):
                        step(dve.tensor_tensor_reduce(scratch, w_st[:, c, h, 0:D], a[:, h, :], 1.0, 0.0,
                                                      ALU.mult, ALU.add, w_st[:, c, h, D + s:D + s + 1]))
                        settle()
            for k in range(NH * DC):
                st = (ysx if k < 4 else ysv)[:, (k % 4) * D:(k % 4 + 1) * D]
                step(dve.tensor_copy(wo2_hi[:, k, 0:D], st))
                settle()
                step(dve.tensor_tensor(wo2_lo[:, k, 0:D], st, wo2_hi[:, k, 0:D].bitcast(F32), ALU.subtract))
                for s in (0, 1):
                    step(dve.tensor_tensor_reduce(scratch, st, brow[:, s * D:(s + 1) * D], 1.0, 0.0, ALU.mult,
                                                  ALU.add, XT["max"][:, s, 0:1]))
                    settle()
                    step(dve.tensor_copy(wo2_hi[:, k, D + s:D + s + 1], XT["max"][:, s, 0:1]))
                    settle()
                    step(dve.tensor_tensor(wo2_lo[:, k, D + s:D + s + 1], XT["max"][:, s, 0:1],
                                           wo2_hi[:, k, D + s:D + s + 1].bitcast(F32), ALU.subtract))
                    settle()
            for c in range(DC):
                for s in (0, 1):
                    step(dve.tensor_tensor_reduce(scratch[:, 0:D1], wl1[:, c, 0:D1], elu_e[:, 0, s * D1:(s + 1) * D1],
                                                  1.0, 0.0, ALU.mult, ALU.add, wl1[:, c, D1 + s:D1 + s + 1]))
                    settle()
            for hi, lo, st in [(wh_hi, wh_lo, w_st), (w1_hi, w1_lo, w1_st)] + [sq[n] + (sq_st[n],) for n in sq]:
                full_ = (slice(None),) * len(st.shape)
                step(dve.tensor_copy(hi[full_], st))
                settle()
                step(dve.tensor_tensor(lo[full_], st, hi[full_].bitcast(F32), ALU.subtract))
            step(dve.tensor_scalar(mask_n[:, :, :], adj_i, 0.0, MASKED, ALU.is_le, ALU.mult))
            for k in (0, 1):
                step(dve.tensor_scalar(mask_t[:, 2 * k:2 * k + 2, :], adj_t_i[k], 0.0, MASKED, ALU.is_le, ALU.mult))
                step(dve.tensor_copy(adjt[:, 2 * k:2 * k + 2, :], adj_t_i[k]))
            settle()
            for i in range(NI):
                step(dve.tensor_copy(elu_e[:, :, :].rearrange("p a b -> p (a b)"), adj_i[:, i, :]))
                settle()
                step(dve.reduce_sum(deg[:, i:i + 1], elu_e[:, :, :].rearrange("p a b -> p (a b)"), AX_X))
                settle()
            step(dve.memset(ks[3 * DH:P, :, :].bitcast(F32), 1.0))
            step(dve.memset(pick[:, :, :, :].bitcast(F32), 0.0))
            settle()
            for k in (2, 3, 5):
                step(dve.tensor_copy(pick[:, :, k, :], ident[:, :].rearrange("p (h d) -> p h d", h=G)))
            step(dve.memset(whx[:, :, :, D + 2:D + 4], 1.0))
            step(dve.memset(wh1[:, :, D1 + 2:D1 + 4], 1.0))
            settle()
            dve.memset(y_junk[:, :, 0:2], 0.0).then_inc(s_init, 1)
            dve.wait_ge(s_init, 1)

            def apart():
                dve.sem_inc(s_apart, 1)

            def stats(chain, T, source):
                def go(b, n):
                    source(b, n)
                    src = {"x0": x_in, "x": x_h, "y": y_x}[chain]
                    for i in range(NI):
                        dve.bn_stats(T["stats"][:, i, :], src[:, i, :]).then_inc(S[f"{chain}_stats"], 1)
                    n = n if chain == "y" else 0
                    for i in range(NI):
                        dve.wait_ge(*after(f"{chain}_stats", b, n * NI + i + 1))
                        apart()
                        dve.bn_aggr(T["mv"][:, i, :], T["stats"][:, i, :]).then_inc(S[f"{chain}_aggr"], 1)
                    dve.wait_ge(*after(f"{chain}_aggr", b, (n + 1) * NI))
                    dve.tensor_scalar(T["var"][:, :], T["mv"][:, :, 1], LN_EPS, None, ALU.add)\
                        .then_inc(S[f"{chain}_var"], 1)
                return go

            def shift(chain, T):
                def go(b, n):
                    dve.wait_ge(*after(f"{chain}_rstd", b, (n if chain == "y" else 0) + 1))
                    dve.scalar_tensor_tensor(out=T["shift"][:, :], in0=T["mv"][:, :, 0], scalar=-1.0,
                                             in1=T["rstd"][:, :], op0=ALU.mult, op1=ALU.mult)\
                        .then_inc(S[f"{chain}_shift"], 1)
                return go

            def x_source(b, n):
                dve.wait_ge(*after("x_ffn", b, 2))

            def x_next_source(b, n):
                dve.wait_ge(*after("x_in_loaded", b, 16))

            def y_source(b, n):
                if n == 0:
                    dve.wait_ge(*after("x_out", b, 1))
                elif n == 1:
                    dve.wait_ge(*after("y_l1", b, NI))
                    dve.wait_ge(*after("y_wh_added", b, 1))
                else:
                    dve.wait_ge(*after("y_o", b, 2))

            def x_lo(b, c):
                bank = bank_of("x", "turn", c)
                dve.wait_ge(*filled("x", b, "turn", c))
                dve.wait_ge(*after("x_hi", b, c + 1))
                dve.tensor_tensor(x_fr[:, 2 + c, :], bank[:, :], x_fr[:, c, :].bitcast(F32), ALU.subtract)\
                    .then_inc(S["x_lo"], 1)

            def x_rowmax(b, h):
                bank = bank_of("x", "f2row", h)
                dve.wait_ge(*filled("x", b, "f2row", h))
                if h == NH:
                    dve.wait_ge(*after("x_elu", b, NH * NI))
                apart()
                for i in range(NI):
                    n = h * NI + i
                    if n >= 2:
                        dve.wait_ge(*after("x_rowmax", b, n - 1))
                        apart()
                    dve.tensor_tensor_reduce(x_junk[:, n % 2, :], mask_n[:, i, :], bank[:, :], 1.0, LOWEST, ALU.add, ALU.max,
                                             XT["max"][:, i, h:h + 1]).then_inc(S["x_rowmax"], 1)

            def offsets(chain, T, b, n, f1, f2, hs):
                name, slope = f"{chain}_small", SLOPE[chain]
                v = {k: T[k][:, :, hs] for k in ("max", "sum", "m", "a", "b", "c", "d")}
                dve.tensor_scalar(v["c"], f2, 1.0 - slope, None, ALU.mult).then_inc(S[name], 1)
                dve.tensor_scalar(v["d"], f2, slope, None, ALU.mult).then_inc(S[name], 1)
                dve.tensor_tensor(v["sum"], v["max"], f1, ALU.add).then_inc(S[name], 1)
                dve.wait_ge(*after(name, b, n + 3))
                dve.scalar_tensor_tensor(out=v["m"], in0=v["sum"], scalar=slope, in1=v["sum"], op0=ALU.mult,
                                         op1=ALU.max).then_inc(S[name], 1)
                dve.wait_ge(*after(name, b, n + 4))
                dve.tensor_tensor(v["a"], f1, v["m"], ALU.subtract).then_inc(S[name], 1)
                dve.scalar_tensor_tensor(out=v["b"], in0=f1, scalar=slope, in1=v["m"], op0=ALU.mult,
                                         op1=ALU.subtract).then_inc(S[name], 1)

            def x_offsets(b, n):
                hs = slice(0, NH) if n == 0 else slice(NH, NH + 1)
                heads = slice(0, NH) if n == 0 else slice(0, 1)
                dve.wait_ge(*after("x_rowmax", b, NH * NI if n == 0 else (NH + 1) * NI))
                offsets("x", XT, b, 6 * n, whx[:, :, heads, D], whx[:, :, heads, D + 1], hs)

            def x_score(b, h, j):
                n = h * NI + j
                if j == 0:
                    bank = bank_of("x", "arow", h)
                    dve.wait_ge(*filled("x", b, "arow", h))
                    dve.wait_ge(*after("x_brow", b, h + 1))
                    dve.wait_ge(*after("x_small", b, 6 if h < NH else 12))
                if n >= XRING and (j == 0 or (n - XRING) % NI == 0):
                    dve.wait_ge(*filled("x", b, "pv", (n - XRING) // NI, NI - 1))
                bank = XB[XU[("arow", h)][0]]
                dve.scalar_tensor_tensor(out=xp[:, n % XRING, :], in0=bank[:, :], scalar=XT["c"][:, j, h:h + 1],
                                         in1=brow[:, :], op0=ALU.add, op1=ALU.max).then_inc(S["x_score"], 1)

            def x_recip(b, h, i):
                bank = bank_of("x", "pv", h, i)
                dve.wait_ge(*filled("x", b, "pv", h, i))
                dve.reciprocal(x_r[:, i:i + 1], bank[:, D + 2:D + 3]).then_inc(S["x_recip"], 1)

            def x_elu(b, h, i):
                n = h * NI + i
                dve.wait_ge(*after("x_elu_exp", b, n + 1))
                dve.tensor_scalar(elu_e[:, n % 2, :], elu_e[:, n % 2, :], 1.0, 1.0, ALU.min, ALU.subtract)\
                    .then_inc(S["x_elu_shift"], 1)
                dve.wait_ge(*after("x_elu_shift", b, n + 1))
                if i == 0 and 0 < h < NH:
                        dve.wait_ge(*filled("x", b, "h_turn", h - 1, 1))
                bank = XB[XU[("pv", h, i)][0]]
                dve.scalar_tensor_tensor(out=x_h[:, i, :], in0=bank[:, 0:D], scalar=x_r[:, i:i + 1],
                                         in1=elu_e[:, n % 2, :], op0=ALU.mult, op1=ALU.max)\
                    .then_inc(S["x_elu"], 1)

            def x_h_lo(b, h, c):
                bank = bank_of("x", "h_turn", h, c)
                dve.wait_ge(*filled("x", b, "h_turn", h, c))
                dve.wait_ge(*after("x_h_hi", b, 2 * h + c + 1))
                k = (h % 2) * 2 + c
                dve.tensor_tensor(x_fr[:, 4 + k, :], bank[:, :], x_fr[:, k, :].bitcast(F32), ALU.subtract)\
                    .then_inc(S["x_h_lo"], 1)

            def x_wh2(b, p, i):
                bank = bank_of("x", "proj2", p, i)
                dve.wait_ge(*filled("x", b, "proj2", p, i))
                dve.wait_ge(*after("x_wh2a", b, NI))
                dve.tensor_tensor(whx[:, i, 0, 0:W0], bank[:, 0:W0], whx[:, i, 0, 0:W0], ALU.add)\
                    .then_inc(S["x_wh2b"], 1)

            def x_o_lo(b, c):
                bank = bank_of("x", "o_turn", c)
                dve.wait_ge(*filled("x", b, "o_turn", c))
                dve.wait_ge(*after("x_o_hi", b, c + 1))
                dve.tensor_tensor(x_fr[:, 2 + c, :], bank[:, :], x_fr[:, c, :].bitcast(F32), ALU.subtract)\
                    .then_inc(S["x_o_lo"], 1)

            def x_ffn_sum(b, p):
                bank = bank_of("x", "ffn2", p)
                dve.wait_ge(*filled("x", b, "ffn2", p))
                dve.wait_ge(*after("x_b2", b, 1))
                part = x_h[:, 2 * p:2 * p + 2, :]
                ins = dve.tensor_tensor(part, bank[:, :].rearrange("p (a n) -> p a n", a=2), part, ALU.add)
                ins.then_inc(S["x_ffn"], 1)

            def x_out(b):
                dve.wait_ge(*after("x_gain", b, 1))
                dve.wait_ge(*after("x_res", b, 1))
                dve.wait_ge(*after("y_stored", b, 0))
                dve.tensor_tensor(y_x[:, :, :], x_h[:, :, :], x_res[:, :, :], ALU.add).then_inc(S["x_out"], 1)

            def y_lo(b, n, c):
                bank = bank_of("y", "turn", n, c)
                dve.wait_ge(*filled("y", b, "turn", n, c))
                dve.wait_ge(*after("y_hi", b, 2 * (n - 1) + c + 1))
                dve.tensor_tensor(y_fr[:, 2 + c, :], bank[:, :], y_fr[:, c, :].bitcast(F32), ALU.subtract)\
                    .then_inc(S["y_lo"], 1)

            def y_l1_rowmax(b):
                bank = bank_of("y", "f2row")
                dve.wait_ge(*filled("y", b, "f2row"))
                apart()
                for i in range(NI):
                    if i >= 2:
                        dve.wait_ge(*after("y_rowmax", b, i - 1))
                        apart()
                    dve.tensor_tensor_reduce(y_junk[:, i % 2, :], mask_n[:, i, :], bank[:, :], 1.0, LOWEST, ALU.add, ALU.max,
                                             YT["max"][:, i, 0:1]).then_inc(S["y_rowmax"], 1)

            def y_l1_offsets(b):
                dve.wait_ge(*after("y_rowmax", b, NI))
                offsets("y", YT, b, 0, wh1[:, :, D1:D1 + 1], wh1[:, :, D1 + 1:D1 + 2], slice(0, 1))

            def y_l1_score(b, j):
                if j == 0:
                    dve.wait_ge(*filled("y", b, "arow"))
                    dve.wait_ge(*after("y_brow", b, 1))
                    dve.wait_ge(*after("y_small", b, 6))
                bank = YB[YU[("arow",)][0]]
                dve.scalar_tensor_tensor(out=yp[:, j, :], in0=bank[:, :], scalar=YT["c"][:, j, 0:1],
                                         in1=y_v[:, 0:2, :].rearrange("p a n -> p (a n)"), op0=ALU.add, op1=ALU.max)\
                    .then_inc(S["y_score"], 1)

            def y_l1_sum(b, p):
                bank = bank_of("y", "l1_pv", p)
                dve.wait_ge(*filled("y", b, "l1_pv", p))
                for i in (0, 1):
                    k = 2 * p + i
                    dve.reciprocal(y_r[:, k:k + 1], bank[:, i * 256 + D1 + 2:i * 256 + D1 + 3]).then_inc(S["y_recip"], 1)
                for i in (0, 1):
                    k = 2 * p + i
                    dve.wait_ge(*after("y_recip", b, k + 1))
                    dve.scalar_tensor_tensor(out=y_x[:, k, 0:D1], in0=bank[:, i * 256:i * 256 + D1],
                                             scalar=y_r[:, k:k + 1], in1=y_x[:, k, 0:D1], op0=ALU.mult, op1=ALU.add)\
                        .then_inc(S["y_l1"], 1)

            def y_qk_lo(b, g, t):
                bank = bank_of("y", "qk", g, t)
                dve.wait_ge(*filled("y", b, "qk", g, t))
                dve.wait_ge(*after("y_qk_hi", b, 2 * g + t + 1))
                dve.scalar_tensor_tensor(out=qk_part[:, 2 * t + 1, :], in0=bank[:, :],
                                         scalar=(bq_col, bk_col)[t][:, g:g + 1], in1=qk_part[:, 2 * t, :].bitcast(F32),
                                         op0=ALU.add, op1=ALU.subtract).then_inc(S["y_qk_lo"], 1)

            def y_v_sum(b, p):
                bank = bank_of("y", "v", p)
                dve.wait_ge(*filled("y", b, "v", p))
                dve.tensor_tensor(y_v[:, 2 * p:2 * p + 2, :], bank[:, :].rearrange("p (a n) -> p a n", a=2),
                                  rows["bv"][:, None, :].broadcast_to([P, 2, D]), ALU.add).then_inc(S["y_v"], 1)

            def y_stack_k(b, h):
                bank = bank_of("y", "stack", h, 1)
                dve.wait_ge(*filled("y", b, "stack", h, 1))
                dve.tensor_copy(ks[0:3 * DH, h % QRING, :], bank[0:3 * DH, :]).then_inc(S["y_stack_k"], 1)

            def y_near_max(b, h, i):
                bank, n = bank_of("y", "near", h, i), h * NI + i
                dve.wait_ge(*filled("y", b, "near", h, i))
                if n >= 2:
                    dve.wait_ge(*after("y_near_max", b, n - 1))
                apart()
                dve.tensor_tensor_reduce(y_junk[:, n % 2, :], mask_n[:, i, :], bank[:, :], 1.0, LOWEST, ALU.add, ALU.max,
                                         max2[:, h % 2, i:i + 1]).then_inc(S["y_near_max"], 1)

            def y_max_lo(b, h):
                bank = bank_of("y", "max_turn", h)
                dve.wait_ge(*filled("y", b, "max_turn", h))
                dve.wait_ge(*after("y_max_hi", b, h + 1))
                dve.scalar_tensor_tensor(out=negm[:, h % 2, 1, :], in0=bank[0:NI, 0:P], scalar=-1.0,
                                         in1=negm[:, h % 2, 0, :].bitcast(F32), op0=ALU.mult, op1=ALU.subtract)\
                    .then_inc(S["y_max_lo"], 1)

            def y_far_recip(b, g):
                bank = bank_of("y", "sum_turn", g)
                dve.wait_ge(*filled("y", b, "sum_turn", g))
                dve.reciprocal(y_rs[:, :, :], bank[:, :].rearrange("p (i h d) -> p i h d", i=NI, h=G)[:, :, :, 0])\
                    .then_inc(S["y_frecip"], 1)
                dve.wait_ge(*after("y_frecip", b, g + 1))
                dve.tensor_copy(y_h[:, 2:4, :].rearrange("p a (i h d) -> p (a i) h d", i=2, h=G),
                                y_rs[:, :, :, None].broadcast_to([P, NI, G, DH])).then_inc(S["y_recip_wide"], 1)

            def y_far_norm(b, g):
                bank = bank_of("y", "recip_rows", g)
                dve.wait_ge(*filled("y", b, "recip_rows", g))
                dve.wait_ge(*after("y_ctx0", b, g + 1))
                dve.tensor_tensor(y_t[:, g, :], bank[:, :], y_t[:, g, :], ALU.mult).then_inc(S["y_ctx"], 1)

            def y_o_sum(b, p):
                bank = bank_of("y", "o_proj", p)
                dve.wait_ge(*filled("y", b, "o_proj", p))
                dve.wait_ge(*after("y_bo", b, 1))
                part = y_x[:, 2 * p:2 * p + 2, :]
                dve.tensor_tensor(part, bank[:, :].rearrange("p (a n) -> p a n", a=2), part, ALU.add)\
                    .then_inc(S["y_o"], 1)

            def y_mj_sum(b, p):
                bank = bank_of("y", "mj", p)
                dve.wait_ge(*filled("y", b, "mj", p))
                dve.tensor_tensor(y_h[:, 2 * p:2 * p + 2, :], bank[:, :].rearrange("p (a n) -> p a n", a=2),
                                  rows["b3"][:, None, :].broadcast_to([P, 2, D]), ALU.add).then_inc(S["y_mj_sum"], 1)

            def y_mj_lo(b, p):
                dve.wait_ge(*after("y_mj_hi", b, p + 1))
                dve.tensor_tensor(qk_part[:, 2 + p, :], y_h[:, 2 * p:2 * p + 2, :].rearrange("p a n -> p (a n)"),
                                  qk_part[:, p, :].bitcast(F32), ALU.subtract).then_inc(S["y_mj_lo"], 1)

            def y_mi_sum(b, p):
                bank = bank_of("y", "mi", p)
                dve.wait_ge(*filled("y", b, "mi", p))
                for i in (0, 1):
                    k = 2 * p + i
                    dve.scalar_tensor_tensor(out=y_x[:, k, :], in0=bank[:, i * D:(i + 1) * D],
                                             scalar=deg[:, k:k + 1], in1=y_x[:, k, :], op0=ALU.mult, op1=ALU.add)\
                        .then_inc(S["y_mi"], 1)

            def y_gather_sum(b, p):
                bank = bank_of("y", "gather", p)
                dve.wait_ge(*filled("y", b, "gather", p))
                dve.wait_ge(*after("y_mi", b, NI))
                part = y_x[:, 2 * p:2 * p + 2, :]
                dve.tensor_tensor(part, bank[:, :].rearrange("p (a n) -> p a n", a=2), part, ALU.add)\
                    .then_inc(S["y_out"], 1)

            turns(dve, {"x_stats": stats("x", XT, x_source), "x_shift": shift("x", XT),
                        "x_next_stats": stats("x0", XT0, x_next_source), "x_next_shift": shift("x0", XT0),
                        "x_next_lo": x_lo,
                        "x_rowmax": x_rowmax, "x_offsets": x_offsets, "x_score": x_score, "x_recip": x_recip,
                        "x_elu": x_elu, "x_h_lo": x_h_lo, "x_wh2": x_wh2, "x_o_lo": x_o_lo,
                        "x_ffn_sum": x_ffn_sum, "x_out": x_out, "y_stats": stats("y", YT, y_source),
                        "y_shift": shift("y", YT), "y_lo": y_lo, "y_l1_rowmax": y_l1_rowmax,
                        "y_l1_offsets": y_l1_offsets, "y_l1_score": y_l1_score, "y_l1_sum": y_l1_sum,
                        "y_qk_lo": y_qk_lo, "y_v_sum": y_v_sum, "y_stack_k": y_stack_k, "y_near_max": y_near_max, "y_max_lo": y_max_lo,
                        "y_far_recip": y_far_recip, "y_far_norm": y_far_norm, "y_o_sum": y_o_sum,
                        "y_mj_sum": y_mj_sum, "y_mj_lo": y_mj_lo, "y_mi_sum": y_mi_sum,
                        "y_gather_sum": y_gather_sum}, "dve")


def kernel(**inputs):
    import numpy as _np
    import concourse.bacc as _bacc
    from concourse import mybir as _mybir
    from concourse.bass_utils import run_bass_kernel_spmd as _run

    g = {n: _np.asarray(a) for n, a in inputs.items()}
    D = g["x"].shape[-1]
    laid = {
        "x": g["x"], "adj": g["adj"], "adj_t": g["adj"].T,
        "w_heads": g["L0_gnn_W_heads"], "a_heads": g["L0_gnn_a_heads"], "w_out": g["L0_gnn_W_out"],
        "a_out": g["L0_gnn_a_out"], "w1": g["L0_gnn_w1"], "b1": g["L0_gnn_b1"], "w2": g["L0_gnn_w2"],
        "b2": g["L0_gnn_b2"], "gamma": g["L0_gnn_ln_gamma"], "beta": g["L0_gnn_ln_beta"],
        "l1_w": g["L1_gnn_W"], "l1_a": g["L1_gnn_a"],
        "wq_t": g["L2_gnn_Wq"].T, "bq": g["L2_gnn_bq"], "wk_t": g["L2_gnn_Wk"].T, "bk": g["L2_gnn_bk"],
        "wv_t": g["L2_gnn_Wv"].T, "bv": g["L2_gnn_bv"], "wo_t": g["L2_gnn_Wo"].T, "bo": g["L2_gnn_bo"],
        "wi_t": g["L3_gnn_W"][:, :D].T, "wj_t": g["L3_gnn_W"][:, D:].T, "b3": g["L3_gnn_b"],
    }
    nc = _bacc.Bacc("TRN2", target_bir_lowering=False, num_devices=1)
    arrays, args = {}, []
    for name, a in laid.items():
        a = _np.ascontiguousarray(a)
        arrays[f"in_{name}_dram"] = a
        args.append(nc.dram_tensor(f"in_{name}_dram", a.shape, _mybir.dt.from_np(a.dtype), kind="ExternalInput").ap())
    args.append(nc.dram_tensor("out_0_dram", g["x"].shape, _mybir.dt.float32, kind="ExternalOutput").ap())
    gnn_stack_kernel(nc, *args)
    r = _run(nc, [arrays], core_ids=[0])
    return r.results[0]["out_0_dram"]
```

```python
from contextlib import ExitStack

import concourse.bass as bass
from concourse import mybir

F32 = mybir.dt.float32
F32R = mybir.dt.float32r
BF16 = mybir.dt.bfloat16
I32 = mybir.dt.int32
ALU = mybir.AluOpType
ACT = mybir.ActivationFunctionType
AX_X = mybir.AxisListType.X

P = 128
MASKED = -1e30
LOWEST = -3e38
LN_EPS = 1e-5
SLOPE = {"x": 0.01, "y": 0.2}
XRING = 6
YRING = 4
QRING = 4


def x_steps(NI, NH):
    s = [("pool", "residual", ())]
    for h in range(NH - 1):
        s += [("pe", "f2row", (h,)), ("dve", "rowmax", (h,))]
    s += [("pe", "f2row", (NH - 1,)), ("dve", "rowmax", (NH - 1,)),
          ("dve", "offsets", (0,))]

    def tiles(h, first, last):
        out = [("pe", "rows", (h,)), ("act", "brow", (h,))] if first == 0 else []
        for j in range(first, last):
            out += [("dve", "score", (h, j)), ("pool", "mask", (h, j)),
                    ("act", "prob", (h, j))]
        return out

    def aggregate(h):
        out = []
        for i in range(NI):
            out += [("pe", "pv", (h, i)), ("dve", "recip", (h, i)), ("act", "elu_exp", (h, i))]
            if i:
                out += [("dve", "elu", (h, i - 1))]
        return out + [("dve", "elu", (h, NI - 1))]

    def turned(h):
        out = []
        for c in range(2):
            out += [("pe", "h_turn", (h, c)), ("act", "h_hi", (h, c)), ("dve", "h_lo", (h, c))]
        return out

    s += tiles(0, 0, NI)
    early = XRING - NI
    for h in range(NH):
        a = aggregate(h)
        n = tiles(h + 1, 0, early) if h + 1 < NH else []
        k = 0
        for step in a:
            s.append(step)
            if step[0] == "pe":
                take = (len(n) + NI - 1) // NI
                s += n[k:k + take]
                k += take
        s += n[k:]
        s += turned(h)
        if h + 1 < NH:
            s += tiles(h + 1, early, NI)
        if h % 2:
            for i in range(NI):
                s += [("pe", "proj2", (h // 2, i)), ("act" if h < 2 else "dve", "wh2", (h // 2, i))]
    s += [("pe", "f2row", (NH,)), ("dve", "rowmax", (NH,)), ("dve", "offsets", (1,))]
    s += tiles(NH, 0, NI) + aggregate(NH)
    for c in range(2):
        s += [("pe", "o_turn", (c,)), ("act", "o_hi", (c,)), ("dve", "o_lo", (c,))]
    s += [("pool", "add_b2", ())]
    s += x_head(NI, NH)[0]
    for m in range(2):
        s += [("pe", "ffn1", (m,)), ("act", "hidden", (m,))]
    for p in range(2):
        s += [("pe", "ffn2", (p,)), ("dve", "ffn_sum", (p,))]
    own = [("dve", "stats", (1,)), ("pool", "rstd", (1,)), ("dve", "shift", (1,)),
           ("act", "norm", (1,)), ("pool", "gain", ()), ("dve", "out", ())]
    ahead = x_head(NI, NH)[1]
    for n, step in enumerate(ahead):
        if n % 2 == 0 and own:
            s.append(own.pop(0))
        s.append(step)
    return s + own


def x_head(NI, NH):
    first = [("dve", "next_stats", (0,)), ("pool", "next_rstd", (0,)), ("dve", "next_shift", (0,)),
             ("act", "next_norm", (0,))]
    second = []
    for c in range(2):
        second += [("pe", "next_turn", (c,)), ("act", "next_hi", (c,)), ("dve", "next_lo", (c,))]
    for h in range(NH):
        for i in range(NI):
            second += [("pe", "next_proj", (h, i)), ("act", "next_wh", (h, i))]
    return first, second


def y_steps(NI, NG, G):
    def norm(n):
        return [("dve", "stats", (n,)), ("pool", "rstd", (n,)), ("dve", "shift", (n,)),
                ("act", "norm", (n,))]

    s = norm(0)
    for c in range(2):
        s += [("pe", "turn", (0, c)), ("act", "hi", (0, c))]
    for p in range(2):
        s += [("pe", "l1_proj", (p,)), ("act", "l1_wh", (p,))]
    s += [("pe", "l1_f2row", ()), ("dve", "l1_rowmax", ()), ("dve", "l1_offsets", ()),
          ("pe", "l1_rows", ()), ("act", "l1_brow", ())]
    for j in range(NI):
        s += [("dve", "l1_score", (j,)), ("pool", "l1_mask", (j,)), ("act", "l1_prob", (j,))]
    s += [("pool", "l1_add_wh", ())]
    for p in range(2):
        s += [("pe", "l1_pv", (p,)), ("dve", "l1_sum", (p,))]
    s += norm(1) + [("pool", "add_bo", ())]
    for c in range(2):
        s += [("pe", "turn", (1, c)), ("act", "hi", (1, c)), ("dve", "lo", (1, c))]

    def qk(g):
        out = []
        for t in range(2):
            out += [("pe", "qk", (g, t)), ("act", "qk_hi", (g, t)), ("dve", "qk_lo", (g, t))]
        return out

    def qv():
        out = []
        for p in range(2):
            out += [("pe", "v", (p,)), ("dve", "v_sum", (p,))]
        return out

    def stack(h):
        return [("pe", "stack", (h, 0)), ("act", "stack_q", (h,)), ("pe", "stack", (h, 1)),
                ("dve", "stack_k", (h,))]

    def far(p, n):
        h, k = 2 * p + n % 2, n // 2
        out = [("pe", "far", (h, k)), ("act", "far_prob", (h, k))]
        if n % 2 and k:
            out += far_pv(p, k - 1)
        return out

    def far_pv(p, k):
        return [("pe", "far_pv", (h, k)) for h in (2 * p, 2 * p + 1)]

    def near(p, n):
        h, i = 2 * p + n // NI, n % NI
        out = [("pe", "near", (h, i)), ("dve", "near_max", (h, i))]
        if i == NI - 1:
            out += [("pe", "max_turn", (h,)), ("act", "max_hi", (h,)), ("dve", "max_lo", (h,))]
        return out

    PAIRS = NG * G // 2
    s += qk(0) + stack(0) + stack(1) + qv()
    for p in range(PAIRS + 1):
        if p < PAIRS:
            s += near(p, 0) + near(p, 1)
        for n in range(2 * NI):
            if p:
                s += far(p - 1, n)
            if p < PAIRS and n + 2 < 2 * NI:
                s += near(p, n + 2)
        if p:
            s += far_pv(p - 1, NI - 1)
        if p and p % (G // 2) == 0:
            g = p // (G // 2) - 1
            s += [("act", "far_sums", (g,)), ("act", "far_ctx", (g,)), ("pe", "sum_turn", (g,)),
                  ("dve", "far_recip", (g,)), ("pe", "recip_rows", (g,)), ("dve", "far_norm", (g,))]
        if p + 1 < PAIRS:
            s += stack(2 * p + 2) + stack(2 * p + 3)
        if p + 2 < PAIRS and (p + 2) % (G // 2) == 0:
            s += qk((p + 2) // (G // 2))
    for p in range(2):
        s += [("pe", "o_proj", (p,)), ("dve", "o_sum", (p,))]
    s += norm(2)
    for c in range(2):
        s += [("pe", "turn", (2, c)), ("act", "hi", (2, c)), ("dve", "lo", (2, c))]
    for p in range(2):
        s += [("pe", "mj", (p,)), ("dve", "mj_sum", (p,)), ("act", "mj_hi", (p,)), ("dve", "mj_lo", (p,))]
    for p in range(2):
        s += [("pe", "mi", (p,)), ("dve", "mi_sum", (p,))]
    for p in range(2):
        s += [("pe", "gather", (p,)), ("dve", "gather_sum", (p,))]
    return s


PACE = [1, 11, 19, 30, 31, 31, 34, 34, 38, 38, 38, 43, 45, 47, 51, 58, 63, 78, 78, 78, 94, 102, 102,
        113, 118, 126, 126, 140, 153, 162, 168, 178, 180, 182, 182, 190, 200, 202, 212, 218, 221, 225,
        236, 242, 249, 253, 254, 270, 284, 284, 293, 294, 295, 297, 301, 303, 303, 305, 307, 314, 316,
        318, 318, 318, 319, 319, 319, 319, 319, 319, 319, 319, 319]


def merged(xs, ys):
    parts = len(PACE) - 1
    marks = [round(len(xs) * k / parts) for k in range(parts + 1)]
    order, y = [], 0
    for k in range(parts if ys else 0):
        for n in range(marks[k], marks[k + 1]):
            due = int(PACE[k] + (PACE[k + 1] - PACE[k]) * (n - marks[k]) / (marks[k + 1] - marks[k]))
            order += [("y",) + s for s in ys[y:due]] + [("x",) + xs[n]]
            y = max(y, due)
    return order + [("y",) + s for s in ys[y:]] if order else [("x",) + s for s in xs] + [("y",) + s for s in ys]


def gnn_stack_kernel(nc, x, adj, adj_t, w_heads, a_heads, w_out, a_out, w1, b1, w2, b2, gamma, beta,
                     l1_w, l1_a, wq_t, bq, wk_t, bk, wv_t, bv, wo_t, bo, wi_t, wj_t, b3, out):
    B, N, D = x.shape
    NI = N // P
    DC = D // P
    NH = w_heads.shape[0]
    D1 = l1_w.shape[1]
    HEADS2, DH = 8, 32
    G = P // DH
    NG = HEADS2 // G
    SCALE = float(DH) ** -0.5
    W0 = D + 2
    W1C = D1 + 2
    assert N == 512 and D == 256 and NI == 4 and DC == 2

    XS, YS = x_steps(NI, NH), y_steps(NI, NG, G)
    TOGETHER = merged(XS, YS)
    X_ALONE, Y_ALONE = merged(XS, []), merged([], YS)
    X_HEAD = merged(sum(x_head(NI, NH), []), [])
    LAST_TOGETHER = [step for step in TOGETHER if not step[2].startswith("next_")]

    ctx = ExitStack()
    with ctx:
        def sb(name, shape, dt=F32):
            return ctx.enter_context(nc.sbuf_tensor(name, shape, dt))

        def sem(name):
            return ctx.enter_context(nc.semaphore(name))

        wh_hi, wh_lo = sb("wh_hi", [P, DC, NH, W0], F32R), sb("wh_lo", [P, DC, NH, W0], F32R)
        wo2_hi, wo2_lo = sb("wo2_hi", [P, NH * DC, W0], F32R), sb("wo2_lo", [P, NH * DC, W0], F32R)
        w1_hi, w1_lo = sb("w1_hi", [P, DC, D], F32R), sb("w1_lo", [P, DC, D], F32R)
        w2_sb, wl1 = sb("w2_sb", [P, DC, D]), sb("wl1", [P, DC, W1C])
        sq = {n: (sb(f"{n}_hi", [P, DC, D], F32R), sb(f"{n}_lo", [P, DC, D], F32R))
              for n in ("wq", "wk", "wv", "wi", "wj")}
        wo_sb = sb("wo_sb", [P, DC, D])
        mask_n, mask_t = sb("mask_n", [P, NI, N], BF16), sb("mask_t", [P, NI, N], BF16)
        adjt = sb("adjt", [P, NI, N], F32R)
        ident, ident_b, ones = sb("ident", [P, P]), sb("ident_b", [P, P], BF16), sb("ones", [P, DH])
        rows = {n: sb(f"{n}_rows", [P, D]) for n in ("b2", "gamma", "beta", "bv", "bo", "b3")}
        b1_col, bq_col, bk_col = sb("b1_col", [P, DC]), sb("bq_col", [P, DC]), sb("bk_col", [P, DC])
        deg, power = sb("deg", [P, NI]), sb("power", [P, NI])

        def small(chain, heads):
            return {
                "stats": sb(f"{chain}_stats", [P, NI, 6]), "mv": sb(f"{chain}_mv", [P, NI, 2]),
                "var": sb(f"{chain}_var", [P, NI]), "rstd": sb(f"{chain}_rstd", [P, NI]),
                "shift": sb(f"{chain}_shift", [P, NI]), "max": sb(f"{chain}_max", [P, NI, heads]),
                "sum": sb(f"{chain}_f12", [P, NI, heads]), "m": sb(f"{chain}_m", [P, NI, heads]),
                "a": sb(f"{chain}_a", [P, NI, heads]), "b": sb(f"{chain}_b", [P, NI, heads]),
                "c": sb(f"{chain}_c", [P, NI, heads]), "d": sb(f"{chain}_d", [P, NI, heads]),
            }

        XT, YT = small("x", NH + 1), small("y", 1)
        XT0 = {"stats": sb("x0_stats", [P, NI, 6]), "mv": sb("x0_mv", [P, NI, 2]), "var": sb("x0_var", [P, NI]),
               "rstd": sb("x0_rstd", [P, NI]), "shift": sb("x0_shift", [P, NI])}

        x_in = sb("x_in", [P, NI, D])
        x_res = sb("x_res", [P, NI, D])
        x_h = sb("x_h", [P, NI, D])
        x_fr = sb("x_fr", [P, 8, N], F32R)
        whx = sb("whx", [P, NI, NH, D + 4])
        brow = sb("brow", [P, N])
        xp = sb("xp", [P, XRING, N])
        x_n = xp[:, 0:2, :].rearrange("p a (i d) -> p (a i) d", i=2)
        elu_e, x_r = sb("elu_e", [P, 2, D]), sb("x_r", [P, NI])
        y_x, y_h = sb("y_x", [P, NI, D]), sb("y_h", [P, NI, D])
        y_fr = sb("y_fr", [P, 4, N], F32R)
        wh1 = sb("wh1", [P, NI, D1 + 4])
        y_v = sb("y_v", [P, NI, D])
        yp = sb("yp", [P, YRING, N])
        y_t = yp[:, 0:DC, :]
        y_ctx = [y_h[:, 0:2, :].rearrange("p a n -> p (a n)"), yp[:, 0, :]]
        y_sums = y_h[:, 2:4, :]
        x_junk, y_junk = elu_e[:, :, :].bitcast(BF16), sb("y_junk", [P, 2, N], BF16)
        qk_part = sb("qk_part", [P, 4, N], F32R)
        qs, ks = sb("qs", [P, QRING, N], F32R), sb("ks", [P, QRING, N], F32R)
        pick = sb("pick", [P, G, 7, DH], F32R)
        max2, y_r = sb("max2", [P, 2, NI]), sb("y_r", [P, NI])
        negm = sb("negm", [NI, 2, 2, P], F32R)
        y_rs = sb("y_rs", [P, NI, G])

        XB = [ctx.enter_context(nc.psum_tensor(f"x_bank{i}", [P, 512], F32)) for i in range(4)]
        YB = [ctx.enter_context(nc.psum_tensor(f"y_bank{i}", [P, 512], F32)) for i in range(4)]

        s_load, s_split, s_init = sem("weights_loaded"), sem("setup_step"), sem("constants_ready")
        s_columns, s_high = sem("columns_ready"), sem("high_parts_ready")
        s_id, s_apart = sem("identity_ready"), sem("wait_kept_apart")
        names = """x_in_loaded x0_stats x0_aggr x0_var x0_rstd x0_shift x0_norm x_stats x_aggr x_var x_rstd x_shift x_norm x_hi x_lo x_wh x_rowmax
        x_small x_brow x_score x_mask x_prob x_recip x_elu_exp x_elu_shift x_elu x_h_hi x_h_lo x_wh2a
        x_wh2b x_o_hi x_o_lo x_b2 x_hidden x_ffn x_gain x_res x_out
        y_stats y_aggr y_var y_rstd y_shift y_norm y_hi0 y_hi y_lo y_wh y_rowmax y_small y_brow y_score
        y_mask y_prob y_wh_added y_recip y_l1 y_bo y_qk_hi y_qk_lo y_v y_stack_q y_stack_k y_near_max y_max_hi y_max_lo
        y_max_row y_far_prob y_far_sums y_ctx0 y_frecip y_recip_wide y_ctx y_o y_mj_sum y_mj_hi y_mj_lo y_mi y_out y_stored""".split()
        S = {n: sem(n) for n in names}
        xfull = [sem(f"x_bank{i}_full") for i in range(4)]
        yfull = [sem(f"y_bank{i}_full") for i in range(4)]

        PER = {n: 1 for n in names}
        PER.update(x_in_loaded=16, x0_stats=NI, x0_aggr=NI, x0_norm=NI, x_stats=NI, x_aggr=NI, x_norm=NI, x_hi=2, x_lo=2, x_wh=NH * NI, x_rowmax=(NH + 1) * NI, x_small=12,
                   x_brow=NH + 1, x_score=(NH + 1) * NI, x_mask=(NH + 1) * NI, x_prob=(NH + 1) * NI,
                   x_recip=(NH + 1) * NI, x_elu_exp=(NH + 1) * NI, x_elu_shift=(NH + 1) * NI,
                   x_elu=(NH + 1) * NI, x_h_hi=NH * 2, x_h_lo=NH * 2, x_wh2a=NI, x_wh2b=NI, x_o_hi=2,
                   x_o_lo=2, x_hidden=2, x_ffn=2, y_stats=3 * NI, y_aggr=3 * NI, y_var=3, y_rstd=3,
                   y_shift=3, y_norm=3 * NI, y_hi0=2, y_hi=4, y_lo=4, y_wh=2, y_rowmax=NI, y_small=6,
                   y_score=NI, y_mask=NI, y_prob=NI, y_recip=NI, y_l1=NI, y_qk_hi=2 * NG,
                   y_qk_lo=2 * NG, y_v=2, y_stack_q=HEADS2, y_stack_k=HEADS2, y_near_max=HEADS2 * NI,
                   y_max_hi=HEADS2, y_max_lo=HEADS2, y_max_row=32 * HEADS2, y_far_prob=HEADS2 * NI,
                   y_far_sums=NG, y_ctx0=NG, y_frecip=2 * NG, y_recip_wide=NG, y_ctx=NG, y_o=2, y_mj_sum=2, y_mj_hi=2, y_mj_lo=2, y_mi=NI, y_out=2, y_stored=16)

        def after(name, b, n):
            v = b * PER[name] + n
            return (s_init, 1) if isinstance(v, int) and v <= 0 else (S[name], v)

        def uses(order, chain, bank_of):
            found, per = {}, [0] * 4
            for c, engine, step, args in order:
                if c == chain and engine == "pe":
                    for key in bank_of(step, args):
                        bank = key[0] if key[0] is not None else (per[0] + per[1]) % 2
                        found[key[1]] = (bank, per[bank])
                        per[bank] += 1
            return found, per

        def x_bank_of(step, args):
            if step == "rows":
                return [(2, ("arow",) + args), (3, ("brow",) + args)]
            if step == "f2row":
                return [(2 + args[0] % 2, ("f2row",) + args)]
            if step == "pv" and args[1] == 2:
                return [(3, ("pv",) + args)]
            return [(None, (step,) + args)]

        def y_bank_of(step, args):
            if step == "l1_rows":
                return [(2, ("arow",)), (3, ("brow",))]
            if step == "l1_f2row":
                return [(2, ("f2row",))]
            if step == "far_pv":
                h, k = args
                return [(2, ("far_sum", h // G)), (3, ("far_ctx", h // G))] if k == 0 and h % G == 0 else []
            return [(None, (step,) + args)]

        X_ORDER = [(c, e, step.replace("next_", ""), args) for c, e, step, args in
                   X_HEAD + [s for s in X_ALONE if not s[2].startswith("next_")]]
        XU, XN = uses(X_ORDER, "x", x_bank_of)
        YU, YN = uses(Y_ALONE, "y", y_bank_of)

        def far_tile(h, k):
            return (h // 2) * 2 * NI + 2 * k + h % 2

        def x_released(key):
            k, a = key[0], key[1:]
            return {"turn": lambda: ("x_lo", a[0] + 1), "proj": lambda: ("x_wh", a[0] * NI + a[1] + 1),
                    "f2row": lambda: ("x_rowmax", (a[0] + 1) * NI), "arow": lambda: ("x_score", (a[0] + 1) * NI),
                    "brow": lambda: ("x_brow", a[0] + 1), "pv": lambda: ("x_elu", a[0] * NI + a[1] + 1),
                    "h_turn": lambda: ("x_h_lo", a[0] * 2 + a[1] + 1),
                    "proj2": lambda: ("x_wh2b" if a[0] else "x_wh2a", a[1] + 1),
                    "o_turn": lambda: ("x_o_lo", a[0] + 1), "ffn1": lambda: ("x_hidden", a[0] + 1),
                    "ffn2": lambda: ("x_ffn", a[0] + 1)}[k]()

        def y_released(key):
            k, a = key[0], key[1:]
            return {"turn": lambda: ("y_hi0", a[1] + 1) if a[0] == 0 else ("y_lo", (a[0] - 1) * 2 + a[1] + 1),
                    "l1_proj": lambda: ("y_wh", a[0] + 1), "f2row": lambda: ("y_rowmax", NI),
                    "arow": lambda: ("y_score", NI), "brow": lambda: ("y_brow", 1),
                    "l1_pv": lambda: ("y_l1", 2 * a[0] + 2),
                    "qk": lambda: ("y_qk_lo", a[0] * 2 + a[1] + 1), "v": lambda: ("y_v", a[0] + 1),
                    "stack": lambda: ("y_stack_k" if a[1] else "y_stack_q", a[0] + 1),
                    "near": lambda: ("y_near_max", a[0] * NI + a[1] + 1),
                    "max_turn": lambda: ("y_max_lo", a[0] + 1),
                    "far": lambda: ("y_far_prob", far_tile(a[0], a[1]) + 1),
                    "far_sum": lambda: ("y_far_sums", a[0] + 1), "far_ctx": lambda: ("y_ctx0", a[0] + 1),
                    "sum_turn": lambda: ("y_frecip", 2 * a[0] + 2), "recip_rows": lambda: ("y_ctx", a[0] + 1),
                    "o_proj": lambda: ("y_o", a[0] + 1), "mj": lambda: ("y_mj_sum", a[0] + 1),
                    "mi": lambda: ("y_mi", 2 * a[0] + 2), "gather": lambda: ("y_out", a[0] + 1)}[k]()

        def emptied(chain, b, *key):
            U, N_, released = (XU, XN, x_released) if chain == "x" else (YU, YN, y_released)
            bank, n = U[key]
            before = [k for k, v in U.items() if v == (bank, n - 1 if n else N_[bank] - 1)][0]
            name, count = released(before)
            if n:
                return after(name, b, count)
            return after(name, b, 0) if chain == "x" else after("x_out", b, 1)

        def bank_of(chain, *key):
            return (XB if chain == "x" else YB)[(XU if chain == "x" else YU)[key][0]]

        def full(chain, *key):
            bank, _ = (XU if chain == "x" else YU)[key]
            return (xfull if chain == "x" else yfull)[bank]

        def filled(chain, b, *key):
            U, N_, fulls = (XU, XN, xfull) if chain == "x" else (YU, YN, yfull)
            bank, n = U[key]
            return fulls[bank], b * N_[bank] + n + 1

        def split3(pe, outp, hi_l, lo_l, hi_r, lo_r, pairs, start=True, stop=True):
            todo = [(a, b_) for l, r in pairs for a, b_ in
                    ((hi_l(l), hi_r(r)), (hi_l(l), lo_r(r)), (lo_l(l), hi_r(r)))]
            for n, (a, b_) in enumerate(todo):
                last = pe.matmul(outp, a, b_, start=start and n == 0, stop=stop and n == len(todo) - 1)
            return last

        x_v = x.rearrange("b (i p) d -> b p i d", p=P)
        out_v = out.rearrange("b (i p) d -> b p i d", p=P)
        block = ctx.enter_context(nc.Block())

        def turns(engine, steps, name):
            def run(order, xb, yb):
                for chain, e, step, args in order:
                    if e == name:
                        graph = yb if chain == "y" else xb + 1 if step.startswith("next_") else xb
                        steps[chain + "_" + step](graph, *args)

            run(X_HEAD, -1, None)
            run(X_ALONE, 0, None)
            with engine.Fori(1, B - 1) as b:
                run(TOGETHER, b, b - 1)
            run(LAST_TOGETHER, B - 1, B - 2)
            run(Y_ALONE, None, B - 1)

        st_w = whx[:, :, :, :].rearrange("p a b c -> p (a b c)")
        st_x = xp[:, :, :].rearrange("p a b -> p (a b)")
        st_y = yp[:, :, :].rearrange("p a b -> p (a b)")
        st_r = x_res[:, :, :].rearrange("p a b -> p (a b)")
        w_st = st_w[:, 0:DC * NH * W0].rearrange("p (c h o) -> p c h o", c=DC, h=NH)
        sq_st = {n: (st_x if k < 4 else st_r)[:, (k % 4) * 512:(k % 4) * 512 + 512].rearrange("p (c o) -> p c o", c=DC)
                 for k, n in enumerate(sq)}
        w1_st = y_h[:, 0:2, :]
        adj_i = st_y[:, 0:2048].bitcast(I32).rearrange("p (i n) -> p i n", i=NI)
        adj_t_i = [(first, first + n, v.bitcast(I32).rearrange("p (i n) -> p i n", i=n)) for first, n, v in
                   ((0, 2, st_x[:, 2048:3072]), (2, 1, y_h[:, 2:4, :].rearrange("p a b -> p (a b)")),
                    (3, 1, st_r[:, 512:1024]))]
        a_st = x_h[:, :, :].rearrange("p a b -> p (a b)")
        a_st2 = x_in[:, :, :].rearrange("p a b -> p (a b)")
        ysx, ysv = y_x[:, :, :].rearrange("p a b -> p (a b)"), y_v[:, :, :].rearrange("p a b -> p (a b)")

        @block.sync
        def _(sp):
            def load(dst, src, name=s_load):
                sp.dma_start(dst, src).then_inc(name, 16)

            for c in range(DC):
                load(w_st[:, c, :, 0:D], w_heads[:, c * P:(c + 1) * P, :].rearrange("h p o -> p h o"))
            load(a_st[:, 0:1024].rearrange("p (h o) -> p h o", h=NH), a_heads[:, 0:D].partition_broadcast(P))
            load(a_st2[:, 0:1024].rearrange("p (h o) -> p h o", h=NH), a_heads[:, D:2 * D].partition_broadcast(P))
            load(brow[:, :], a_out.partition_broadcast(P))
            load(elu_e[:, 0, :], l1_a.rearrange("s o u -> (s o u)").partition_broadcast(P))
            for c in range(DC):
                load(wl1[:, c, 0:D1], l1_w[c * P:(c + 1) * P, :])
                load(w2_sb[:, c, :], w2[c * P:(c + 1) * P, :])
                load(wo_sb[:, c, :], wo_t[c * P:(c + 1) * P, :])
                load(w1_st[:, c, :], w1[c * P:(c + 1) * P, :])
            for n, src in (("wq", wq_t), ("wk", wk_t), ("wv", wv_t), ("wi", wi_t), ("wj", wj_t)):
                load(sq_st[n], src.rearrange("(c p) o -> p c o", p=P))
            load(adj_i, adj.rearrange("(i p) n -> p i n", p=P))
            for n, src in (("b2", b2), ("gamma", gamma), ("beta", beta), ("bv", bv), ("bo", bo), ("b3", b3)):
                load(rows[n][:, :], src.partition_broadcast(P))
            for t, src in ((b1_col, b1), (bq_col, bq), (bk_col, bk)):
                sp.dma_start(t[:, :], src.rearrange("(c p) -> p c", p=P), allow_slow_non_contiguous=True)\
                    .then_inc(s_load, 16)
            load(ysx, w_out[0:4 * P, :].rearrange("(k p) o -> p k o", p=P))
            load(ysv, w_out[4 * P:8 * P, :].rearrange("(k p) o -> p k o", p=P))
            for first, end, tile in adj_t_i:
                load(tile, adj_t[first * P:end * P, :].rearrange("(i p) n -> p i n", p=P))

            def x_load(b):
                sp.wait_ge(*after("x0_norm", b, 0))
                sp.wait_ge(*after("x_res", b, 0))
                sp.dma_start(x_in[:, :, :], x_v[b]).then_inc(S["x_in_loaded"], 16)

            def y_max_row(b, h):
                for r, name in ((0, "y_max_hi"), (1, "y_max_lo")):
                    sp.wait_ge(*after(name, b, h + 1))
                    sp.dma_start(qs[3 * DH + r:3 * DH + r + 1, h % QRING, :].rearrange("p (i n) -> p i n", i=NI).bitcast(F32),
                                 negm[:, h % 2, r, :].bitcast(F32)).then_inc(S["y_max_row"], 16)

            def y_store(b):
                sp.wait_ge(*after("y_out", b, 2))
                sp.dma_start(out_v[b], y_x[:, :, :]).then_inc(S["y_stored"], 16)

            sp.wait_ge(s_init, 1)
            x_load(0)
            x_load(1)

            def y_all(b):
                for h in range(HEADS2):
                    y_max_row(b, h)

            with sp.Fori(1, B - 1) as b:
                x_load(b + 1)
                y_all(b - 1)
                y_store(b - 1)
            y_all(B - 2)
            y_store(B - 2)
            y_all(B - 1)
            y_store(B - 1)
            sp.wait_ge(S["y_stored"], 16 * B)

        SPLIT = [(wo2_hi[:, 4 * a:4 * a + 4, 0:D], wo2_lo[:, 4 * a:4 * a + 4, 0:D],
                  st.rearrange("p (k o) -> p k o", k=4)) for a, st in ((0, ysx), (1, ysv))]
        SPLIT += [(hi[:, :, :], lo[:, :, :], st) for hi, lo, st in
                  [(w1_hi, w1_lo, w1_st)] + [sq[n] + (sq_st[n],) for n in sq]]
        SPLIT += [(wh_hi[:, :, :, :], wh_lo[:, :, :, :], w_st)]

        N_LOADS = DC + 4 + DC * 4 + 5 + 1 + 6 + 3 + 2 + len(adj_t_i)

        @block.gpsimd
        def _(pool):
            pool.memset(ident[:, :], 0.0).then_inc(s_id, 1)
            pool.memset(ident_b[:, :], 0.0).then_inc(s_id, 1)
            pool.wait_ge(s_id, 2)
            for t in (ident, ident_b):
                pool.affine_select(out=t[:, :], in_=t[:, :], compare_op=ALU.not_equal, fill=1.0, base=0,
                                   pattern=[[-1, P]], channel_multiplier=1).then_inc(s_id, 1)
            pool.memset(ones[:, :], 1.0).then_inc(s_id, 1)
            pool.memset(power[:, :], -0.5).then_inc(s_id, 1)
            pool.wait_ge(s_id, 6)
            pool.wait_ge(s_init, 1)

            def rstd(chain, T, k):
                def step(b, n):
                    pool.wait_ge(*after(f"{chain}_var", b, (n if chain == "y" else 0) + 1))
                    pool.tensor_tensor(T["rstd"][:, :], T["var"][:, :], power[:, :], ALU.pow)\
                        .then_inc(S[f"{chain}_rstd"], 1)
                return step

            def x_mask(b, h, j):
                n = h * NI + j
                pool.wait_ge(*after("x_score", b, n + 1))
                pool.tensor_tensor(xp[:, n % XRING, :], xp[:, n % XRING, :], mask_t[:, j, :], ALU.add)\
                    .then_inc(S["x_mask"], 1)

            def x_add_b2(b):
                pool.wait_ge(*filled("x", b, "o_turn", 1))
                pool.wait_ge(*after("x_elu", b, (NH + 1) * NI))
                pool.tensor_tensor(x_h[:, :, :], x_h[:, :, :], rows["b2"][:, None, :].broadcast_to([P, NI, D]),
                                   ALU.add).then_inc(S["x_b2"], 1)

            def x_residual(b):
                pool.wait_ge(*after("x_in_loaded", b, 16))
                pool.wait_ge(*after("x_out", b, 0))
                pool.tensor_tensor(x_res[:, :, :], x_in[:, :, :], rows["beta"][:, None, :].broadcast_to([P, NI, D]),
                                   ALU.add).then_inc(S["x_res"], 1)

            def x_gain(b):
                pool.wait_ge(*after("x_norm", b, NI))
                pool.tensor_tensor(x_h[:, :, :], x_h[:, :, :], rows["gamma"][:, None, :].broadcast_to([P, NI, D]),
                                   ALU.mult).then_inc(S["x_gain"], 1)

            def y_l1_mask(b, j):
                pool.wait_ge(*after("y_score", b, j + 1))
                pool.tensor_tensor(yp[:, j, :], yp[:, j, :], mask_t[:, j, :], ALU.add).then_inc(S["y_mask"], 1)

            def y_l1_add_wh(b):
                pool.wait_ge(*after("y_norm", b, NI))
                pool.wait_ge(*after("y_wh", b, 2))
                pool.tensor_tensor(y_x[:, :, D1:D], y_x[:, :, D1:D], wh1[:, :, 0:D1], ALU.add)\
                    .then_inc(S["y_wh_added"], 1)

            def y_add_bo(b):
                pool.wait_ge(*after("y_norm", b, 2 * NI))
                pool.tensor_tensor(y_x[:, :, :], y_x[:, :, :], rows["bo"][:, None, :].broadcast_to([P, NI, D]),
                                   ALU.add).then_inc(S["y_bo"], 1)

            turns(pool, {"x_rstd": rstd("x", XT, 2), "x_next_rstd": rstd("x0", XT0, 1), "x_residual": x_residual, "x_mask": x_mask, "x_add_b2": x_add_b2, "x_gain": x_gain,
                         "y_rstd": rstd("y", YT, 3), "y_l1_mask": y_l1_mask, "y_l1_add_wh": y_l1_add_wh,
                         "y_add_bo": y_add_bo}, "pool")

        @block.scalar
        def _(act):
            act.wait_ge(s_load, 16 * N_LOADS)
            for n, (hi, lo, st) in enumerate(SPLIT):
                if n == len(SPLIT) - 1:
                    act.wait_ge(s_columns, 1)
                act.activation(hi, st, ACT.Copy).then_inc(s_high, 1)
            act.wait_ge(s_init, 1)

            def x_next_norm(b, n):
                act.wait_ge(*after("x0_shift", b, 1))
                act.wait_ge(*after("x0_rstd", b, 1))
                if not isinstance(b, int) or b > 0:
                    act.wait_ge(*filled("x", b - 1, "pv", NH, NI - 1))
                for i in range(NI):
                    act.activation(x_n[:, i, :], x_in[:, i, :], ACT.Relu, bias=XT0["shift"][:, i:i + 1],
                                   scale=XT0["rstd"][:, i:i + 1]).then_inc(S["x0_norm"], 1)

            def x_norm(b, n):
                act.wait_ge(*after("x_shift", b, 1))
                act.wait_ge(*after("x_rstd", b, 1))
                for i in range(NI):
                    act.activation(x_h[:, i, :], x_h[:, i, :], ACT.Identity, bias=XT["shift"][:, i:i + 1],
                                   scale=XT["rstd"][:, i:i + 1]).then_inc(S["x_norm"], 1)

            def y_norm(b, n):
                act.wait_ge(*after("y_shift", b, n + 1))
                act.wait_ge(*after("y_rstd", b, n + 1))
                for i in range(NI):
                    act.activation(y_h[:, i, :], y_x[:, i, :], ACT.Relu,
                                   bias=YT["shift"][:, i:i + 1], scale=YT["rstd"][:, i:i + 1])\
                        .then_inc(S["y_norm"], 1)

            def x_hi(b, c):
                act.wait_ge(*filled("x", b, "turn", c))
                act.activation(x_fr[:, c, :], bank_of("x", "turn", c)[:, :], ACT.Copy).then_inc(S["x_hi"], 1)

            def x_wh(b, h, i):
                act.wait_ge(*filled("x", b, "proj", h, i))
                act.activation(whx[:, i, h, 0:W0], bank_of("x", "proj", h, i)[:, 0:W0], ACT.Copy)\
                    .then_inc(S["x_wh"], 1)

            def x_brow(b, h):
                bank = bank_of("x", "brow", h)
                act.wait_ge(*filled("x", b, "brow", h))
                act.wait_ge(*after("x_score", b, h * NI))
                act.activation(brow[:, :], bank[:, :], ACT.Copy).then_inc(S["x_brow"], 1)

            def x_prob(b, h, j):
                n = h * NI + j
                act.wait_ge(*after("x_mask", b, n + 1))
                act.activation(xp[:, n % XRING, :], xp[:, n % XRING, :], ACT.Exp, bias=XT["d"][:, j, h:h + 1])\
                    .then_inc(S["x_prob"], 1)

            def x_elu_exp(b, h, i):
                n = h * NI + i
                bank = bank_of("x", "pv", h, i)
                act.wait_ge(*after("x_recip", b, n + 1))
                act.wait_ge(*after("x_elu", b, max(n - 1, 0)))
                act.activation(elu_e[:, n % 2, :], bank[:, 0:D], ACT.Exp, scale=x_r[:, i:i + 1])\
                    .then_inc(S["x_elu_exp"], 1)

            def x_h_hi(b, h, c):
                act.wait_ge(*filled("x", b, "h_turn", h, c))
                act.activation(x_fr[:, (h % 2) * 2 + c, :], bank_of("x", "h_turn", h, c)[:, :], ACT.Copy)\
                    .then_inc(S["x_h_hi"], 1)

            def x_wh2(b, p, i):
                act.wait_ge(*filled("x", b, "proj2", p, i))
                act.activation(whx[:, i, 0, 0:W0], bank_of("x", "proj2", p, i)[:, 0:W0], ACT.Copy)\
                    .then_inc(S["x_wh2a"], 1)

            def x_o_hi(b, c):
                act.wait_ge(*filled("x", b, "o_turn", c))
                act.activation(x_fr[:, c, :], bank_of("x", "o_turn", c)[:, :], ACT.Copy)\
                    .then_inc(S["x_o_hi"], 1)

            def x_hidden(b, m):
                bank = bank_of("x", "ffn1", m)
                act.wait_ge(*filled("x", b, "ffn1", m))
                act.activation(whx[:, m, 1:3, 0:D], bank[:, :].rearrange("p (a n) -> p a n", a=2), ACT.Relu,
                               bias=b1_col[:, m:m + 1]).then_inc(S["x_hidden"], 1)

            def y_hi(b, n, c):
                bank = bank_of("y", "turn", n, c)
                act.wait_ge(*filled("y", b, "turn", n, c))
                if n == 0:
                    act.activation(y_t[:, c, :], bank[:, :], ACT.Copy).then_inc(S["y_hi0"], 1)
                else:
                    act.activation(y_fr[:, c, :], bank[:, :], ACT.Copy).then_inc(S["y_hi"], 1)

            def y_l1_wh(b, p):
                bank = bank_of("y", "l1_proj", p)
                act.wait_ge(*filled("y", b, "l1_proj", p))
                act.activation(wh1[:, 2 * p:2 * p + 2, 0:W1C],
                               bank[:, 0:2 * W1C].rearrange("p (a n) -> p a n", a=2), ACT.Copy)\
                    .then_inc(S["y_wh"], 1)

            def y_l1_brow(b):
                bank = bank_of("y", "brow")
                act.wait_ge(*filled("y", b, "brow"))
                act.activation(y_v[:, 0:2, :].rearrange("p a n -> p (a n)"), bank[:, :], ACT.Copy)\
                    .then_inc(S["y_brow"], 1)

            def y_l1_prob(b, j):
                act.wait_ge(*after("y_mask", b, j + 1))
                act.activation(yp[:, j, :], yp[:, j, :], ACT.Exp, bias=YT["d"][:, j, 0:1]).then_inc(S["y_prob"], 1)

            def y_qk_hi(b, g, t):
                bank = bank_of("y", "qk", g, t)
                act.wait_ge(*filled("y", b, "qk", g, t))
                act.activation(qk_part[:, 2 * t, :], bank[:, :], ACT.Identity,
                               bias=(bq_col, bk_col)[t][:, g:g + 1]).then_inc(S["y_qk_hi"], 1)

            def y_stack_q(b, h):
                bank = bank_of("y", "stack", h, 0)
                act.wait_ge(*filled("y", b, "stack", h, 0))
                act.activation(qs[0:3 * DH, h % QRING, :], bank[0:3 * DH, :], ACT.Copy).then_inc(S["y_stack_q"], 1)

            def y_max_hi(b, h):
                bank = bank_of("y", "max_turn", h)
                act.wait_ge(*filled("y", b, "max_turn", h))
                if h >= 2:
                    act.wait_ge(*after("y_max_row", b, 32 * (h - 1)))
                act.activation(negm[:, h % 2, 0, :], bank[0:NI, 0:P], ACT.Copy, scale=-1.0)\
                    .then_inc(S["y_max_hi"], 1)

            def y_far_prob(b, h, k):
                n = far_tile(h, k)
                bank = bank_of("y", "far", h, k)
                act.wait_ge(*filled("y", b, "far", h, k))
                act.activation(yp[:, n % YRING, :], bank[:, :], ACT.Exp, scale=SCALE).then_inc(S["y_far_prob"], 1)

            def y_far_sums(b, g):
                act.wait_ge(*filled("y", b, "far_sum", g))
                act.activation(y_sums.rearrange("p a n -> p (a n)"), bank_of("y", "far_sum", g)[:, :],
                               ACT.Copy).then_inc(S["y_far_sums"], 1)

            def y_far_ctx(b, g):
                act.wait_ge(*filled("y", b, "far_ctx", g))
                act.activation(y_ctx[g], bank_of("y", "far_ctx", g)[:, :], ACT.Copy).then_inc(S["y_ctx0"], 1)

            def y_mj_hi(b, p):
                act.wait_ge(*after("y_mj_sum", b, p + 1))
                act.activation(qk_part[:, p, :], y_h[:, 2 * p:2 * p + 2, :].rearrange("p a n -> p (a n)"), ACT.Copy)\
                    .then_inc(S["y_mj_hi"], 1)

            turns(act, {"x_norm": x_norm, "x_next_norm": x_next_norm, "x_next_hi": x_hi, "x_next_wh": x_wh, "x_brow": x_brow, "x_prob": x_prob,
                        "x_elu_exp": x_elu_exp, "x_h_hi": x_h_hi, "x_wh2": x_wh2, "x_o_hi": x_o_hi,
                        "x_hidden": x_hidden, "y_norm": y_norm, "y_hi": y_hi, "y_l1_wh": y_l1_wh,
                        "y_l1_brow": y_l1_brow, "y_l1_prob": y_l1_prob, "y_qk_hi": y_qk_hi,
                        "y_stack_q": y_stack_q,
                        "y_max_hi": y_max_hi, "y_far_prob": y_far_prob, "y_far_sums": y_far_sums,
                        "y_far_ctx": y_far_ctx, "y_mj_hi": y_mj_hi}, "act")

        @block.tensor
        def _(pe):
            pe.wait_ge(s_id, 6)
            pe.wait_ge(s_init, 1)

            def turned(chain, src, bank, c, key, rows_=P):
                for i in range(NI):
                    last = pe.transpose(bank[:, i * P:(i + 1) * P], src[:, i, c * P:(c + 1) * P], ident[:, :])
                last.then_inc(full(chain, *key), 1)

            def broadcast(chain, columns, bank, key):
                for i in range(NI):
                    last = pe.transpose(bank[:, i * P:(i + 1) * P], columns(i).broadcast_to([P, P]), ident[:, :])
                last.then_inc(full(chain, *key), 1)

            def x_turn(b, c):
                bank = bank_of("x", "turn", c)
                pe.wait_ge(*emptied("x", b, "turn", c))
                if c == 0:
                    pe.wait_ge(*after("x0_norm", b, NI))
                turned("x", x_n, bank, c, ("turn", c))

            def x_proj(b, h, i):
                bank = bank_of("x", "proj", h, i)
                pe.wait_ge(*emptied("x", b, "proj", h, i))
                if h == 0 and i == 0:
                    pe.wait_ge(*after("x_lo", b, DC))
                n = slice(i * P, (i + 1) * P)
                split3(pe, bank[:, 0:W0], lambda c: x_fr[:, c, n], lambda c: x_fr[:, 2 + c, n],
                       lambda c: wh_hi[:, c, h, :], lambda c: wh_lo[:, c, h, :], [(c, c) for c in range(DC)])\
                    .then_inc(full("x", "proj", h, i), 1)

            def x_f2row(b, h):
                bank = bank_of("x", "f2row", h)
                pe.wait_ge(*emptied("x", b, "f2row", h))
                if h < NH:
                    pe.wait_ge(*after("x_wh", b, (h + 1) * NI))
                else:
                    pe.wait_ge(*after("x_wh2b", b, NI))
                broadcast("x", lambda i: whx[:, i, h % NH, D + 1:D + 2], bank, ("f2row", h))

            def x_rows(b, h):
                bank = bank_of("x", "arow", h)
                pe.wait_ge(*emptied("x", b, "arow", h))
                pe.wait_ge(*after("x_small", b, 6 if h < NH else 12))
                broadcast("x", lambda i: XT["a"][:, i, h:h + 1], bank, ("arow", h))
                bank = bank_of("x", "brow", h)
                pe.wait_ge(*emptied("x", b, "brow", h))
                broadcast("x", lambda i: XT["b"][:, i, h:h + 1], bank, ("brow", h))

            def x_pv(b, h, i):
                bank = bank_of("x", "pv", h, i)
                pe.wait_ge(*emptied("x", b, "pv", h, i))
                if i == 0:
                    pe.wait_ge(*after("x_prob", b, (h + 1) * NI))
                for j in range(NI):
                    t = xp[:, (h * NI + j) % XRING, i * P:(i + 1) * P]
                    last = pe.matmul(bank[:, 0:D + 3], t, whx[:, j, h % NH, 0:D + 3], start=(j == 0), stop=(j == NI - 1))
                last.then_inc(full("x", "pv", h, i), 1)

            def x_h_turn(b, h, c):
                bank = bank_of("x", "h_turn", h, c)
                pe.wait_ge(*emptied("x", b, "h_turn", h, c))
                if c == 0:
                    pe.wait_ge(*after("x_elu", b, (h + 1) * NI))
                turned("x", x_h, bank, c, ("h_turn", h, c))

            def x_proj2(b, p, i):
                bank = bank_of("x", "proj2", p, i)
                pe.wait_ge(*emptied("x", b, "proj2", p, i))
                if i == 0:
                    pe.wait_ge(*after("x_h_lo", b, 4 * (p + 1)))
                n = slice(i * P, (i + 1) * P)
                split3(pe, bank[:, 0:W0], lambda k: x_fr[:, k, n], lambda k: x_fr[:, 4 + k, n],
                       lambda k: wo2_hi[:, 4 * p + k, :], lambda k: wo2_lo[:, 4 * p + k, :],
                       [(k, k) for k in range(4)]).then_inc(full("x", "proj2", p, i), 1)

            def x_o_turn(b, c):
                bank = bank_of("x", "o_turn", c)
                pe.wait_ge(*emptied("x", b, "o_turn", c))
                if c == 0:
                    pe.wait_ge(*after("x_elu", b, (NH + 1) * NI))
                turned("x", x_h, bank, c, ("o_turn", c))

            def x_ffn1(b, m):
                bank = bank_of("x", "ffn1", m)
                pe.wait_ge(*emptied("x", b, "ffn1", m))
                if m == 0:
                    pe.wait_ge(*after("x_o_lo", b, DC))
                n = slice(m * P, (m + 1) * P)
                split3(pe, bank[:, :], lambda c: w1_hi[:, c, n], lambda c: w1_lo[:, c, n],
                       lambda c: x_fr[:, c, :], lambda c: x_fr[:, 2 + c, :], [(c, c) for c in range(DC)])\
                    .then_inc(full("x", "ffn1", m), 1)

            def x_ffn2(b, p):
                bank = bank_of("x", "ffn2", p)
                pe.wait_ge(*emptied("x", b, "ffn2", p))
                if p == 0:
                    pe.wait_ge(*after("x_hidden", b, 2))
                for i in (0, 1):
                    for m in range(DC):
                        last = pe.matmul(bank[:, i * D:(i + 1) * D], whx[:, m, 1 + p, i * P:(i + 1) * P],
                                         w2_sb[:, m, :], start=(m == 0), stop=(m == DC - 1))
                last.then_inc(full("x", "ffn2", p), 1)

            def y_turn(b, n, c):
                bank = bank_of("y", "turn", n, c)
                pe.wait_ge(*emptied("y", b, "turn", n, c))
                if c == 0:
                    pe.wait_ge(*after("y_norm", b, (n + 1) * NI))
                turned("y", y_h, bank, c, ("turn", n, c))

            def y_l1_proj(b, p):
                bank = bank_of("y", "l1_proj", p)
                pe.wait_ge(*emptied("y", b, "l1_proj", p))
                if p == 0:
                    pe.wait_ge(*after("y_hi0", b, DC))
                for i in (0, 1):
                    for c in range(DC):
                        last = pe.matmul(bank[:, i * W1C:(i + 1) * W1C], y_t[:, c, (2 * p + i) * P:(2 * p + i + 1) * P],
                                         wl1[:, c, :], start=(c == 0), stop=(c == DC - 1))
                last.then_inc(full("y", "l1_proj", p), 1)

            def y_l1_f2row(b):
                bank = bank_of("y", "f2row")
                pe.wait_ge(*emptied("y", b, "f2row"))
                pe.wait_ge(*after("y_wh", b, 2))
                broadcast("y", lambda i: wh1[:, i, D1 + 1:D1 + 2], bank, ("f2row",))

            def y_l1_rows(b):
                bank = bank_of("y", "arow")
                pe.wait_ge(*emptied("y", b, "arow"))
                pe.wait_ge(*after("y_small", b, 6))
                broadcast("y", lambda i: YT["a"][:, i, 0:1], bank, ("arow",))
                bank = bank_of("y", "brow")
                pe.wait_ge(*emptied("y", b, "brow"))
                broadcast("y", lambda i: YT["b"][:, i, 0:1], bank, ("brow",))

            def y_l1_pv(b, p):
                bank = bank_of("y", "l1_pv", p)
                pe.wait_ge(*emptied("y", b, "l1_pv", p))
                if p == 0:
                    pe.wait_ge(*after("y_prob", b, NI))
                for i in (0, 1):
                    for j in range(NI):
                        last = pe.matmul(bank[:, i * 256:i * 256 + D1 + 3], yp[:, j, (2 * p + i) * P:(2 * p + i + 1) * P],
                                         wh1[:, j, 0:D1 + 3], start=(j == 0), stop=(j == NI - 1))
                last.then_inc(full("y", "l1_pv", p), 1)

            def y_qk(b, g, t):
                bank = bank_of("y", "qk", g, t)
                pe.wait_ge(*emptied("y", b, "qk", g, t))
                if g == 0 and t == 0:
                    pe.wait_ge(*after("y_lo", b, DC))
                w_hi, w_lo = sq[("wq", "wk")[t]]
                n = slice(g * P, (g + 1) * P)
                split3(pe, bank[:, :], lambda c: w_hi[:, c, n], lambda c: w_lo[:, c, n],
                       lambda c: y_fr[:, c, :], lambda c: y_fr[:, 2 + c, :], [(c, c) for c in range(DC)])\
                    .then_inc(full("y", "qk", g, t), 1)

            def nodes_by(b, key, p, name):
                bank = bank_of("y", *key)
                pe.wait_ge(*emptied("y", b, *key))
                w_hi, w_lo = sq[name]
                for i in (0, 1):
                    n = slice((2 * p + i) * P, (2 * p + i + 1) * P)
                    last = split3(pe, bank[:, i * D:(i + 1) * D], lambda c: y_fr[:, c, n], lambda c: y_fr[:, 2 + c, n],
                                  lambda c: w_hi[:, c, :], lambda c: w_lo[:, c, :], [(c, c) for c in range(DC)])
                last.then_inc(full("y", *key), 1)

            def y_v_(b, p):
                nodes_by(b, ("v", p), p, "wv")

            def y_stack(b, h, t):
                bank = bank_of("y", "stack", h, t)
                g = h // G
                pe.wait_ge(*emptied("y", b, "stack", h, t))
                if h % G == 0:
                    pe.wait_ge(*after("y_qk_lo", b, 2 * g + t + 1))
                for part, first in ((0, (2, 3)[t]), (1, (0, 4)[t])):
                    last = pe.matmul(bank[0:3 * DH, :],
                                     pick[:, h % G, first:first + 3, :].rearrange("p a n -> p (a n)"),
                                     qk_part[:, 2 * t + part, :], start=(part == 0), stop=(part == 1))
                last.then_inc(full("y", "stack", h, t), 1)

            def y_near(b, h, i):
                bank, slot = bank_of("y", "near", h, i), h % QRING
                pe.wait_ge(*emptied("y", b, "near", h, i))
                if i == 0:
                    pe.wait_ge(*after("y_stack_q", b, h + 1))
                    pe.wait_ge(*after("y_stack_k", b, h + 1))
                pe.matmul(bank[:, :], qs[0:3 * DH, slot, i * P:(i + 1) * P], ks[0:3 * DH, slot, :], start=True, stop=True)\
                    .then_inc(full("y", "near", h, i), 1)

            def y_max_turn(b, h):
                bank = bank_of("y", "max_turn", h)
                pe.wait_ge(*emptied("y", b, "max_turn", h))
                pe.wait_ge(*after("y_near_max", b, (h + 1) * NI))
                pe.transpose(bank[0:NI, 0:P], max2[:, h % 2, :], ident[:, :]).then_inc(full("y", "max_turn", h), 1)

            def y_far(b, h, k):
                bank, slot = bank_of("y", "far", h, k), h % QRING
                pe.wait_ge(*emptied("y", b, "far", h, k))
                if k == 0 and h % 2 == 0:
                    pe.wait_ge(*after("y_max_row", b, 32 * (h + 2)))
                pe.matmul(bank[:, :], ks[0:3 * DH + 2, slot, k * P:(k + 1) * P], qs[0:3 * DH + 2, slot, :],
                          start=True, stop=False)
                pe.matmul(bank[:, :], ident_b[:, :], mask_t[:, k, :], start=False, stop=True)\
                    .then_inc(full("y", "far", h, k), 1)

            def y_far_pv(b, h, k):
                if k == 0 and h % G == 0:
                    pe.wait_ge(*emptied("y", b, "far_sum", h // G))
                    pe.wait_ge(*emptied("y", b, "far_ctx", h // G))
                    if h == 0:
                        pe.wait_ge(*after("y_v", b, 2))
                n = far_tile(h, k)
                if h % 2 == 0:
                    pe.wait_ge(*after("y_far_prob", b, n + 2))
                q, q_sum = (slice(DH * (k_ % G), DH * (k_ % G + 1)) for k_ in (h, h + 2))
                probs = yp[:, n % YRING, :]
                a = pe.matmul(YB[2][q_sum, :], ones[:, :], probs, start=(k == 0), stop=(k == NI - 1))
                c = pe.matmul(YB[3][q, :], y_v[:, k, h * DH:(h + 1) * DH], probs, start=(k == 0), stop=(k == NI - 1))
                if k == NI - 1 and h % G == G - 1:
                    a.then_inc(full("y", "far_sum", h // G), 1)
                    c.then_inc(full("y", "far_ctx", h // G), 1)

            def y_sum_turn(b, g):
                bank = bank_of("y", "sum_turn", g)
                pe.wait_ge(*emptied("y", b, "sum_turn", g))
                pe.wait_ge(*after("y_far_sums", b, g + 1))
                sums = y_sums.rearrange("p a n -> p (a n)")
                for i in range(NI):
                    last = pe.transpose(bank[:, i * P:(i + 1) * P], sums[:, i * P:(i + 1) * P], ident[:, :])
                last.then_inc(full("y", "sum_turn", g), 1)

            def y_recip_rows(b, g):
                bank = bank_of("y", "recip_rows", g)
                pe.wait_ge(*emptied("y", b, "recip_rows", g))
                pe.wait_ge(*after("y_recip_wide", b, g + 1))
                wide = y_sums.rearrange("p a n -> p (a n)")
                for i in range(NI):
                    last = pe.transpose(bank[:, i * P:(i + 1) * P], wide[:, i * P:(i + 1) * P], ident[:, :])
                last.then_inc(full("y", "recip_rows", g), 1)

            def y_o_proj(b, p):
                bank = bank_of("y", "o_proj", p)
                pe.wait_ge(*emptied("y", b, "o_proj", p))
                if p == 0:
                    pe.wait_ge(*after("y_ctx", b, NG))
                for i in (0, 1):
                    for c in range(DC):
                        last = pe.matmul(bank[:, i * D:(i + 1) * D], y_ctx[c][:, (2 * p + i) * P:(2 * p + i + 1) * P],
                                         wo_sb[:, c, :], start=(c == 0), stop=(c == DC - 1))
                last.then_inc(full("y", "o_proj", p), 1)

            def y_mj(b, p):
                if p == 0:
                    pe.wait_ge(*after("y_lo", b, 2 * DC))
                nodes_by(b, ("mj", p), p, "wj")

            def y_mi(b, p):
                nodes_by(b, ("mi", p), p, "wi")

            def y_gather(b, p):
                bank = bank_of("y", "gather", p)
                pe.wait_ge(*emptied("y", b, "gather", p))
                if p == 0:
                    pe.wait_ge(*after("y_mj_lo", b, 2))
                for i in (0, 1):
                    n = slice((2 * p + i) * P, (2 * p + i + 1) * P)
                    for j in range(NI):
                        for part in (0, 2):
                            mj = qk_part[:, part + j // 2, (j % 2) * D:(j % 2 + 1) * D]
                            last = pe.matmul(bank[:, i * D:(i + 1) * D], adjt[:, j, n], mj,
                                             start=(j == 0 and part == 0), stop=(j == NI - 1 and part == 2))
                last.then_inc(full("y", "gather", p), 1)

            turns(pe, {"x_next_turn": x_turn, "x_next_proj": x_proj, "x_f2row": x_f2row, "x_rows": x_rows, "x_pv": x_pv,
                       "x_h_turn": x_h_turn, "x_proj2": x_proj2, "x_o_turn": x_o_turn, "x_ffn1": x_ffn1,
                       "x_ffn2": x_ffn2, "y_turn": y_turn, "y_l1_proj": y_l1_proj, "y_l1_f2row": y_l1_f2row,
                       "y_l1_rows": y_l1_rows, "y_l1_pv": y_l1_pv, "y_qk": y_qk, "y_v": y_v_, "y_stack": y_stack, "y_near": y_near,
                       "y_max_turn": y_max_turn, "y_far": y_far, "y_far_pv": y_far_pv,
                       "y_sum_turn": y_sum_turn, "y_recip_rows": y_recip_rows, "y_o_proj": y_o_proj,
                       "y_mj": y_mj, "y_mi": y_mi, "y_gather": y_gather}, "pe")

        @block.vector
        def _(dve):
            done = [0]

            def step(ins):
                done[0] += 1
                ins.then_inc(s_split, 1)

            def settle():
                dve.wait_ge(s_split, done[0])

            step(dve.memset(ks[3 * DH:P, :, :].bitcast(F32), 1.0))
            step(dve.memset(pick[:, :, :, :].bitcast(F32), 0.0))
            step(dve.memset(wh1[:, :, D1 + 2:D1 + 4], 1.0))
            settle()
            dve.wait_ge(s_id, 6)
            for k in (2, 3, 5):
                step(dve.tensor_copy(pick[:, :, k, :], ident[:, :].rearrange("p (h d) -> p h d", h=G)))

            dve.wait_ge(s_load, 16 * N_LOADS)
            a1 = a_st[:, 0:1024].rearrange("p (h o) -> p h o", h=NH)
            a2 = a_st2[:, 0:1024].rearrange("p (h o) -> p h o", h=NH)
            scratch = y_junk[:, :, :].rearrange("p a n -> p (a n)").bitcast(F32).rearrange("p (a n) -> p a n", a=2)

            def column(out_column, weights, vector, width=D):
                half = done[0] % 2
                step(dve.tensor_tensor_reduce(scratch[:, half, 0:width], weights, vector, 1.0, 0.0, ALU.mult, ALU.add,
                                              out_column))
                dve.wait_ge(s_split, done[0] - 1)

            for c in range(DC):
                for h in range(NH):
                    for s, a in ((0, a1), (1, a2)):
                        column(w_st[:, c, h, D + s:D + s + 1], w_st[:, c, h, 0:D], a[:, h, :])
            settle()
            dve.sem_inc(s_columns, 1)
            columns2 = XT["max"]
            for k in range(NH * DC):
                for s in (0, 1):
                    at = 2 * (k // 4) + s
                    column(columns2[:, k % 4, at:at + 1], (ysx if k < 4 else ysv)[:, (k % 4) * D:(k % 4 + 1) * D],
                           brow[:, s * D:(s + 1) * D])
            for c in range(DC):
                for s in (0, 1):
                    column(wl1[:, c, D1 + s:D1 + s + 1], wl1[:, c, 0:D1], elu_e[:, 0, s * D1:(s + 1) * D1], D1)
            settle()
            for a in (0, 1):
                step(dve.tensor_copy(wo2_hi[:, 4 * a:4 * a + 4, D:D + 2], columns2[:, :, 2 * a:2 * a + 2]))
            settle()
            for a in (0, 1):
                step(dve.tensor_tensor(wo2_lo[:, 4 * a:4 * a + 4, D:D + 2], columns2[:, :, 2 * a:2 * a + 2],
                                       wo2_hi[:, 4 * a:4 * a + 4, D:D + 2].bitcast(F32), ALU.subtract))
            for n, (hi, lo, st) in enumerate(SPLIT):
                dve.wait_ge(s_high, n + 1)
                step(dve.tensor_tensor(lo, st, hi.bitcast(F32), ALU.subtract))
            step(dve.tensor_scalar(mask_n[:, :, :], adj_i, 0.0, MASKED, ALU.is_le, ALU.mult))
            for first, end, tile in adj_t_i:
                step(dve.tensor_scalar(mask_t[:, first:end, :], tile, 0.0, MASKED, ALU.is_le, ALU.mult))
                step(dve.tensor_copy(adjt[:, first:end, :], tile))
            settle()
            adj_f = yp[:, :, :]
            step(dve.tensor_copy(adj_f, adj_i))
            settle()
            step(dve.reduce_sum(deg[:, :], adj_f, AX_X))
            step(dve.memset(whx[:, :, :, D + 2:D + 4], 1.0))
            settle()
            dve.memset(y_junk[:, :, 0:2], 0.0).then_inc(s_init, 1)
            dve.wait_ge(s_init, 1)

            def apart():
                dve.sem_inc(s_apart, 1)

            def stats(chain, T, source):
                def go(b, n):
                    source(b, n)
                    src = {"x0": x_in, "x": x_h, "y": y_x}[chain]
                    for i in range(NI):
                        dve.bn_stats(T["stats"][:, i, :], src[:, i, :]).then_inc(S[f"{chain}_stats"], 1)
                    n = n if chain == "y" else 0
                    for i in range(NI):
                        dve.wait_ge(*after(f"{chain}_stats", b, n * NI + i + 1))
                        apart()
                        dve.bn_aggr(T["mv"][:, i, :], T["stats"][:, i, :]).then_inc(S[f"{chain}_aggr"], 1)
                    dve.wait_ge(*after(f"{chain}_aggr", b, (n + 1) * NI))
                    dve.tensor_scalar(T["var"][:, :], T["mv"][:, :, 1], LN_EPS, None, ALU.add)\
                        .then_inc(S[f"{chain}_var"], 1)
                return go

            def shift(chain, T):
                def go(b, n):
                    dve.wait_ge(*after(f"{chain}_rstd", b, (n if chain == "y" else 0) + 1))
                    dve.scalar_tensor_tensor(out=T["shift"][:, :], in0=T["mv"][:, :, 0], scalar=-1.0,
                                             in1=T["rstd"][:, :], op0=ALU.mult, op1=ALU.mult)\
                        .then_inc(S[f"{chain}_shift"], 1)
                return go

            def x_source(b, n):
                dve.wait_ge(*after("x_ffn", b, 2))

            def x_next_source(b, n):
                dve.wait_ge(*after("x_in_loaded", b, 16))

            def y_source(b, n):
                if n == 0:
                    dve.wait_ge(*after("x_out", b, 1))
                elif n == 1:
                    dve.wait_ge(*after("y_l1", b, NI))
                    dve.wait_ge(*after("y_wh_added", b, 1))
                else:
                    dve.wait_ge(*after("y_o", b, 2))

            def x_lo(b, c):
                bank = bank_of("x", "turn", c)
                dve.wait_ge(*after("x_hi", b, c + 1))
                dve.tensor_tensor(x_fr[:, 2 + c, :], bank[:, :], x_fr[:, c, :].bitcast(F32), ALU.subtract)\
                    .then_inc(S["x_lo"], 1)

            def x_rowmax(b, h):
                bank = bank_of("x", "f2row", h)
                dve.wait_ge(*filled("x", b, "f2row", h))
                if h == NH:
                    dve.wait_ge(*after("x_elu", b, NH * NI))
                apart()
                for i in range(NI):
                    n = h * NI + i
                    if n >= 2:
                        dve.wait_ge(*after("x_rowmax", b, n - 1))
                        apart()
                    dve.tensor_tensor_reduce(x_junk[:, n % 2, :], mask_n[:, i, :], bank[:, :], 1.0, LOWEST, ALU.add, ALU.max,
                                             XT["max"][:, i, h:h + 1]).then_inc(S["x_rowmax"], 1)

            def offsets(chain, T, b, n, f1, f2, hs):
                name, slope = f"{chain}_small", SLOPE[chain]
                v = {k: T[k][:, :, hs] for k in ("max", "sum", "m", "a", "b", "c", "d")}
                dve.tensor_scalar(v["c"], f2, 1.0 - slope, None, ALU.mult).then_inc(S[name], 1)
                dve.tensor_scalar(v["d"], f2, slope, None, ALU.mult).then_inc(S[name], 1)
                dve.tensor_tensor(v["sum"], v["max"], f1, ALU.add).then_inc(S[name], 1)
                dve.wait_ge(*after(name, b, n + 3))
                dve.scalar_tensor_tensor(out=v["m"], in0=v["sum"], scalar=slope, in1=v["sum"], op0=ALU.mult,
                                         op1=ALU.max).then_inc(S[name], 1)
                dve.wait_ge(*after(name, b, n + 4))
                dve.tensor_tensor(v["a"], f1, v["m"], ALU.subtract).then_inc(S[name], 1)
                dve.scalar_tensor_tensor(out=v["b"], in0=f1, scalar=slope, in1=v["m"], op0=ALU.mult,
                                         op1=ALU.subtract).then_inc(S[name], 1)

            def x_offsets(b, n):
                hs = slice(0, NH) if n == 0 else slice(NH, NH + 1)
                heads = slice(0, NH) if n == 0 else slice(0, 1)
                dve.wait_ge(*after("x_rowmax", b, NH * NI if n == 0 else (NH + 1) * NI))
                offsets("x", XT, b, 6 * n, whx[:, :, heads, D], whx[:, :, heads, D + 1], hs)

            def x_score(b, h, j):
                n = h * NI + j
                if j == 0:
                    bank = bank_of("x", "arow", h)
                    dve.wait_ge(*filled("x", b, "arow", h))
                    dve.wait_ge(*after("x_brow", b, h + 1))
                    dve.wait_ge(*after("x_small", b, 6 if h < NH else 12))
                if n >= XRING and (j == 0 or (n - XRING) % NI == 0):
                    dve.wait_ge(*filled("x", b, "pv", (n - XRING) // NI, NI - 1))
                bank = XB[XU[("arow", h)][0]]
                dve.scalar_tensor_tensor(out=xp[:, n % XRING, :], in0=bank[:, :], scalar=XT["c"][:, j, h:h + 1],
                                         in1=brow[:, :], op0=ALU.add, op1=ALU.max).then_inc(S["x_score"], 1)

            def x_recip(b, h, i):
                bank = bank_of("x", "pv", h, i)
                dve.wait_ge(*filled("x", b, "pv", h, i))
                dve.reciprocal(x_r[:, i:i + 1], bank[:, D + 2:D + 3]).then_inc(S["x_recip"], 1)

            def x_elu(b, h, i):
                n = h * NI + i
                dve.wait_ge(*after("x_elu_exp", b, n + 1))
                dve.tensor_scalar(elu_e[:, n % 2, :], elu_e[:, n % 2, :], 1.0, 1.0, ALU.min, ALU.subtract)\
                    .then_inc(S["x_elu_shift"], 1)
                dve.wait_ge(*after("x_elu_shift", b, n + 1))
                if i == 0 and 0 < h < NH:
                        dve.wait_ge(*filled("x", b, "h_turn", h - 1, 1))
                bank = XB[XU[("pv", h, i)][0]]
                dve.scalar_tensor_tensor(out=x_h[:, i, :], in0=bank[:, 0:D], scalar=x_r[:, i:i + 1],
                                         in1=elu_e[:, n % 2, :], op0=ALU.mult, op1=ALU.max)\
                    .then_inc(S["x_elu"], 1)

            def x_h_lo(b, h, c):
                bank = bank_of("x", "h_turn", h, c)
                dve.wait_ge(*after("x_h_hi", b, 2 * h + c + 1))
                k = (h % 2) * 2 + c
                dve.tensor_tensor(x_fr[:, 4 + k, :], bank[:, :], x_fr[:, k, :].bitcast(F32), ALU.subtract)\
                    .then_inc(S["x_h_lo"], 1)

            def x_wh2(b, p, i):
                bank = bank_of("x", "proj2", p, i)
                dve.wait_ge(*filled("x", b, "proj2", p, i))
                dve.wait_ge(*after("x_wh2a", b, NI))
                dve.tensor_tensor(whx[:, i, 0, 0:W0], bank[:, 0:W0], whx[:, i, 0, 0:W0], ALU.add)\
                    .then_inc(S["x_wh2b"], 1)

            def x_o_lo(b, c):
                bank = bank_of("x", "o_turn", c)
                dve.wait_ge(*after("x_o_hi", b, c + 1))
                dve.tensor_tensor(x_fr[:, 2 + c, :], bank[:, :], x_fr[:, c, :].bitcast(F32), ALU.subtract)\
                    .then_inc(S["x_o_lo"], 1)

            def x_ffn_sum(b, p):
                bank = bank_of("x", "ffn2", p)
                dve.wait_ge(*filled("x", b, "ffn2", p))
                dve.wait_ge(*after("x_b2", b, 1))
                part = x_h[:, 2 * p:2 * p + 2, :]
                ins = dve.tensor_tensor(part, bank[:, :].rearrange("p (a n) -> p a n", a=2), part, ALU.add)
                ins.then_inc(S["x_ffn"], 1)

            def x_out(b):
                dve.wait_ge(*after("x_gain", b, 1))
                dve.wait_ge(*after("x_res", b, 1))
                dve.wait_ge(*after("y_stored", b, 0))
                dve.tensor_tensor(y_x[:, :, :], x_h[:, :, :], x_res[:, :, :], ALU.add).then_inc(S["x_out"], 1)

            def y_lo(b, n, c):
                bank = bank_of("y", "turn", n, c)
                dve.wait_ge(*after("y_hi", b, 2 * (n - 1) + c + 1))
                dve.tensor_tensor(y_fr[:, 2 + c, :], bank[:, :], y_fr[:, c, :].bitcast(F32), ALU.subtract)\
                    .then_inc(S["y_lo"], 1)

            def y_l1_rowmax(b):
                bank = bank_of("y", "f2row")
                dve.wait_ge(*filled("y", b, "f2row"))
                apart()
                for i in range(NI):
                    if i >= 2:
                        dve.wait_ge(*after("y_rowmax", b, i - 1))
                        apart()
                    dve.tensor_tensor_reduce(y_junk[:, i % 2, :], mask_n[:, i, :], bank[:, :], 1.0, LOWEST, ALU.add, ALU.max,
                                             YT["max"][:, i, 0:1]).then_inc(S["y_rowmax"], 1)

            def y_l1_offsets(b):
                dve.wait_ge(*after("y_rowmax", b, NI))
                offsets("y", YT, b, 0, wh1[:, :, D1:D1 + 1], wh1[:, :, D1 + 1:D1 + 2], slice(0, 1))

            def y_l1_score(b, j):
                if j == 0:
                    dve.wait_ge(*filled("y", b, "arow"))
                    dve.wait_ge(*after("y_brow", b, 1))
                    dve.wait_ge(*after("y_small", b, 6))
                bank = YB[YU[("arow",)][0]]
                dve.scalar_tensor_tensor(out=yp[:, j, :], in0=bank[:, :], scalar=YT["c"][:, j, 0:1],
                                         in1=y_v[:, 0:2, :].rearrange("p a n -> p (a n)"), op0=ALU.add, op1=ALU.max)\
                    .then_inc(S["y_score"], 1)

            def y_l1_sum(b, p):
                bank = bank_of("y", "l1_pv", p)
                dve.wait_ge(*filled("y", b, "l1_pv", p))
                for i in (0, 1):
                    k = 2 * p + i
                    dve.reciprocal(y_r[:, k:k + 1], bank[:, i * 256 + D1 + 2:i * 256 + D1 + 3]).then_inc(S["y_recip"], 1)
                for i in (0, 1):
                    k = 2 * p + i
                    dve.wait_ge(*after("y_recip", b, k + 1))
                    dve.scalar_tensor_tensor(out=y_x[:, k, 0:D1], in0=bank[:, i * 256:i * 256 + D1],
                                             scalar=y_r[:, k:k + 1], in1=y_x[:, k, 0:D1], op0=ALU.mult, op1=ALU.add)\
                        .then_inc(S["y_l1"], 1)

            def y_qk_lo(b, g, t):
                bank = bank_of("y", "qk", g, t)
                dve.wait_ge(*after("y_qk_hi", b, 2 * g + t + 1))
                dve.scalar_tensor_tensor(out=qk_part[:, 2 * t + 1, :], in0=bank[:, :],
                                         scalar=(bq_col, bk_col)[t][:, g:g + 1], in1=qk_part[:, 2 * t, :].bitcast(F32),
                                         op0=ALU.add, op1=ALU.subtract).then_inc(S["y_qk_lo"], 1)

            def y_v_sum(b, p):
                bank = bank_of("y", "v", p)
                dve.wait_ge(*filled("y", b, "v", p))
                dve.tensor_tensor(y_v[:, 2 * p:2 * p + 2, :], bank[:, :].rearrange("p (a n) -> p a n", a=2),
                                  rows["bv"][:, None, :].broadcast_to([P, 2, D]), ALU.add).then_inc(S["y_v"], 1)

            def y_stack_k(b, h):
                bank = bank_of("y", "stack", h, 1)
                dve.wait_ge(*filled("y", b, "stack", h, 1))
                dve.tensor_copy(ks[0:3 * DH, h % QRING, :], bank[0:3 * DH, :]).then_inc(S["y_stack_k"], 1)

            def y_near_max(b, h, i):
                bank, n = bank_of("y", "near", h, i), h * NI + i
                dve.wait_ge(*filled("y", b, "near", h, i))
                if n >= 2:
                    dve.wait_ge(*after("y_near_max", b, n - 1))
                apart()
                dve.tensor_tensor_reduce(y_junk[:, n % 2, :], mask_n[:, i, :], bank[:, :], 1.0, LOWEST, ALU.add, ALU.max,
                                         max2[:, h % 2, i:i + 1]).then_inc(S["y_near_max"], 1)

            def y_max_lo(b, h):
                bank = bank_of("y", "max_turn", h)
                dve.wait_ge(*after("y_max_hi", b, h + 1))
                dve.scalar_tensor_tensor(out=negm[:, h % 2, 1, :], in0=bank[0:NI, 0:P], scalar=-1.0,
                                         in1=negm[:, h % 2, 0, :].bitcast(F32), op0=ALU.mult, op1=ALU.subtract)\
                    .then_inc(S["y_max_lo"], 1)

            def y_far_recip(b, g):
                bank = bank_of("y", "sum_turn", g)
                sums = bank[:, :].rearrange("p (i h d) -> p i h d", i=NI, h=G)
                dve.wait_ge(*filled("y", b, "sum_turn", g))
                for h, at in ((0, 2), (2, 0)):
                    dve.reciprocal(y_rs[:, :, h:h + 2], sums[:, :, at:at + 2, 0]).then_inc(S["y_frecip"], 1)
                dve.wait_ge(*after("y_frecip", b, 2 * g + 2))
                dve.tensor_copy(y_sums.rearrange("p a (i h d) -> p (a i) h d", i=2, h=G),
                                y_rs[:, :, :, None].broadcast_to([P, NI, G, DH])).then_inc(S["y_recip_wide"], 1)

            def y_far_norm(b, g):
                bank = bank_of("y", "recip_rows", g)
                dve.wait_ge(*filled("y", b, "recip_rows", g))
                dve.wait_ge(*after("y_ctx0", b, g + 1))
                dve.tensor_tensor(y_ctx[g], bank[:, :], y_ctx[g], ALU.mult).then_inc(S["y_ctx"], 1)

            def y_o_sum(b, p):
                bank = bank_of("y", "o_proj", p)
                dve.wait_ge(*filled("y", b, "o_proj", p))
                dve.wait_ge(*after("y_bo", b, 1))
                part = y_x[:, 2 * p:2 * p + 2, :]
                dve.tensor_tensor(part, bank[:, :].rearrange("p (a n) -> p a n", a=2), part, ALU.add)\
                    .then_inc(S["y_o"], 1)

            def y_mj_sum(b, p):
                bank = bank_of("y", "mj", p)
                dve.wait_ge(*filled("y", b, "mj", p))
                dve.tensor_tensor(y_h[:, 2 * p:2 * p + 2, :], bank[:, :].rearrange("p (a n) -> p a n", a=2),
                                  rows["b3"][:, None, :].broadcast_to([P, 2, D]), ALU.add).then_inc(S["y_mj_sum"], 1)

            def y_mj_lo(b, p):
                dve.wait_ge(*after("y_mj_hi", b, p + 1))
                dve.tensor_tensor(qk_part[:, 2 + p, :], y_h[:, 2 * p:2 * p + 2, :].rearrange("p a n -> p (a n)"),
                                  qk_part[:, p, :].bitcast(F32), ALU.subtract).then_inc(S["y_mj_lo"], 1)

            def y_mi_sum(b, p):
                bank = bank_of("y", "mi", p)
                dve.wait_ge(*filled("y", b, "mi", p))
                for i in (0, 1):
                    k = 2 * p + i
                    dve.scalar_tensor_tensor(out=y_x[:, k, :], in0=bank[:, i * D:(i + 1) * D],
                                             scalar=deg[:, k:k + 1], in1=y_x[:, k, :], op0=ALU.mult, op1=ALU.add)\
                        .then_inc(S["y_mi"], 1)

            def y_gather_sum(b, p):
                bank = bank_of("y", "gather", p)
                dve.wait_ge(*filled("y", b, "gather", p))
                dve.wait_ge(*after("y_mi", b, NI))
                part = y_x[:, 2 * p:2 * p + 2, :]
                dve.tensor_tensor(part, bank[:, :].rearrange("p (a n) -> p a n", a=2), part, ALU.add)\
                    .then_inc(S["y_out"], 1)

            turns(dve, {"x_stats": stats("x", XT, x_source), "x_shift": shift("x", XT),
                        "x_next_stats": stats("x0", XT0, x_next_source), "x_next_shift": shift("x0", XT0),
                        "x_next_lo": x_lo,
                        "x_rowmax": x_rowmax, "x_offsets": x_offsets, "x_score": x_score, "x_recip": x_recip,
                        "x_elu": x_elu, "x_h_lo": x_h_lo, "x_wh2": x_wh2, "x_o_lo": x_o_lo,
                        "x_ffn_sum": x_ffn_sum, "x_out": x_out, "y_stats": stats("y", YT, y_source),
                        "y_shift": shift("y", YT), "y_lo": y_lo, "y_l1_rowmax": y_l1_rowmax,
                        "y_l1_offsets": y_l1_offsets, "y_l1_score": y_l1_score, "y_l1_sum": y_l1_sum,
                        "y_qk_lo": y_qk_lo, "y_v_sum": y_v_sum, "y_stack_k": y_stack_k, "y_near_max": y_near_max, "y_max_lo": y_max_lo,
                        "y_far_recip": y_far_recip, "y_far_norm": y_far_norm, "y_o_sum": y_o_sum,
                        "y_mj_sum": y_mj_sum, "y_mj_lo": y_mj_lo, "y_mi_sum": y_mi_sum,
                        "y_gather_sum": y_gather_sum}, "dve")


def kernel(**inputs):
    import numpy as _np
    import concourse.bacc as _bacc
    from concourse import mybir as _mybir
    from concourse.bass_utils import run_bass_kernel_spmd as _run

    g = {n: _np.asarray(a) for n, a in inputs.items()}
    D = g["x"].shape[-1]
    laid = {
        "x": g["x"], "adj": g["adj"], "adj_t": g["adj"].T,
        "w_heads": g["L0_gnn_W_heads"], "a_heads": g["L0_gnn_a_heads"], "w_out": g["L0_gnn_W_out"],
        "a_out": g["L0_gnn_a_out"], "w1": g["L0_gnn_w1"], "b1": g["L0_gnn_b1"], "w2": g["L0_gnn_w2"],
        "b2": g["L0_gnn_b2"], "gamma": g["L0_gnn_ln_gamma"], "beta": g["L0_gnn_ln_beta"],
        "l1_w": g["L1_gnn_W"], "l1_a": g["L1_gnn_a"],
        "wq_t": g["L2_gnn_Wq"].T, "bq": g["L2_gnn_bq"], "wk_t": g["L2_gnn_Wk"].T, "bk": g["L2_gnn_bk"],
        "wv_t": g["L2_gnn_Wv"].T, "bv": g["L2_gnn_bv"], "wo_t": g["L2_gnn_Wo"].T, "bo": g["L2_gnn_bo"],
        "wi_t": g["L3_gnn_W"][:, :D].T, "wj_t": g["L3_gnn_W"][:, D:].T, "b3": g["L3_gnn_b"],
    }
    nc = _bacc.Bacc("TRN2", target_bir_lowering=False, num_devices=1)
    arrays, args = {}, []
    for name, a in laid.items():
        a = _np.ascontiguousarray(a)
        arrays[f"in_{name}_dram"] = a
        args.append(nc.dram_tensor(f"in_{name}_dram", a.shape, _mybir.dt.from_np(a.dtype), kind="ExternalInput").ap())
    args.append(nc.dram_tensor("out_0_dram", g["x"].shape, _mybir.dt.float32, kind="ExternalOutput").ap())
    gnn_stack_kernel(nc, *args)
    r = _run(nc, [arrays], core_ids=[0])
    return r.results[0]["out_0_dram"]
```
